# Optimizing a Trainium2 kernel written in Bass

```python
import numpy as np
import jax
import jax.numpy as jnp

def _softmax(x, axis=-1):
    return jax.nn.softmax(x, axis=axis)

def _gelu(x):
    return jax.nn.gelu(x, approximate=True)

def _silu(x):
    return jax.nn.silu(x)

def _sigmoid(x):
    return jax.nn.sigmoid(x)

def _layernorm(x, axis=-1, eps=1e-05):
    m = jnp.mean(x, axis=axis, keepdims=True)
    v = jnp.var(x, axis=axis, keepdims=True)
    return (x - m) / jnp.sqrt(v + eps)

def _scatter_add(tgt, idx, src, axis=0):
    return tgt.at[idx].add(src)

def _segment_sum(src, seg, n):
    return jax.ops.segment_sum(src, seg, n)
kernel_name = 'mk_early_fusion_d2_tok_img768_r4_c56a71'

def setup_inputs(seed: int=0):
    np.random.seed(seed)
    _w = jnp.asarray

    def _rec_inputs():
        import jax
        import jax.numpy as jnp
        _rk = jax.random.key(seed)
        x = -0.000147625 + 0.999875 * jax.random.normal(jax.random.fold_in(_rk, 1), (32, 12, 224, 224), jnp.float32)
        txt = -0.0221329 + 10 * jax.random.normal(jax.random.fold_in(_rk, 2), (32, 77, 192), jnp.float32)
        return (x, txt)
    x, txt = _rec_inputs()

    def _L0_tok_setup():
        import jax, jax.numpy as jnp
        import numpy as np
        IMG = 224
        PATCH = 16
        EMBED = 192
        C = 12
        B = 64
        key = jax.random.key(seed)
        k1, k2 = jax.random.split(key)
        x = jax.random.normal(k1, (B, C, IMG, IMG), dtype=jnp.float32)
        channel_weights = jax.random.normal(k2, (C, EMBED), dtype=jnp.float32)
        return {'x': x, 'channel_weights': channel_weights}
    _L0_tok_all = _L0_tok_setup()
    _L0_tok_in = {k: v for k, v in _L0_tok_all.items() if k in ('channel_weights',)}
    del _L0_tok_all

    def _L0_attn_setup():
        import jax, jax.numpy as jnp
        import numpy as np
        LEVEL = 8
        NUM_HEADS = 12
        QN_SYM = float(-(LEVEL // 2))
        QP_SYM = float(LEVEL // 2 - 1)
        QN_ASYM = 0.0
        QP_ASYM = float(LEVEL - 1)

        def fake_quant(x, s, qn, qp):
            xc = jnp.clip(x / s, qn, qp)
            xr = xc + jax.lax.stop_gradient(jnp.round(xc) - xc)
            return s * xr
        key = jax.random.key(seed)
        k0, k1, k2 = jax.random.split(key, 3)
        B, N, C = (4, 512, 192)
        x = jax.random.normal(k0, (B, N, C), dtype=jnp.float32)
        Wqkv = jax.random.normal(k1, (3 * C, C), dtype=jnp.float32) * C ** (-0.5)
        Wproj = jax.random.normal(k2, (C, C), dtype=jnp.float32) * C ** (-0.5)
        bproj = jnp.zeros((C,), dtype=jnp.float32)
        s_q = jnp.asarray(1.0, dtype=jnp.float32)
        s_k = jnp.asarray(1.0, dtype=jnp.float32)
        s_v = jnp.asarray(1.0, dtype=jnp.float32)
        s_attn = jnp.asarray(1.0 / QP_ASYM, dtype=jnp.float32)
        s_after = jnp.asarray(1.0, dtype=jnp.float32)
        return {'x': x, 'Wqkv': Wqkv, 'Wproj': Wproj, 'bproj': bproj, 's_q': s_q, 's_k': s_k, 's_v': s_v, 's_attn': s_attn, 's_after': s_after}
    _L0_attn_all = _L0_attn_setup()
    _L0_attn_in = {k: v for k, v in _L0_attn_all.items() if k in ('Wqkv', 'Wproj', 'bproj', 's_q', 's_k', 's_v', 's_attn', 's_after')}
    del _L0_attn_all

    def _L0_ffn_setup():
        import jax, jax.numpy as jnp
        import numpy as np
        B, L, D, H, F = (4, 512, 192, 12, 768)
        ROUTE_FRAC = 0.15
        LN_EPS = 1e-05

        def _ln(x, g, b):
            m = jnp.mean(x, axis=-1, keepdims=True)
            v = jnp.mean((x - m) ** 2, axis=-1, keepdims=True)
            return (x - m) * jax.lax.rsqrt(v + LN_EPS) * g + b
        key = jax.random.key(seed)
        ks = jax.random.split(key, 20)
        s = 0.02
        return {'hidden_states': jax.random.normal(ks[0], (B, L, D), dtype=jnp.float32), 'g1': jnp.ones((D,), jnp.float32), 'b1': jnp.zeros((D,), jnp.float32), 'g2': jnp.ones((D,), jnp.float32), 'b2': jnp.zeros((D,), jnp.float32), 'Wr': jax.random.normal(ks[1], (D,), jnp.float32) * s, 'br': jnp.zeros((), jnp.float32), 'Wq': jax.random.normal(ks[2], (D, D), jnp.float32) * s, 'bq': jnp.zeros((D,), jnp.float32), 'Wk': jax.random.normal(ks[3], (D, D), jnp.float32) * s, 'bk': jnp.zeros((D,), jnp.float32), 'Wv': jax.random.normal(ks[4], (D, D), jnp.float32) * s, 'bv': jnp.zeros((D,), jnp.float32), 'Wo': jax.random.normal(ks[5], (D, D), jnp.float32) * s, 'bo': jnp.zeros((D,), jnp.float32), 'Wm': jax.random.normal(ks[6], (D, D), jnp.float32) * s, 'bm': jnp.zeros((D,), jnp.float32), 'W1': jax.random.normal(ks[7], (D, F), jnp.float32) * s, 'bf1': jnp.zeros((F,), jnp.float32), 'W2': jax.random.normal(ks[8], (F, D), jnp.float32) * s, 'bf2': jnp.zeros((D,), jnp.float32)}
    _L0_ffn_all = _L0_ffn_setup()
    _L0_ffn_in = {k: v for k, v in _L0_ffn_all.items() if k in ('g1', 'b1', 'g2', 'b2', 'Wr', 'br', 'Wq', 'bq', 'Wk', 'bk', 'Wv', 'bv', 'Wo', 'bo', 'Wm', 'bm', 'W1', 'bf1', 'W2', 'bf2')}
    del _L0_ffn_all

    def _L1_attn_setup():
        import jax, jax.numpy as jnp
        import numpy as np
        import math
        DIM = 192
        NUM_HEADS = 12

        def _xavier_uniform(key, out_f, in_f):
            a = math.sqrt(6.0 / (in_f + out_f))
            return jax.random.uniform(key, (out_f, in_f), jnp.float32, -a, a)
        key = jax.random.key(seed)
        k_x, k_qw, k_qB, k_pw, k_pB = jax.random.split(key, 5)
        B, N = (16, 256)
        x = jax.random.normal(k_x, (B, N, DIM), jnp.float32)
        qkv_w = _xavier_uniform(k_qw, 3 * DIM, DIM)
        qkv_b = jnp.zeros((3 * DIM,), jnp.float32)
        qkv_B = jax.random.normal(k_qB, (3 * DIM, DIM), jnp.float32) * math.sqrt(1.0 / DIM)
        proj_w = _xavier_uniform(k_pw, DIM, DIM)
        proj_b = jnp.zeros((DIM,), jnp.float32)
        proj_B = jax.random.normal(k_pB, (DIM, DIM), jnp.float32) * math.sqrt(1.0 / DIM)
        return {'x': x, 'qkv_w': qkv_w, 'qkv_b': qkv_b, 'qkv_B': qkv_B, 'proj_w': proj_w, 'proj_b': proj_b, 'proj_B': proj_B}
    _L1_attn_all = _L1_attn_setup()
    _L1_attn_in = {k: v for k, v in _L1_attn_all.items() if k in ('qkv_w', 'qkv_b', 'qkv_B', 'proj_w', 'proj_b', 'proj_B')}
    del _L1_attn_all

    def _L1_ffn_setup():
        import jax, jax.numpy as jnp
        import numpy as np
        B, S, H, I = (4, 512, 192, 384)
        E, K = (3, 2)
        INIT = 0.02

        def _expert(x, gw, uw, dw):
            return jax.nn.silu(x @ gw) * (x @ uw) @ dw
        key = jax.random.key(seed)
        ks = jax.random.split(key, 8)
        f32 = jnp.float32
        return {'x': jax.random.normal(ks[0], (B, S, H), f32), 'shared_gate': jax.random.normal(ks[1], (H, I), f32) * INIT, 'shared_up': jax.random.normal(ks[2], (H, I), f32) * INIT, 'shared_down': jax.random.normal(ks[3], (I, H), f32) * INIT, 'routed_gate': jax.random.normal(ks[4], (E, H, I), f32) * INIT, 'routed_up': jax.random.normal(ks[5], (E, H, I), f32) * INIT, 'routed_down': jax.random.normal(ks[6], (E, I, H), f32) * INIT, 'router_w': jax.random.normal(ks[7], (H, E), f32) * INIT, 'routing_bias': jnp.zeros((E,), f32)}
    _L1_ffn_all = _L1_ffn_setup()
    _L1_ffn_in = {k: v for k, v in _L1_ffn_all.items() if k in ('shared_gate', 'shared_up', 'shared_down', 'routed_gate', 'routed_up', 'routed_down', 'router_w', 'routing_bias')}
    del _L1_ffn_all
    return {'x': x, 'txt': txt, 'L0_tok_channel_weights': _L0_tok_in['channel_weights'], 'L0_attn_Wqkv': _L0_attn_in['Wqkv'], 'L0_attn_Wproj': _L0_attn_in['Wproj'], 'L0_attn_bproj': _L0_attn_in['bproj'], 'L0_attn_s_q': _L0_attn_in['s_q'], 'L0_attn_s_k': _L0_attn_in['s_k'], 'L0_attn_s_v': _L0_attn_in['s_v'], 'L0_attn_s_attn': _L0_attn_in['s_attn'], 'L0_attn_s_after': _L0_attn_in['s_after'], 'L0_ffn_g1': _L0_ffn_in['g1'], 'L0_ffn_b1': _L0_ffn_in['b1'], 'L0_ffn_g2': _L0_ffn_in['g2'], 'L0_ffn_b2': _L0_ffn_in['b2'], 'L0_ffn_Wr': _L0_ffn_in['Wr'], 'L0_ffn_br': _L0_ffn_in['br'], 'L0_ffn_Wq': _L0_ffn_in['Wq'], 'L0_ffn_bq': _L0_ffn_in['bq'], 'L0_ffn_Wk': _L0_ffn_in['Wk'], 'L0_ffn_bk': _L0_ffn_in['bk'], 'L0_ffn_Wv': _L0_ffn_in['Wv'], 'L0_ffn_bv': _L0_ffn_in['bv'], 'L0_ffn_Wo': _L0_ffn_in['Wo'], 'L0_ffn_bo': _L0_ffn_in['bo'], 'L0_ffn_Wm': _L0_ffn_in['Wm'], 'L0_ffn_bm': _L0_ffn_in['bm'], 'L0_ffn_W1': _L0_ffn_in['W1'], 'L0_ffn_bf1': _L0_ffn_in['bf1'], 'L0_ffn_W2': _L0_ffn_in['W2'], 'L0_ffn_bf2': _L0_ffn_in['bf2'], 'L1_attn_qkv_w': _L1_attn_in['qkv_w'], 'L1_attn_qkv_b': _L1_attn_in['qkv_b'], 'L1_attn_qkv_B': _L1_attn_in['qkv_B'], 'L1_attn_proj_w': _L1_attn_in['proj_w'], 'L1_attn_proj_b': _L1_attn_in['proj_b'], 'L1_attn_proj_B': _L1_attn_in['proj_B'], 'L1_ffn_shared_gate': _L1_ffn_in['shared_gate'], 'L1_ffn_shared_up': _L1_ffn_in['shared_up'], 'L1_ffn_shared_down': _L1_ffn_in['shared_down'], 'L1_ffn_routed_gate': _L1_ffn_in['routed_gate'], 'L1_ffn_routed_up': _L1_ffn_in['routed_up'], 'L1_ffn_routed_down': _L1_ffn_in['routed_down'], 'L1_ffn_router_w': _L1_ffn_in['router_w'], 'L1_ffn_routing_bias': _L1_ffn_in['routing_bias']}

def reference(x, txt, L0_tok_channel_weights, L0_attn_Wqkv, L0_attn_Wproj, L0_attn_bproj, L0_attn_s_q, L0_attn_s_k, L0_attn_s_v, L0_attn_s_attn, L0_attn_s_after, L0_ffn_g1, L0_ffn_b1, L0_ffn_g2, L0_ffn_b2, L0_ffn_Wr, L0_ffn_br, L0_ffn_Wq, L0_ffn_bq, L0_ffn_Wk, L0_ffn_bk, L0_ffn_Wv, L0_ffn_bv, L0_ffn_Wo, L0_ffn_bo, L0_ffn_Wm, L0_ffn_bm, L0_ffn_W1, L0_ffn_bf1, L0_ffn_W2, L0_ffn_bf2, L1_attn_qkv_w, L1_attn_qkv_b, L1_attn_qkv_B, L1_attn_proj_w, L1_attn_proj_b, L1_attn_proj_B, L1_ffn_shared_gate, L1_ffn_shared_up, L1_ffn_shared_down, L1_ffn_routed_gate, L1_ffn_routed_up, L1_ffn_routed_down, L1_ffn_router_w, L1_ffn_routing_bias):
    import jax
    import jax.numpy as jnp

    def _L0_tok_ref(x, channel_weights):
        import jax, jax.numpy as jnp
        import numpy as np
        IMG = 224
        PATCH = 16
        EMBED = 192
        C = 12
        B = 64
        Bb, Cc, H, W = x.shape
        K = PATCH
        n = H // K
        pooled = x.reshape(Bb, Cc, n, K, n, K).sum(axis=(3, 5))
        out = jnp.einsum('bcij,ce->bije', pooled, channel_weights)
        return out.reshape(Bb, n * n, EMBED)

    def _L0_attn_ref(x, Wqkv, Wproj, bproj, s_q, s_k, s_v, s_attn, s_after):
        import jax, jax.numpy as jnp
        import numpy as np
        LEVEL = 8
        NUM_HEADS = 12
        QN_SYM = float(-(LEVEL // 2))
        QP_SYM = float(LEVEL // 2 - 1)
        QN_ASYM = 0.0
        QP_ASYM = float(LEVEL - 1)

        def fake_quant(x, s, qn, qp):
            xc = jnp.clip(x / s, qn, qp)
            xr = xc + jax.lax.stop_gradient(jnp.round(xc) - xc)
            return s * xr
        B, N, C = x.shape
        H = NUM_HEADS
        D = C // H
        scale = D ** (-0.5)
        qkv = jnp.einsum('bnc,dc->bnd', x, Wqkv).reshape(B, N, 3, H, D).transpose(2, 0, 3, 1, 4)
        q, k, v = (qkv[0], qkv[1], qkv[2])
        q = fake_quant(q, s_q, QN_SYM, QP_SYM) * scale
        k = fake_quant(k, s_k, QN_SYM, QP_SYM)
        v = fake_quant(v, s_v, QN_SYM, QP_SYM)
        attn = jnp.einsum('bhnd,bhmd->bhnm', q, k)
        attn = fake_quant(attn / N, s_attn, QN_ASYM, QP_ASYM)
        out = jnp.einsum('bhnm,bhmd->bhnd', attn, v)
        out = fake_quant(out, s_after, QN_SYM, QP_SYM)
        out = out.transpose(0, 2, 1, 3).reshape(B, N, C)
        return out @ Wproj.T + bproj

    def _L0_ffn_ref(hidden_states, g1, b1, g2, b2, Wr, br, Wq, bq, Wk, bk, Wv, bv, Wo, bo, Wm, bm, W1, bf1, W2, bf2):
        import jax, jax.numpy as jnp
        import numpy as np
        B, L, D, H, F = (4, 512, 192, 12, 768)
        ROUTE_FRAC = 0.15
        LN_EPS = 1e-05

        def _ln(x, g, b):
            m = jnp.mean(x, axis=-1, keepdims=True)
            v = jnp.mean((x - m) ** 2, axis=-1, keepdims=True)
            return (x - m) * jax.lax.rsqrt(v + LN_EPS) * g + b
        b, l, d = hidden_states.shape
        dh = d // H
        normed = _ln(hidden_states, g1, b1)
        scores = jax.nn.sigmoid(jnp.einsum('bld,d->bl', normed, Wr) + br)
        k = max(1, int(round(ROUTE_FRAC * l)))
        _, idx = jax.lax.top_k(-scores, k)
        attn_mask = jnp.zeros((b, l), bool).at[jnp.arange(b)[:, None], idx].set(True)
        q = (normed @ Wq + bq).reshape(b, l, H, dh)
        kk = (normed @ Wk + bk).reshape(b, l, H, dh)
        v = (normed @ Wv + bv).reshape(b, l, H, dh)
        logits = jnp.einsum('blhd,bmhd->bhlm', q, kk) / jnp.sqrt(jnp.float32(dh))
        probs = jax.nn.softmax(logits, axis=-1)
        ctx = jnp.einsum('bhlm,bmhd->blhd', probs, v).reshape(b, l, d)
        attn_out = ctx @ Wo + bo
        w = scores / (jnp.sum(scores, axis=1, keepdims=True) + 1e-06)
        pooled = jnp.einsum('bl,bld->bd', w, normed)
        mix_out = (normed + scores[..., None] * pooled[:, None, :]) @ Wm + bm
        merged = jnp.where(attn_mask[..., None], attn_out, mix_out)
        h = hidden_states + merged
        n2 = _ln(h, g2, b2)
        ffn = jax.nn.gelu(n2 @ W1 + bf1, approximate=False) @ W2 + bf2
        return h + ffn

    def _L1_attn_ref(x, qkv_w, qkv_b, qkv_B, proj_w, proj_b, proj_B):
        import jax, jax.numpy as jnp
        import numpy as np
        import math
        DIM = 192
        NUM_HEADS = 12

        def _xavier_uniform(key, out_f, in_f):
            a = math.sqrt(6.0 / (in_f + out_f))
            return jax.random.uniform(key, (out_f, in_f), jnp.float32, -a, a)
        B, N, C = x.shape
        hd = C // NUM_HEADS
        scale = hd ** (-0.5)
        qkv = x @ qkv_w.T + qkv_b
        qkv = qkv.reshape(B, N, 3, NUM_HEADS, hd).transpose(2, 0, 3, 1, 4)
        q, k, v = (qkv[0], qkv[1], qkv[2])
        attn = jnp.einsum('bhnd,bhmd->bhnm', q, k) * scale
        attn = jax.nn.softmax(attn, axis=-1)
        out = jnp.einsum('bhnm,bhmd->bhnd', attn, v)
        out = out.transpose(0, 2, 1, 3).reshape(B, N, C)
        return out @ proj_w.T + proj_b

    def _L1_ffn_ref(x, shared_gate, shared_up, shared_down, routed_gate, routed_up, routed_down, router_w, routing_bias):
        import jax, jax.numpy as jnp
        import numpy as np
        B, S, H, I = (4, 512, 192, 384)
        E, K = (3, 2)
        INIT = 0.02

        def _expert(x, gw, uw, dw):
            return jax.nn.silu(x @ gw) * (x @ uw) @ dw
        shared_out = _expert(x, shared_gate, shared_up, shared_down)
        routing_probs = jax.nn.sigmoid(x @ router_w + routing_bias)
        scores, indices = jax.lax.top_k(routing_probs, K)
        scores = scores / scores.sum(axis=-1, keepdims=True)
        combine_w = (jax.nn.one_hot(indices, E, dtype=x.dtype) * scores[..., None]).sum(axis=-2)
        g = jnp.einsum('bsh,ehi->ebsi', x, routed_gate)
        u = jnp.einsum('bsh,ehi->ebsi', x, routed_up)
        h = jax.nn.silu(g) * u
        out_e = jnp.einsum('ebsi,eih->ebsh', h, routed_down)
        combined = jnp.einsum('ebsh,bse->bsh', out_e, combine_w)
        return shared_out + combined
    h = _L0_tok_ref(x, L0_tok_channel_weights)
    h = jnp.concatenate([h, txt], axis=1)
    h = h + _L0_attn_ref(_layernorm(h, axis=-1), L0_attn_Wqkv, L0_attn_Wproj, L0_attn_bproj, L0_attn_s_q, L0_attn_s_k, L0_attn_s_v, L0_attn_s_attn, L0_attn_s_after)
    h = h + _L0_ffn_ref(_layernorm(h, axis=-1), L0_ffn_g1, L0_ffn_b1, L0_ffn_g2, L0_ffn_b2, L0_ffn_Wr, L0_ffn_br, L0_ffn_Wq, L0_ffn_bq, L0_ffn_Wk, L0_ffn_bk, L0_ffn_Wv, L0_ffn_bv, L0_ffn_Wo, L0_ffn_bo, L0_ffn_Wm, L0_ffn_bm, L0_ffn_W1, L0_ffn_bf1, L0_ffn_W2, L0_ffn_bf2)
    h = h + _L1_attn_ref(_layernorm(h, axis=-1), L1_attn_qkv_w, L1_attn_qkv_b, L1_attn_qkv_B, L1_attn_proj_w, L1_attn_proj_b, L1_attn_proj_B)
    h = h + _L1_ffn_ref(_layernorm(h, axis=-1), L1_ffn_shared_gate, L1_ffn_shared_up, L1_ffn_shared_down, L1_ffn_routed_gate, L1_ffn_routed_up, L1_ffn_routed_down, L1_ffn_router_w, L1_ffn_routing_bias)
    return h

_drawn_inputs = setup_inputs


def setup_inputs(seed=0):
    import zlib

    import numpy as np

    out = dict(_drawn_inputs(seed))
    spreads = {'L0_attn_bproj': (0.0, 0.8),
     'L0_ffn_g1': (1.0, 0.6),
     'L0_ffn_b1': (0.0, 0.8),
     'L0_ffn_g2': (1.0, 0.6),
     'L0_ffn_b2': (0.0, 0.8),
     'L0_ffn_bq': (0.0, 0.8),
     'L0_ffn_bk': (0.0, 2.0),
     'L0_ffn_bv': (0.0, 0.8),
     'L0_ffn_bo': (0.0, 0.8),
     'L0_ffn_bm': (0.0, 0.8),
     'L0_ffn_bf1': (0.0, 0.8),
     'L0_ffn_bf2': (0.0, 0.8),
     'L1_attn_qkv_b': (0.0, 0.8),
     'L1_attn_proj_b': (0.0, 2.0),
     'L1_ffn_routing_bias': (0.0, 0.8)}
    factors = {'L0_ffn_Wr': 8.0,
     'L0_ffn_Wq': 8.0,
     'L0_ffn_Wk': 8.0,
     'L0_ffn_Wv': 8.0,
     'L0_ffn_Wo': 8.0,
     'L0_ffn_Wm': 8.0,
     'L0_ffn_W1': 8.0,
     'L0_ffn_W2': 8.0,
     'L1_attn_qkv_w': 8.0,
     'L1_attn_proj_w': 8.0,
     'L1_ffn_shared_gate': 8.0,
     'L1_ffn_shared_up': 8.0,
     'L1_ffn_shared_down': 8.0,
     'L1_ffn_routed_gate': 8.0,
     'L1_ffn_routed_up': 8.0,
     'L1_ffn_routed_down': 8.0,
     'L1_ffn_router_w': 8.0}
    for name, (base, spread) in spreads.items():
        noise = np.random.default_rng([zlib.crc32(name.encode()), seed]).standard_normal(out[name].shape)
        drawn = base * np.exp(spread * noise) if base else spread * noise
        out[name] = jnp.asarray(drawn.astype(out[name].dtype))
    for name, factor in factors.items():
        out[name] = (out[name] * factor).astype(out[name].dtype)
    return out
```

```python
from contextlib import ExitStack

import concourse.bass as bass
from concourse import mybir

F32 = mybir.dt.float32
BF16 = mybir.dt.bfloat16
ALU = mybir.AluOpType
ACT = mybir.ActivationFunctionType
AX = mybir.AxisListType

BATCH, CH, IMG, PATCH, D, TXT = 32, 12, 224, 16, 192, 77
GRID = IMG // PATCH
IMG_TOK = GRID * GRID
T = IMG_TOK + TXT
NC_ = 3
TC = T // NC_
KC = 96
NK = D // KC
H, HD = 12, 16
HP = 32
NG = 3
SEL = 41
F0, F1, NEXP = 768, 384, 4
EPS = 1e-5
MAGIC = 12582912.0
OFF = 128.0
HALF_ROWS = PATCH // 2
RING = 3
XP = 112
XG = CH * GRID * 2 // XP
TAIL = IMG_TOK - 2 * TC

STAGES = ["tokens", "norm0", "qkv0", "attn0", "proj0", "norm1", "gate", "route", "pick", "attn1", "merge",
          "norm2", "ffn0", "norm3", "qkv1", "rowmax", "attn2", "proj1", "norm4", "router", "ffn1"]
USES = {
    "A": dict(qkv0=1, attn0=6, route=1, attn1=2, merge=1, ffn0=1, qkv1=1, rowmax=6, attn2=6, ffn1=4),
    "B": dict(qkv0=1, attn0=6, attn1=1, ffn0=1, qkv1=1, rowmax=6, attn2=6, ffn1=4),
    "M": dict(tokens=1, norm0=1, qkv0=2, attn0=3, proj0=1, norm1=1, gate=1, route=2, pick=4, attn1=4,
              merge=1, norm2=1, ffn0=1, norm3=1, qkv1=1, rowmax=1, attn2=1, proj1=2, norm4=1, router=1, ffn1=4),
}
SLOTS = 2
TURNS = BATCH // SLOTS
TOTAL = {a: SLOTS * sum(USES[a].values()) for a in USES}
NORMS = 6
TURNED = ["norm0", "norm1", "norm2", "norm3", "norm4"]
VECTOR_STEPS, POOL_STEPS, CONSTS = 80, 14, 20


def use(area, stage, slot, k=0):
    before = sum(SLOTS * USES[area].get(s, 0) for s in STAGES[:STAGES.index(stage)])
    return before + slot * USES[area][stage] + k


def early_fusion(nc, ins, out):
    pooled_dram = nc.dram_tensor("pooled_dram", (BATCH, CH, GRID, 2, GRID), F32).ap()
    ctx = ExitStack()
    with ctx:
        def sb(name, shape, dt=F32):
            return ctx.enter_context(nc.sbuf_tensor(name, shape, dt))

        def sem(name):
            return ctx.enter_context(nc.semaphore(name))

        area = {"A": ctx.enter_context(nc.psum_tensor("area_a", [128, 3, 512], F32)),
                "B": ctx.enter_context(nc.psum_tensor("area_b", [128, 3, 512], F32)),
                "M": ctx.enter_context(nc.psum_tensor("area_m", [128, 2, 512], F32))}
        A, B, M = area["A"], area["B"], area["M"]
        m_tok = M[0:TC, :, :].rearrange("p b (h n) -> p (b h) n", h=2)[:, 0:NC_, 0:D]
        m_chan = M[0:KC, :, 0:T]

        ident = sb("ident", [128, 128])
        ones = sb("ones", [128, 128])
        ones_b = sb("ones_b", [128, 1], BF16)
        minus_half = sb("minus_half", [128, NC_])
        ranks = sb("ranks", [128, SEL])
        earlier = sb("earlier", [TC, NC_, T], BF16)
        head_row = sb("head_row", [44, H, TC], BF16)
        head_mask = sb("head_mask", [KC, 6])
        scal = sb("scal", [128, 16])
        cw = sb("cw", [CH, D])
        w_qk0 = sb("w_qk0", [KC, NK, 2, H, HP])
        w_v0 = sb("w_v0", [KC, NK, D])
        w_p0 = sb("w_p0", [128, 3, NG, D], BF16)
        rows = sb("rows", [TC, 10, D])
        bproj0, g1, b1, bv0, bo, g2, b2, bf2, bv1, bproj1 = [rows[:, i, :] for i in range(10)]
        w_r = sb("w_r", [KC, NK])
        w_f = sb("w_f", [KC, NK, 5, D])
        W_Q, W_K, W_V, W_O, W_M = range(5)
        b_qk = sb("b_qk", [KC, 2, NK])
        w1 = sb("w1", [KC, NK, F0])
        bf1 = sb("bf1", [128, F0 // 128])
        w2 = sb("w2", [128, F0 // 128, D])
        w_qk1 = sb("w_qk1", [KC, NK, 2, H, HP])
        b_qk1 = sb("b_qk1", [128, 2, NG])
        w_v1 = sb("w_v1", [KC, NK, D])
        w_p1 = sb("w_p1", [KC, NK, D])
        w_gu = sb("w_gu", [KC, NK, NEXP, 2, F1])
        w_dn = sb("w_dn", [128, NEXP, F1 // 128, D])
        w_router = sb("w_router", [KC, NK, 3])
        b_router = sb("b_router", [TC, 3])

        def two(name, shape, dt=F32):
            return [sb(f"{name}{s}", shape, dt) for s in range(SLOTS)]

        img = sb("img", [XP, RING, HALF_ROWS * IMG])
        part = two("part", [XP, XG, GRID])
        h = two("h", [TC, NC_, D])
        hb = two("hb", [TC, NC_, D])
        stats = two("stats", [TC, NC_, 6])
        mv = two("mv", [TC, NC_, 2])
        rstd = two("rstd", [TC, NC_])
        xn = two("xn", [TC, NC_, D])
        xn2 = two("xn2", [TC, NC_, D])
        v32 = xn2
        xT = two("xT", [KC, NK, T])
        vr = two("vr", [TC, NC_, D], BF16)
        v0 = two("v0", [TC, NC_, H, HP], BF16)
        vsum = two("vsum", [128, NG])
        pa = [sb(f"pa{i}", [TC, NC_, T], BF16) for i in range(2)]
        pq = [sb(f"pq{i}", [TC, NC_, T], BF16) for i in range(2)]
        o32 = two("o32", [128, T])
        o0 = two("o0", [128, NG, T], BF16)
        qkr = o0
        hid = two("hid", [128, F0 // 128, T])
        q2, k2 = ([x[:, 3 * i:3 * i + 3, :] for x in hid] for i in range(2))
        p1T = [x[0:TC, :, :].rearrange("p c t -> p (c t)")[:, 0:NC_ * 4 * 3 * SEL].rearrange(
            "p (c n) -> p c n", c=NC_) for x in hid]
        w_p0f, w_p0r = (x[:, 0:NG, 0:D] for x in hid)
        q0, k0 = ([x[:, 2 * i:2 * i + 2, :].rearrange("p c t -> p (c t)").bitcast(BF16)[:, 0:NG * T].rearrange(
            "p (g t) -> p g t", g=NG) for x in hid] for i in range(2))
        sg = two("sg", [128, NG, T])
        halves = [x[0:CH, 0:2, :].rearrange("p c t -> p (c t)")[:, 0:2 * IMG_TOK].rearrange(
            "p (i a j) -> p i a j", i=GRID, a=2) for x in sg]
        pooled = [x[0:CH, 2, 0:IMG_TOK] for x in sg]
        score_b = [x[0:TC, 0, :].rearrange("p (c t) -> p c t", c=NC_) for x in sg]
        ties = [x[0:TC, 2, :] for x in sg]
        qblk = [x[0:KC, 0:2, :].rearrange("p c t -> p (c t)")[:, 0:NK * 6 * SEL].rearrange(
            "p (c j q) -> p c j q", c=NK, j=6) for x in sg]
        qk32 = sg
        pTs = sb("pTs", [128, 2, NG, T])
        pT = [pTs[0:TC, i, :, :] for i in range(2)]
        p1 = [pTs[0:3 * SEL, :, :, :].rearrange("p a c t -> p (a c t)")[:, 0:4 * T].rearrange(
            "p (g t) -> p g t", g=4)] * SLOTS
        e_s = two("e_s", [TC, NC_])
        score = two("score", [TC, NC_])
        score_row = two("score_row", [TC, T])
        rank = two("rank", [TC, NC_])
        unpicked = two("unpicked", [TC, NC_])
        pick = two("pick", [TC, NC_, SEL])
        mean_s = two("mean_s", [KC, 4])
        mix_l = two("mix_l", [2, T])
        mix_r = two("mix_r", [2, D])
        selT = two("selT", [KC, NK, SEL])
        qsel = two("qsel", [KC, NK, SEL])
        k1 = two("k1", [KC, NK, T])
        v1 = two("v1", [TC, NC_, H, HD + 1])
        smx = two("smx", [3 * SEL, 4])
        rec = two("rec", [SEL, H])
        ctx1 = two("ctx1", [SEL, D])
        ctxT = two("ctxT", [KC, NK, SEL])
        ao = two("ao", [SEL, D])
        pickT = two("pickT", [SEL, T])
        hs = two("hs", [TC, NC_, D])
        mx = two("mx", [TC, NC_, H])
        mrow = two("mrow", [44, T], BF16)
        rec2 = two("rec2", [TC, NC_, H])
        lg = two("lg", [TC, NC_, 3])
        er = two("er", [TC, NC_, 3])
        pr = two("pr", [TC, NC_, 3])
        cmp_ = two("cmp", [TC, NC_, 6])
        cwt = two("cwt", [TC, NC_, 3])
        tot = two("tot", [TC, NC_])
        outb = hs

        full = {a: sem(f"{a.lower()}_full") for a in area}
        taken = {a: sem(f"{a.lower()}_taken") for a in area}
        (vector_step, pool_step, weights_in, zeroed, consts_ready, weights_ready,
         part_ready, pooled_ready, hb_ready, q0_ready, k0_ready, v0_ready,
         vsum_ready, clamped, o0_ready, h1_ready, spread_ready, score_ready, e_ready, row_ready,
         mean_ready, pick_ready, qblk_ready, v1_ready, smx_ready, p1_ready, ctx_ready, ao_ready,
         hs_ready, h2_ready, mx_ready, mrow_ready, o2_ready, h3_ready,
         logit_ready, er_ready, out_ready, out_done) = [sem(n) for n in (
             "vector_step pool_step weights_in zeroed consts_ready weights_ready "
             "part_ready pooled_ready hb_ready q0_ready k0_ready v0_ready "
             "vsum_ready clamped o0_ready h1_ready spread_ready score_ready e_ready row_ready "
             "mean_ready pick_ready qblk_ready v1_ready smx_ready p1_ready ctx_ready ao_ready "
             "hs_ready h2_ready mx_ready mrow_ready o2_ready h3_ready "
             "logit_ready er_ready out_ready out_done").split()]
        waits_apart = sem("waits_apart")
        image_in = [sem(f"image_in{i}") for i in range(RING)]
        text_in, halves_out, halves_in = ([sem(f"{x}{s}") for s in range(SLOTS)]
                                          for x in ("text_in", "halves_out", "halves_in"))
        stats_ready, rstd_ready = sem("stats_ready"), sem("rstd_ready")
        xn_ready = sem("xn_ready")
        pv0_used, pv2_used, hidden_ready = sem("pv0_used"), sem("pv2_used"), sem("hidden_ready")

        S_Q, S_K, S_V, S_ATT, S_AFT, BR, R_Q, R_K, R_V, C_P, C_O, N_BR, TMP = range(13)
        col = lambda c, n=128: scal[0:n, c:c + 1]

        loads = []

        def load(dst, src):
            loads.append((dst, src))

        for c, name in ((S_Q, "s_q"), (S_K, "s_k"), (S_V, "s_v"), (S_ATT, "s_attn"), (S_AFT, "s_after")):
            load(col(c), ins[f"L0_attn_{name}"].partition_broadcast(128))
        load(col(BR), ins["L0_ffn_br"].partition_broadcast(128))
        load(cw[:, :], ins["L0_tok_channel_weights"])
        for wt, name in ((w_qk0, "L0_attn_WqkvT"), (w_qk1, "L1_attn_qkv_wT")):
            for kc in range(NK):
                for j in range(2):
                    load(wt[:, kc, j, :, 0:HD],
                         ins[name][kc * KC:(kc + 1) * KC, j * D:(j + 1) * D].rearrange("p (h d) -> p h d", d=HD))
        chan = lambda a: a.rearrange("(k p) n -> p k n", p=KC)
        load(w_v0[:, :, :], chan(ins["L0_attn_WqkvT"][:, 2 * D:3 * D]))
        load(w_v1[:, :, :], chan(ins["L1_attn_qkv_wT"][:, 2 * D:3 * D]))
        wp = ins["L0_attn_WprojT"].rearrange("(g j d) n -> j d g n", g=NG, d=HD)
        for j in range(4):
            load(w_p0f[HP * j:HP * j + HD, :, :], wp[j])
        for i, name in enumerate(("L0_attn_bproj", "L0_ffn_g1", "L0_ffn_b1", "L0_ffn_bv", "L0_ffn_bo", "L0_ffn_g2",
                                  "L0_ffn_b2", "L0_ffn_bf2", None, "L1_attn_proj_b")):
            src = ins[name] if name else ins["L1_attn_qkv_b"][2 * D:3 * D]
            load(rows[:, i, :], src.partition_broadcast(TC))
        load(w_r[:, :], ins["L0_ffn_Wr"].rearrange("(k p) -> p k", p=KC))
        for i, name in enumerate(("Wq", "Wk", "Wv", "Wo", "Wm")):
            load(w_f[:, :, i, :], chan(ins[f"L0_ffn_{name}"]))
        for i, name in enumerate(("bq", "bk")):
            load(b_qk[:, i, :], ins[f"L0_ffn_{name}"].rearrange("(k p) -> p k", p=KC))
        load(w1[:, :, :], chan(ins["L0_ffn_W1"]))
        load(bf1[:, :], ins["L0_ffn_bf1"].rearrange("(c p) -> p c", p=128))
        load(w2[:, :, :], ins["L0_ffn_W2"].rearrange("(c p) n -> p c n", p=128))
        for i in range(2):
            bias = ins["L1_attn_qkv_b"][i * D:(i + 1) * D].rearrange("(g j d) -> j d g", g=NG, d=HD)
            for j in range(4):
                load(b_qk1[HP * j:HP * j + HD, i, :], bias[j])
        load(w_p1[:, :, :], chan(ins["L1_attn_proj_wT"]))
        for i, name in enumerate(("gate", "up")):
            load(w_gu[:, :, 0, i, :], chan(ins[f"L1_ffn_shared_{name}"]))
            for e in range(3):
                load(w_gu[:, :, e + 1, i, :], chan(ins[f"L1_ffn_routed_{name}"][e]))
        down = lambda a: a.rearrange("(c p) n -> p c n", p=128)
        load(w_dn[:, 0, :, :], down(ins["L1_ffn_shared_down"]))
        for e in range(3):
            load(w_dn[:, e + 1, :, :], down(ins["L1_ffn_routed_down"][e]))
        load(w_router[:, :, :], chan(ins["L1_ffn_router_w"]))
        load(b_router[:, :], ins["L1_ffn_routing_bias"].partition_broadcast(TC))
        for s in range(SLOTS):
            load(mix_r[s][1:2, :], ins["L0_ffn_bm"].rearrange("(a n) -> a n", a=1))

        img_dram = ins["x"].rearrange("b c (i r) w -> b (c i r w)", r=PATCH).rearrange(
            "b (g p n) -> b p g n", g=XG, p=XP)
        half_dram = pooled_dram.rearrange("b c i a j -> b (c i a j)").rearrange(
            "b (g p n) -> b p g n", g=XG, p=XP)

        def apart(eng):
            eng.sem_inc(waits_apart, 1)

        block = ctx.enter_context(nc.Block())

        @block.sync
        def _(sp):
            sp.wait_ge(zeroed, 7)
            with nc.allow_non_contiguous_dma(reason="vectors onto partitions, once"):
                for dst, src in loads:
                    sp.dma_start(dst, src).then_inc(weights_in, 16)
            for p_ in range(RING):
                sp.dma_start(img[:, p_, :], img_dram[p_ // XG, :, p_ % XG, :]).then_inc(image_in[p_], 16)

            def turn(it, first, last):
                base = it * SLOTS
                for s in range(SLOTS):
                    if not first:
                        sp.wait_ge(out_ready, base + (s - 1))
                    sp.dma_start(h[s][TAIL:TC, 2, :], ins["txt"][base + s]).then_inc(text_in[s], 16)
                for s in range(SLOTS):
                    for g_ in range(XG):
                        sp.wait_ge(part_ready, base * XG + (s * XG + g_ + 1))
                        if not (last and s == SLOTS - 1):
                            sp.dma_start(img[:, g_, :], img_dram[base + (s + 1), :, g_, :]).then_inc(image_in[g_], 16)
                    sp.dma_start(half_dram[base + s], part[s][:, :, :]).then_inc(halves_out[s], 16)
                    sp.wait_ge(halves_out[s], it * 16 + 16)
                    sp.dma_start(halves[s][:, :, :, :], pooled_dram[base + s]).then_inc(halves_in[s], 16)
                for s in range(SLOTS):
                    sp.wait_ge(out_ready, base + (s + 1))
                    for c in range(NC_):
                        sp.dma_start(out[base + s, c * TC:(c + 1) * TC, :], outb[s][:, c, :]).then_inc(out_done, 16)

            turn(0, True, False)
            with sp.Fori(1, TURNS - 1) as it:
                turn(it, False, False)
            turn(TURNS - 1, False, True)
            sp.wait_ge(out_done, 16 * NC_ * BATCH + 1)

        @block.gpsimd
        def _(pool):
            g = nc.gpsimd
            for t_ in (w_qk0[:, :, :, :, :], w_qk1[:, :, :, :, :], w_p0f[:, :, :], b_qk1[:, :, :], scal[:, :]):
                g.memset(t_, 0.0).then_inc(zeroed, 1)
            for s in range(SLOTS):
                g.memset(mix_l[s][:, :], 1.0).then_inc(zeroed, 1)
            n = 0

            def const(ins_):
                nonlocal n
                n += 1
                ins_.then_inc(consts_ready, 1)
                pool.wait_ge(consts_ready, n)

            const(g.memset(ident[:, :], 0.0))
            const(g.affine_select(out=ident[:, :], in_=ident[:, :], compare_op=ALU.not_equal, fill=1.0, base=0,
                                  pattern=[[-1, 128]], channel_multiplier=1))
            const(g.memset(ones[:, :], 1.0))
            const(g.memset(ones_b[:, :], 1.0))
            const(g.memset(minus_half[:, :], -0.5))
            const(g.iota(ranks[:, :], pattern=[[1, SEL]], base=0, channel_multiplier=0,
                         allow_small_or_imprecise_dtypes=True))
            const(g.memset(earlier[:, :, :], 1.0))
            const(g.affine_select(out=earlier[:, :, :], in_=earlier[:, :, :], compare_op=ALU.is_gt, fill=0.0, base=0,
                                  pattern=[[TC, NC_], [-1, T]], channel_multiplier=1))
            const(g.memset(head_row[:, :, :], 0.0))
            for base in (0, -32):
                const(g.affine_select(out=head_row[:, :, :], in_=head_row[:, :, :], compare_op=ALU.not_equal, fill=1.0,
                                      base=base, pattern=[[-1, H], [0, TC]], channel_multiplier=1))
            const(g.memset(head_mask[:, :], 1.0))
            const(g.affine_select(out=head_mask[:, :], in_=head_mask[:, :], compare_op=ALU.is_ge, fill=0.0, base=0,
                                  pattern=[[-HD, 6]], channel_multiplier=1))
            const(g.affine_select(out=head_mask[:, :], in_=head_mask[:, :], compare_op=ALU.is_ge, fill=0.0,
                                  base=HD - 1, pattern=[[HD, 6]], channel_multiplier=-1))
            for s in range(SLOTS):
                const(g.memset(v0[s][:, :, :, :], 0.0))
                const(g.memset(v1[s][:, :, :, :], 1.0))
                const(g.memset(mrow[s][:, :], 0.0))
            assert n == CONSTS, n
            pool.wait_ge(weights_in, 16 * len(loads))

            with pool.Fori(0, TURNS) as it:
                item = [pool.snap(it * SLOTS + (s + 1)) for s in range(SLOTS)]
                base_step = pool.snap(it * POOL_STEPS)
                base_norm = pool.snap(it * (SLOTS * NORMS))
                pool_a = pool.snap(it * TOTAL["A"])
                steps = 0

                def link(ins_):
                    nonlocal steps
                    steps += 1
                    ins_.then_inc(pool_step, 1)
                    pool.wait_ge(pool_step, base_step + steps)

                def inv_std(k):
                    for s in range(SLOTS):
                        pool.wait_ge(stats_ready, base_norm + (SLOTS * k + s + 1))
                        apart(pool)
                        link(g.tensor_scalar(rstd[s][:, :], mv[s][:, :, 1], EPS, None, ALU.add))
                        g.tensor_tensor(rstd[s][:, :], rstd[s][:, :], minus_half[0:TC, :],
                                        ALU.pow).then_inc(rstd_ready, 1)

                def add_row(dst, src, row):
                    return g.tensor_tensor(dst[:, :, :], src[:, :, :],
                                           row.unsqueeze(1).to_broadcast([TC, NC_, D]), ALU.add)

                inv_std(0)
                for s in range(SLOTS):
                    add_row(hb[s], h[s], bproj0).then_inc(hb_ready, 1)
                inv_std(1)
                inv_std(2)
                for s in range(SLOTS):
                    pool.wait_ge(taken["A"], pool_a + (use("A", "route", s) + 2))
                    apart(pool)
                    g.tensor_copy(mix_l[s][0:1, :], score_row[s][0:1, :]).then_inc(row_ready, 1)
                inv_std(3)
                for s in range(SLOTS):
                    pool.wait_ge(hs_ready, item[s])
                    link(g.tensor_tensor(hb[s][:, :, :], h[s][:, :, :], hs[s][:, :, :], ALU.add))
                    add_row(hb[s], hb[s], bf2).then_inc(hb_ready, 1)
                inv_std(4)
                for s in range(SLOTS):
                    pool.wait_ge(h2_ready, item[s])
                    add_row(hb[s], h[s], bproj1).then_inc(hb_ready, 1)
                inv_std(5)
                assert steps == POOL_STEPS, steps

        @block.scalar
        def _(act):
            a = nc.scalar
            act.wait_ge(consts_ready, CONSTS)
            act.wait_ge(weights_in, 16 * len(loads))
            act.wait_ge(weights_ready, 1)
            with act.Fori(0, TURNS) as it:
                item = [act.snap(it * SLOTS + (s + 1)) for s in range(SLOTS)]
                bases = {x: act.snap(it * TOTAL[x]) for x in area}
                heads = act.snap(it * (SLOTS * H))

                def await_full(x, stage, s, k=0):
                    act.wait_ge(full[x], bases[x] + (use(x, stage, s, k) + 1))

                def turned(stage):
                    for s in range(SLOTS):
                        await_full("M", stage, s)
                        a.copy(xT[s][:, :, :], m_chan).then_inc(taken["M"], 1)

                for s in range(SLOTS):
                    await_full("M", "tokens", s)
                    a.copy(h[s][:, 0:2, :], m_tok[:, 0:2, :])
                    a.copy(h[s][0:TAIL, 2, :], m_tok[0:TAIL, 2, :]).then_inc(taken["M"], 1)
                turned("norm0")
                for s in range(SLOTS):
                    act.wait_ge(vsum_ready, item[s])
                    for hh in range(H):
                        x = "AB"[hh % 2]
                        await_full(x, "attn0", s, hh // 2)
                        if s * H + hh >= 2:
                            act.wait_ge(clamped, heads + (s * H + hh - 1))
                        a.activation(pa[hh % 2][:, :, :], area[x][0:TC, :, 0:T], ACT.Copy, bias=OFF,
                                     scale=scal[0:TC, C_P:C_P + 1]).then_inc(taken[x], 1)
                turned("norm1")
                for s in range(SLOTS):
                    await_full("M", "gate", s)
                    a.activation(e_s[s][:, :], M[0:TC, 0, 0:NC_], ACT.Exp, bias=scal[0:TC, N_BR:N_BR + 1],
                                 scale=-1.0).then_inc(taken["M"], 1)
                for s in range(SLOTS):
                    await_full("M", "route", s, 1)
                    a.copy(mix_r[s][0:1, :], M[0:1, 0, 0:D]).then_inc(taken["M"], 1)
                for s in range(SLOTS):
                    await_full("M", "pick", s, 0)
                    a.copy(selT[s][:, :, :], M[0:KC, :, 0:SEL]).then_inc(taken["M"], 1)
                    await_full("M", "pick", s, 2)
                    for kc in range(NK):
                        last = a.activation(k1[s][:, kc, :], M[0:KC, kc, 0:T], ACT.Identity,
                                            bias=b_qk[:, 1, kc:kc + 1])
                    last.then_inc(taken["M"], 1)
                for s in range(SLOTS):
                    act.wait_ge(smx_ready, item[s])
                    for g_ in range(4):
                        x, at = ("A", g_) if g_ < 2 else ("B", g_ - 2)
                        ins_ = a.activation(p1[s][:, g_, :], area[x][0:3 * SEL, at, 0:T], ACT.Exp,
                                            bias=smx[s][:, g_:g_ + 1], scale=0.25)
                        if g_ % 2:
                            ins_.then_inc(taken[x], 1)
                    await_full("A", "attn1", s, 1)
                    a.copy(p1T[s][:, :, :], A[0:TC, :, 0:4 * 3 * SEL]).then_inc(taken["A"], 1)
                    await_full("M", "attn1", s, 1)
                    a.copy(ctxT[s][:, :, :], M[0:KC, :, 0:SEL]).then_inc(taken["M"], 1)
                    await_full("M", "attn1", s, 3)
                    a.copy(pickT[s][:, :], M[0:SEL, 0, 0:T]).then_inc(taken["M"], 1)
                turned("norm2")
                for s in range(SLOTS):
                    for x in "AB":
                        await_full(x, "ffn0", s)
                        for j in range(3):
                            i = j + 3 * "AB".index(x)
                            last = a.activation(hid[s][:, i, :], area[x][:, j, 0:T], ACT.Gelu, bias=bf1[:, i:i + 1])
                        last.then_inc(taken[x], 1)
                turned("norm3")
                for s in range(SLOTS):
                    await_full("B", "qkv1", s)
                    for g_ in range(NG):
                        last = a.activation(k2[s][:, g_, :], B[:, g_, 0:T], ACT.Identity, bias=b_qk1[:, 1, g_:g_ + 1])
                    last.then_inc(taken["B"], 1)
                for s in range(SLOTS):
                    for hh in range(H):
                        x = "AB"[hh % 2]
                        await_full(x, "attn2", s, hh // 2)
                        if s * H + hh >= 2:
                            act.wait_ge(pv2_used, heads + (s * H + hh - 1))
                        a.activation(pT[hh % 2][:, :, :], area[x][0:TC, :, 0:T], ACT.Exp,
                                     scale=0.25).then_inc(taken[x], 1)
                for s in range(SLOTS):
                    await_full("M", "proj1", s, 0)
                    a.copy(xT[s][:, :, :], m_chan).then_inc(taken["M"], 1)
                turned("norm4")
                for s in range(SLOTS):
                    act.wait_ge(logit_ready, item[s])
                    a.activation(er[s][:, :, :], lg[s][:, :, :], ACT.Exp, scale=-1.0).then_inc(er_ready, 1)
                for s in range(SLOTS):
                    for e in range(NEXP):
                        await_full("A", "ffn1", s, e)
                        if e:
                            act.wait_ge(taken["B"], bases["B"] + (use("B", "ffn1", s, e - 1) + 2))
                        a.activation(sg[s][:, :, :], A[:, :, 0:T], ACT.Silu).then_inc(taken["A"], 1)

        @block.vector
        def _(dve):
            v = nc.vector
            dve.wait_ge(weights_in, 16 * len(loads))
            dve.wait_ge(consts_ready, CONSTS)
            for x in area:
                dve.sem_inc(taken[x], 1)
            dve.sem_inc(out_done, 1)
            n = 0

            def once(ins_):
                nonlocal n
                n += 1
                ins_.then_inc(vector_step, 1)
                dve.wait_ge(vector_step, n)

            for dst, src in ((R_Q, S_Q), (R_K, S_K), (R_V, S_V)):
                once(v.reciprocal(col(dst), col(src)))
            once(v.tensor_scalar(col(TMP), col(S_ATT), float(T), None, ALU.mult))
            once(v.reciprocal(col(TMP), col(TMP)))
            once(v.tensor_tensor(col(C_P), col(S_Q), col(S_K), ALU.mult))
            once(v.tensor_scalar(col(C_P), col(C_P), col(TMP), HD ** -0.5, ALU.mult, ALU.mult))
            once(v.reciprocal(col(TMP), col(S_AFT)))
            once(v.tensor_tensor(col(C_O), col(S_ATT), col(S_V), ALU.mult))
            once(v.tensor_tensor(col(C_O), col(C_O), col(TMP), ALU.mult))
            once(v.tensor_scalar(col(N_BR), col(BR), -1.0, None, ALU.mult))
            once(v.tensor_copy(w_p0[:, 0, :, :], w_p0f[:, :, :]))
            once(v.tensor_tensor(w_p0r[:, :, :], w_p0f[:, :, :], w_p0[:, 0, :, :], ALU.subtract))
            once(v.tensor_copy(w_p0[:, 1, :, :], w_p0r[:, :, :]))
            once(v.tensor_tensor(w_p0r[:, :, :], w_p0r[:, :, :], w_p0[:, 1, :, :], ALU.subtract))
            once(v.tensor_copy(w_p0[:, 2, :, :], w_p0r[:, :, :]))
            v.tensor_copy(scal[:, 15:16], scal[:, TMP:TMP + 1]).then_inc(weights_ready, 1)
            once_steps = n

            with dve.Fori(0, TURNS) as it:
                item = [dve.snap(it * SLOTS + (s + 1)) for s in range(SLOTS)]
                bases = {x: dve.snap(it * TOTAL[x]) for x in area}
                base_step = dve.snap(it * VECTOR_STEPS + once_steps)
                base_norm = dve.snap(it * (SLOTS * NORMS))
                it16 = dve.snap(it * 16 + 16)
                hb_base = dve.snap(it * (SLOTS * 3))
                heads = dve.snap(it * (SLOTS * H))
                steps = 0

                def link(ins_):
                    nonlocal steps
                    steps += 1
                    ins_.then_inc(vector_step, 1)
                    dve.wait_ge(vector_step, base_step + steps)

                def await_full(x, stage, s, k=0):
                    dve.wait_ge(full[x], bases[x] + (use(x, stage, s, k) + 1))

                def norm(k, src, dst, gain=None, shift=None, signal=True):
                    for s in range(SLOTS):
                        for c in range(NC_):
                            last = v.bn_stats(stats[s][:, c, :], src[s][:, c, :])
                        link(last)
                        apart(dve)
                        for c in range(NC_):
                            last = v.bn_aggr(mv[s][:, c, :], stats[s][:, c, :])
                        last.then_inc(stats_ready, 1)
                    for s in range(SLOTS):
                        dve.wait_ge(rstd_ready, base_norm + (SLOTS * k + s + 1))
                        for c in range(NC_):
                            last = v.tensor_scalar(dst[s][:, c, :], src[s][:, c, :], mv[s][:, c, 0:1],
                                                   rstd[s][:, c:c + 1], ALU.subtract, ALU.mult)
                        if gain is not None:
                            link(last)
                            link(v.tensor_tensor(dst[s][:, :, :], dst[s][:, :, :],
                                                 gain.unsqueeze(1).to_broadcast([TC, NC_, D]), ALU.mult))
                            last = v.tensor_tensor(dst[s][:, :, :], dst[s][:, :, :],
                                                   shift.unsqueeze(1).to_broadcast([TC, NC_, D]), ALU.add)
                        if signal:
                            last.then_inc(xn_ready, 1)
                        else:
                            link(last)

                def quantise(dst, src, inv, t32, tr, x, ready):
                    v.tensor_scalar(t32, src, inv, MAGIC, ALU.mult, ALU.add).then_inc(taken[x], 1)
                    return t32, tr, dst, ready

                for s in range(SLOTS):
                    for g_ in range(XG):
                        dve.wait_ge(image_in[g_], it * (16 * SLOTS) + 16 * (s + 1))
                        v.tensor_reduce(
                            part[s][:, g_, :],
                            img[:, g_, :].rearrange("p (r j w) -> p j r w", r=HALF_ROWS, j=GRID), AX.XY,
                            ALU.add).then_inc(part_ready, 1)
                for s in range(SLOTS):
                    dve.wait_ge(halves_in[s], it16)
                    v.tensor_tensor(pooled[s][:, :].rearrange("p (i j) -> p i j", i=GRID), halves[s][:, :, 0, :],
                                    halves[s][:, :, 1, :], ALU.add).then_inc(pooled_ready, 1)
                for s in range(SLOTS):
                    dve.wait_ge(text_in[s], it16)
                    dve.wait_ge(taken["M"], bases["M"] + (use("M", "tokens", s) + 2))
                norm(0, h, xn)
                for s in range(SLOTS):
                    for x, inv, dst, ready in (("A", R_Q, q0, q0_ready), ("B", R_K, k0, k0_ready)):
                        await_full(x, "qkv0", s)
                        v.tensor_scalar(qk32[s][:, :, :], area[x][:, :, 0:T], col(inv), MAGIC, ALU.mult,
                                        ALU.add).then_inc(taken[x], 1)
                        dve.wait_ge(taken[x], bases[x] + (use(x, "qkv0", s) + 2))
                        link(v.tensor_scalar(qkr[s][:, :, :], qk32[s][:, :, :], MAGIC, -4.0, ALU.subtract, ALU.max))
                        v.tensor_scalar(dst[s][:, :, :], qkr[s][:, :, :], 3.0, None, ALU.min).then_inc(ready, 1)
                    await_full("M", "qkv0", s, 0)
                    v.tensor_scalar(v32[s][:, :, :], m_tok, col(R_V, TC), MAGIC, ALU.mult, ALU.add).then_inc(taken["M"], 1)
                    dve.wait_ge(taken["M"], bases["M"] + (use("M", "qkv0", s, 0) + 2))
                    link(v.tensor_scalar(vr[s][:, :, :], v32[s][:, :, :], MAGIC, -4.0, ALU.subtract, ALU.max))
                    v.tensor_scalar(v0[s][:, :, :, 0:HD].rearrange("p c h d -> p (c h) d"),
                                    vr[s][:, :, :].rearrange("p c (h d) -> p (c h) d", d=HD), 3.0, None,
                                    ALU.min).then_inc(v0_ready, 1)
                    await_full("M", "qkv0", s, 1)
                    v.tensor_scalar(vsum[s][:, :], M[:, 0, 0:NG], OFF, None, ALU.mult).then_inc(taken["M"], 1)
                    dve.wait_ge(taken["M"], bases["M"] + (use("M", "qkv0", s, 1) + 2))
                    v.tensor_copy(scal[:, 14:15], scal[:, TMP:TMP + 1]).then_inc(vsum_ready, 1)
                for s in range(SLOTS):
                    for hh in range(H + 1):
                        if hh < H:
                            x = "AB"[hh % 2]
                            dve.wait_ge(taken[x], bases[x] + (use(x, "attn0", s, hh // 2) + 2))
                            if s * H + hh >= 2:
                                dve.wait_ge(pv0_used, heads + (s * H + hh - 1))
                            v.tensor_scalar(pq[hh % 2][:, :, :], pa[hh % 2][:, :, :], OFF, OFF + 7.0, ALU.max,
                                            ALU.min).then_inc(clamped, 1)
                        if hh and hh % 4 == 0:
                            gr = hh // 4 - 1
                            await_full("M", "attn0", s, gr)
                            v.tensor_scalar(o32[s][:, :], M[:, gr % 2, 0:T], vsum[s][:, gr:gr + 1], col(C_O),
                                            ALU.subtract, ALU.mult).then_inc(taken["M"], 1)
                            dve.wait_ge(taken["M"], bases["M"] + (use("M", "attn0", s, gr) + 2))
                            link(v.tensor_scalar(o32[s][:, :], o32[s][:, :], MAGIC, MAGIC, ALU.add, ALU.subtract))
                            v.tensor_scalar(o0[s][:, gr, :], o32[s][:, :], -4.0, 3.0, ALU.max,
                                            ALU.min).then_inc(o0_ready, 1)
                for s in range(SLOTS):
                    await_full("M", "proj0", s)
                    dve.wait_ge(hb_ready, hb_base + (s + 1))
                    v.scalar_tensor_tensor(h[s][:, :, :], m_tok, col(S_AFT, TC), hb[s][:, :, :], ALU.mult,
                                           ALU.add).then_inc(taken["M"], 1)
                    dve.wait_ge(taken["M"], bases["M"] + (use("M", "proj0", s) + 2))
                norm(1, h, xn2, signal=False)
                norm(2, xn2, xn, g1, b1)
                for s in range(SLOTS):
                    dve.wait_ge(taken["M"], bases["M"] + (use("M", "gate", s) + 2))
                    link(v.tensor_scalar(score[s][:, :], e_s[s][:, :], 1.0, None, ALU.add))
                    link(v.reciprocal(score[s][:, :], score[s][:, :]))
                    v.tensor_copy(score_b[s][:, :, :], score[s][:, :].unsqueeze(2).to_broadcast([TC, NC_, TC]))\
                        .then_inc(spread_ready, 1)
                for s in range(SLOTS):
                    await_full("A", "route", s)
                    v.tensor_copy(score_row[s][:, :], A[0:TC, 0, 0:T]).then_inc(taken["A"], 1)
                    dve.wait_ge(taken["A"], bases["A"] + (use("A", "route", s) + 2))
                    await_full("M", "route", s, 0)
                    v.tensor_copy(mean_s[s][:, 0:3], M[0:KC, 0, 0:3]).then_inc(taken["M"], 1)
                    dve.wait_ge(taken["M"], bases["M"] + (use("M", "route", s, 0) + 2))
                    link(v.tensor_scalar(mean_s[s][:, 2:3], mean_s[s][:, 2:3], 1e-6, None, ALU.add))
                    link(v.reciprocal(mean_s[s][:, 3:4], mean_s[s][:, 2:3]))
                    v.tensor_scalar(mean_s[s][:, 0:2], mean_s[s][:, 0:2], mean_s[s][:, 3:4], None,
                                    ALU.mult).then_inc(mean_ready, 1)
                    for c in range(NC_):
                        link(v.scalar_tensor_tensor(ties[s][:, :], score_row[s][:, :], score[s][:, c:c + 1],
                                                    earlier[:, c, :], ALU.is_equal, ALU.mult))
                        link(v.scalar_tensor_tensor(ties[s][:, :], score_row[s][:, :], score[s][:, c:c + 1],
                                                    ties[s][:, :], ALU.is_lt, ALU.add, accum_out=rank[s][:, c:c + 1]))
                    for c in range(NC_):
                        v.tensor_scalar(pick[s][:, c, :], ranks[0:TC, :], rank[s][:, c:c + 1], None, ALU.is_equal)
                    v.tensor_scalar(unpicked[s][:, :], rank[s][:, :], float(SEL), None, ALU.is_ge)\
                        .then_inc(pick_ready, 1)
                for s in range(SLOTS):
                    await_full("M", "pick", s, 1)
                    v.tensor_tensor(qsel[s][:, :, :], M[0:KC, :, 0:SEL],
                                    b_qk[:, 0, :].unsqueeze(2).to_broadcast([KC, NK, SEL]), ALU.add)\
                        .then_inc(taken["M"], 1)
                    dve.wait_ge(taken["M"], bases["M"] + (use("M", "pick", s, 1) + 2))
                    for kc in range(NK):
                        last = v.tensor_tensor(qblk[s][:, kc, :, :],
                                               qsel[s][:, kc, :].unsqueeze(1).to_broadcast([KC, 6, SEL]),
                                               head_mask[:, :].unsqueeze(2).to_broadcast([KC, 6, SEL]), ALU.mult)
                    last.then_inc(qblk_ready, 1)
                    await_full("M", "pick", s, 3)
                    for c in range(NC_):
                        last = v.tensor_tensor(v1[s][:, c, :, 0:HD], m_tok[:, c, :].rearrange("p (h d) -> p h d", d=HD),
                                               bv0.rearrange("p (h d) -> p h d", d=HD), ALU.add)
                    last.then_inc(taken["M"], 1)
                for s in range(SLOTS):
                    for x, at in (("A", 0), ("B", 2)):
                        await_full(x, "attn1", s, 0)
                        last = v.tensor_reduce(smx[s][:, at:at + 2], area[x][0:3 * SEL, 0:2, 0:T], AX.X, ALU.max)
                    link(last)
                    v.tensor_scalar(smx[s][:, :], smx[s][:, :], -0.25, None, ALU.mult).then_inc(smx_ready, 1)
                    await_full("M", "attn1", s, 0)
                    heads_out = M[0:SEL, 0, 0:H * (HD + 1)].rearrange("p (h d) -> p h d", d=HD + 1)
                    link(v.reciprocal(rec[s][:, :], heads_out[:, :, HD]))
                    v.tensor_tensor(ctx1[s][:, :].rearrange("p (h d) -> p h d", d=HD), heads_out[:, :, 0:HD],
                                    rec[s][:, :].unsqueeze(2).to_broadcast([SEL, H, HD]), ALU.mult)\
                        .then_inc(taken["M"], 1)
                    await_full("M", "attn1", s, 2)
                    v.tensor_tensor(ao[s][:, :], M[0:SEL, 0, 0:D], bo[0:SEL, :], ALU.add).then_inc(taken["M"], 1)
                dve.wait_ge(out_done, it * (SLOTS * NC_ * 16) + 1)
                for s in range(SLOTS):
                    await_full("M", "merge", s)
                    v.tensor_tensor(hs[s][:, :, :], m_tok, xn2[s][:, :, :], ALU.add).then_inc(taken["M"], 1)
                    dve.wait_ge(taken["M"], bases["M"] + (use("M", "merge", s) + 2))
                    await_full("A", "merge", s)
                    for c in range(NC_):
                        last = v.scalar_tensor_tensor(hs[s][:, c, :], A[0:TC, c, 0:D], unpicked[s][:, c:c + 1],
                                                      hs[s][:, c, :], ALU.mult, ALU.add)
                    last.then_inc(taken["A"], 1)
                    dve.wait_ge(taken["A"], bases["A"] + (use("A", "merge", s) + 2))
                    v.tensor_copy(scal[:, 14:15], scal[:, TMP:TMP + 1]).then_inc(hs_ready, 1)
                norm(3, hs, xn, g2, b2)
                for s in range(SLOTS):
                    await_full("M", "ffn0", s)
                    dve.wait_ge(hb_ready, hb_base + (SLOTS + s + 1))
                    v.tensor_tensor(h[s][:, :, :], m_tok, hb[s][:, :, :], ALU.add).then_inc(taken["M"], 1)
                    dve.wait_ge(taken["M"], bases["M"] + (use("M", "ffn0", s) + 2))
                    v.tensor_copy(scal[:, 14:15], scal[:, TMP:TMP + 1]).then_inc(h2_ready, 1)
                norm(4, h, xn)
                for s in range(SLOTS):
                    await_full("A", "qkv1", s)
                    v.tensor_tensor(q2[s][:, :, :], A[:, :, 0:T],
                                    b_qk1[:, 0, :].unsqueeze(2).to_broadcast([128, NG, T]), ALU.add)\
                        .then_inc(taken["A"], 1)
                    await_full("M", "qkv1", s)
                    for c in range(NC_):
                        last = v.tensor_tensor(v1[s][:, c, :, 0:HD], m_tok[:, c, :].rearrange("p (h d) -> p h d", d=HD),
                                               bv1.rearrange("p (h d) -> p h d", d=HD), ALU.add)
                    last.then_inc(taken["M"], 1)
                for s in range(SLOTS):
                    for hh in range(H):
                        x = "AB"[hh % 2]
                        await_full(x, "rowmax", s, hh // 2)
                        v.tensor_reduce(mx[s][:, :, hh], area[x][0:TC, :, 0:T], AX.X, ALU.max).then_inc(taken[x], 1)
                    dve.wait_ge(taken["B"], bases["B"] + (use("B", "rowmax", s, 5) + 2))
                    v.tensor_scalar(mx[s][:, :, :], mx[s][:, :, :], -1.0, None, ALU.mult).then_inc(mx_ready, 1)
                    await_full("M", "rowmax", s)
                    link(v.tensor_copy(mrow[s][0:H, :], M[0:H, 0, 0:T]))
                    v.tensor_tensor(mrow[s][32:32 + H, :], M[0:H, 0, 0:T], mrow[s][0:H, :], ALU.subtract)\
                        .then_inc(taken["M"], 1)
                for s in range(SLOTS):
                    await_full("M", "attn2", s)
                    heads_out = M[0:TC, :, :].rearrange("p b (i n) -> p (b i) n", i=2)[:, 0:NC_, 0:H * (HD + 1)]
                    link(v.reciprocal(rec2[s][:, :, :],
                                      heads_out.rearrange("p c (h d) -> p c h d", d=HD + 1)[:, :, :, HD]))
                    for c in range(NC_):
                        last = v.tensor_tensor(xn[s][:, c, :].rearrange("p (h d) -> p h d", d=HD),
                                               heads_out[:, c, :].rearrange("p (h d) -> p h d", d=HD + 1)[:, :, 0:HD],
                                               rec2[s][:, c, :].unsqueeze(2).to_broadcast([TC, H, HD]), ALU.mult)
                    last.then_inc(taken["M"], 1)
                for s in range(SLOTS):
                    await_full("M", "proj1", s, 1)
                    dve.wait_ge(hb_ready, hb_base + (2 * SLOTS + s + 1))
                    v.tensor_tensor(h[s][:, :, :], m_tok, hb[s][:, :, :], ALU.add).then_inc(taken["M"], 1)
                    dve.wait_ge(taken["M"], bases["M"] + (use("M", "proj1", s, 1) + 2))
                norm(5, h, xn)
                for s in range(SLOTS):
                    await_full("M", "router", s)
                    v.tensor_tensor(lg[s][:, :, :], M[0:TC, 0, 0:9].rearrange("p (c e) -> p c e", e=3),
                                    b_router[:, :].unsqueeze(1).to_broadcast([TC, NC_, 3]), ALU.add)\
                        .then_inc(taken["M"], 1)
                    dve.wait_ge(taken["M"], bases["M"] + (use("M", "router", s) + 2))
                    v.tensor_copy(scal[:, 14:15], scal[:, TMP:TMP + 1]).then_inc(logit_ready, 1)
                for s in range(SLOTS):
                    dve.wait_ge(er_ready, item[s])
                    link(v.tensor_scalar(pr[s][:, :, :], er[s][:, :, :], 1.0, None, ALU.add))
                    link(v.reciprocal(pr[s][:, :, :], pr[s][:, :, :]))
                    pe_ = [pr[s][:, :, e] for e in range(3)]
                    pairs = ((0, 1, ALU.is_lt), (0, 2, ALU.is_lt), (1, 0, ALU.is_le), (1, 2, ALU.is_lt),
                             (2, 0, ALU.is_le), (2, 1, ALU.is_le))
                    for i, (e, o, op) in enumerate(pairs):
                        last = v.tensor_tensor(cmp_[s][:, :, i], pe_[e], pe_[o], op)
                    link(last)
                    for e in range(3):
                        last = v.tensor_tensor(cwt[s][:, :, e], cmp_[s][:, :, 2 * e], cmp_[s][:, :, 2 * e + 1], ALU.mult)
                    link(last)
                    link(v.tensor_scalar(cwt[s][:, :, :], cwt[s][:, :, :], -1.0, 1.0, ALU.mult, ALU.add))
                    link(v.tensor_tensor(cwt[s][:, :, :], cwt[s][:, :, :], pr[s][:, :, :], ALU.mult))
                    link(v.tensor_reduce(tot[s][:, :], cwt[s][:, :, :], AX.X, ALU.add))
                    link(v.reciprocal(tot[s][:, :], tot[s][:, :]))
                    link(v.tensor_tensor(cwt[s][:, :, :], cwt[s][:, :, :],
                                         tot[s][:, :].unsqueeze(2).to_broadcast([TC, NC_, 3]), ALU.mult))
                for s in range(SLOTS):
                    for e in range(NEXP):
                        await_full("B", "ffn1", s, e)
                        dve.wait_ge(taken["A"], bases["A"] + (use("A", "ffn1", s, e) + 2))
                        if e >= 2:
                            await_full("M", "ffn1", s, e - 2)
                        v.tensor_tensor(hid[s][:, 3 * (e % 2):3 * (e % 2) + 3, :], sg[s][:, :, :], B[:, :, 0:T],
                                        ALU.mult).then_inc(taken["B"], 1)
                        if e:
                            await_full("M", "ffn1", s, e - 1)
                            if e == 1:
                                v.tensor_tensor(outb[s][:, :, :], m_tok, h[s][:, :, :], ALU.add).then_inc(taken["M"], 1)
                            else:
                                for c in range(NC_):
                                    last = v.scalar_tensor_tensor(outb[s][:, c, :], m_tok[:, c, :],
                                                                  cwt[s][:, c, e - 2:e - 1], outb[s][:, c, :],
                                                                  ALU.mult, ALU.add)
                                last.then_inc(taken["M"], 1)
                            dve.wait_ge(taken["M"], bases["M"] + (use("M", "ffn1", s, e - 1) + 2))
                    await_full("M", "ffn1", s, 3)
                    for c in range(NC_):
                        last = v.scalar_tensor_tensor(outb[s][:, c, :], m_tok[:, c, :], cwt[s][:, c, 2:3],
                                                      outb[s][:, c, :], ALU.mult, ALU.add)
                    last.then_inc(taken["M"], 1)
                    dve.wait_ge(taken["M"], bases["M"] + (use("M", "ffn1", s, 3) + 2))
                    v.tensor_copy(scal[:, 14:15], scal[:, TMP:TMP + 1]).then_inc(out_ready, 1)
                assert steps == VECTOR_STEPS, steps

        @block.tensor
        def _(pe):
            mm = nc.tensor.matmul
            pe.wait_ge(consts_ready, CONSTS)
            pe.wait_ge(weights_in, 16 * len(loads))
            pe.wait_ge(weights_ready, 1)
            with pe.Fori(0, TURNS) as it:
                item = [pe.snap(it * SLOTS + (s + 1)) for s in range(SLOTS)]
                bases = {x: pe.snap(it * TOTAL[x]) for x in area}
                turned_base = pe.snap(it * (SLOTS * len(TURNED)))
                heads = pe.snap(it * (SLOTS * H))
                o0_base = pe.snap(it * (SLOTS * NG))

                def begin(x, stage, s, k=0, lag=0):
                    pe.wait_ge(taken[x], bases[x] + (use(x, stage, s, k) + 1 - lag))

                def await_taken(x, stage, s, k=0):
                    pe.wait_ge(taken[x], bases[x] + (use(x, stage, s, k) + 2))

                def turn_tokens(stage, s, src):
                    pe.wait_ge(xn_ready, turned_base + (SLOTS * TURNED.index(stage) + s + 1))
                    begin("M", stage, s)
                    for kc in range(NK):
                        for c in range(NC_):
                            last = nc.tensor.transpose(M[0:KC, kc, c * TC:(c + 1) * TC],
                                                       src[:, c, kc * KC:(kc + 1) * KC], ident[0:TC, 0:TC])
                    last.then_inc(full["M"], 1)

                def channels(x, outs, w, rhs, n=T):
                    for o_, w_ in zip(outs, w):
                        for kc in range(NK):
                            last = mm(o_, w_(kc), rhs[:, kc, 0:n], start=(kc == 0), stop=(kc == NK - 1))
                    last.then_inc(full[x], 1)

                def tokens(lhs, w, x="M", dst=None, more=None):
                    for c in range(NC_):
                        parts = len(w)
                        for i in range(parts):
                            last = mm((m_tok if dst is None else dst)[:, c, :], lhs(i, c), w[i],
                                      start=(i == 0), stop=(i == parts - 1))
                    last.then_inc(full[x], 1)

                for s in range(SLOTS):
                    pe.wait_ge(pooled_ready, item[s])
                    begin("M", "tokens", s)
                    for c in range(NC_):
                        n_ = TC if c < 2 else TAIL
                        last = mm(m_tok[0:n_, c, :], pooled[s][:, c * TC:c * TC + n_], cw[:, :], start=True, stop=True)
                    last.then_inc(full["M"], 1)
                for s in range(SLOTS):
                    turn_tokens("norm0", s, xn[s])
                for s in range(SLOTS):
                    await_taken("M", "norm0", s)
                    for j, x in enumerate("AB"):
                        begin(x, "qkv0", s)
                        channels(x, [area[x][:, g_, 0:T] for g_ in range(NG)],
                                 [lambda kc, g_=g_: w_qk0[:, kc, j, 4 * g_:4 * g_ + 4, :].rearrange("p h d -> p (h d)")
                                  for g_ in range(NG)], xT[s])
                    begin("M", "qkv0", s, 0)
                    tokens(lambda i, c: xT[s][:, i, c * TC:(c + 1) * TC], [w_v0[:, i, :] for i in range(NK)])
                    pe.wait_ge(v0_ready, item[s])
                    begin("M", "qkv0", s, 1)
                    for g_ in range(NG):
                        for c in range(NC_):
                            last = mm(M[:, 0, g_:g_ + 1],
                                      v0[s][:, c, 4 * g_:4 * g_ + 4, :].rearrange("p h d -> p (h d)"),
                                      ones_b[0:TC, :], start=(c == 0), stop=(c == NC_ - 1))
                    last.then_inc(full["M"], 1)

                def scores(x, s, hh, stage, lhs, rhs):
                    begin(x, stage, s, hh // 2)
                    g_, j = hh // 4, hh % 4
                    rows_ = slice(HP * j, HP * j + HD)
                    for c in range(NC_):
                        last = mm(area[x][0:TC, c, 0:T], lhs[s][rows_, g_, c * TC:(c + 1) * TC], rhs[s][rows_, g_, :],
                                  start=True, stop=(stage != "attn2"))
                        if stage == "attn2":
                            last = mm(area[x][0:TC, c, 0:T], head_row[:, hh, :], mrow[s][:, :], start=False, stop=True)
                    last.then_inc(full[x], 1)

                for s in range(SLOTS):
                    pe.wait_ge(q0_ready, item[s])
                    pe.wait_ge(k0_ready, item[s])
                    for hh in range(H + 1):
                        if hh < H:
                            scores("AB"[hh % 2], s, hh, "attn0", k0, q0)
                        if hh:
                            p = hh - 1
                            g_, j = p // 4, p % 4
                            if j == 0:
                                begin("M", "attn0", s, g_, lag=(1 if g_ else 0))
                            pe.wait_ge(clamped, heads + (s * H + p + 1))
                            for c in range(NC_):
                                last = mm(M[HP * j:HP * j + HP, g_ % 2, 0:T], v0[s][:, c, p, :], pq[p % 2][:, c, :],
                                          start=(c == 0), stop=(c == NC_ - 1))
                            last.then_inc(pv0_used, 1)
                            if j == 3:
                                nc.tensor.matmul(M[0:1, g_ % 2, T:T + 1], ones_b[0:1, :], ones_b[0:1, :], start=True, stop=True).then_inc(full["M"], 1)
                for s in range(SLOTS):
                    pe.wait_ge(o0_ready, o0_base + (NG * (s + 1)))
                    begin("M", "proj0", s)
                    tokens(lambda i, c: o0[s][:, i % NG, c * TC:(c + 1) * TC],
                           [w_p0[:, i // NG, i % NG, :] for i in range(3 * NG)])
                for s in range(SLOTS):
                    turn_tokens("norm1", s, xn[s])
                for s in range(SLOTS):
                    await_taken("M", "norm1", s)
                    begin("M", "gate", s)
                    for c in range(NC_):
                        for kc in range(NK):
                            last = mm(M[0:TC, 0, c:c + 1], xT[s][:, kc, c * TC:(c + 1) * TC], w_r[:, kc:kc + 1],
                                      start=(kc == 0), stop=(kc == NK - 1))
                    last.then_inc(full["M"], 1)
                for s in range(SLOTS):
                    pe.wait_ge(spread_ready, item[s])
                    begin("A", "route", s)
                    apart(pe)
                    for c in range(NC_):
                        last = nc.tensor.transpose(A[0:TC, 0, c * TC:(c + 1) * TC], score_b[s][:, c, :],
                                                   ident[0:TC, 0:TC])
                    last.then_inc(full["A"], 1)
                    begin("M", "route", s, 0)
                    for j in range(NK + 1):
                        for c in range(NC_):
                            lhs = xn[s][:, c, j * KC:(j + 1) * KC] if j < NK else ones[0:TC, 0:KC]
                            last = mm(M[0:KC, 0, j:j + 1], lhs, score[s][:, c:c + 1], start=(c == 0), stop=(c == NC_ - 1))
                    last.then_inc(full["M"], 1)
                    pe.wait_ge(mean_ready, item[s])
                    begin("M", "route", s, 1)
                    for kc in range(NK):
                        last = mm(M[0:1, 0, 0:D], mean_s[s][:, kc:kc + 1], w_f[:, kc, W_M, :], start=(kc == 0),
                                  stop=(kc == NK - 1))
                    last.then_inc(full["M"], 1)
                for s in range(SLOTS):
                    pe.wait_ge(pick_ready, item[s])
                    begin("M", "pick", s, 0)
                    for kc in range(NK):
                        for c in range(NC_):
                            last = mm(M[0:KC, kc, 0:SEL], xn[s][:, c, kc * KC:(kc + 1) * KC], pick[s][:, c, :],
                                      start=(c == 0), stop=(c == NC_ - 1))
                    last.then_inc(full["M"], 1)
                    begin("M", "pick", s, 1)
                    channels("M", [M[0:KC, m, 0:SEL] for m in range(NK)],
                             [lambda kc, m=m: w_f[:, kc, W_Q, m * KC:(m + 1) * KC] for m in range(NK)], selT[s], SEL)
                    begin("M", "pick", s, 2)
                    channels("M", [M[0:KC, m, 0:T] for m in range(NK)],
                             [lambda kc, m=m: w_f[:, kc, W_K, m * KC:(m + 1) * KC] for m in range(NK)], xT[s])
                    begin("M", "pick", s, 3)
                    tokens(lambda i, c: xT[s][:, i, c * TC:(c + 1) * TC], [w_f[:, i, W_V, :] for i in range(NK)])
                for s in range(SLOTS):
                    pe.wait_ge(qblk_ready, item[s])
                    await_taken("M", "pick", s, 2)
                    for x, at in (("A", 0), ("B", 2)):
                        begin(x, "attn1", s, 0)
                        for b_ in range(2):
                            g_ = at + b_
                            lhs = qblk[s][:, g_ // 2, 3 * (g_ % 2):3 * (g_ % 2) + 3, :].rearrange("p h q -> p (h q)")
                            last = mm(area[x][0:3 * SEL, b_, 0:T], lhs, k1[s][:, g_ // 2, :], start=True, stop=True)
                        last.then_inc(full[x], 1)
                    await_taken("B", "attn1", s, 0)
                    begin("A", "attn1", s, 1)
                    apart(pe)
                    for c in range(NC_):
                        for g_ in range(4):
                            last = nc.tensor.transpose(A[0:TC, c, g_ * 3 * SEL:(g_ + 1) * 3 * SEL],
                                                       p1[s][:, g_, c * TC:(c + 1) * TC], ident[0:3 * SEL, 0:3 * SEL])
                    last.then_inc(full["A"], 1)
                    await_taken("A", "attn1", s, 1)
                    begin("M", "attn1", s, 0)
                    for hh in range(H):
                        for c in range(NC_):
                            last = mm(M[0:SEL, 0, hh * (HD + 1):(hh + 1) * (HD + 1)],
                                      p1T[s][:, c, hh * SEL:(hh + 1) * SEL], v1[s][:, c, hh, :],
                                      start=(c == 0), stop=(c == NC_ - 1))
                    last.then_inc(full["M"], 1)
                    begin("M", "attn1", s, 1)
                    apart(pe)
                    for kc in range(NK):
                        last = nc.tensor.transpose(M[0:KC, kc, 0:SEL], ctx1[s][:, kc * KC:(kc + 1) * KC],
                                                   ident[0:SEL, 0:SEL])
                    last.then_inc(full["M"], 1)
                    begin("M", "attn1", s, 2)
                    for kc in range(NK):
                        last = mm(M[0:SEL, 0, 0:D], ctxT[s][:, kc, :], w_f[:, kc, W_O, :], start=(kc == 0),
                                  stop=(kc == NK - 1))
                    last.then_inc(full["M"], 1)
                    begin("M", "attn1", s, 3)
                    apart(pe)
                    for c in range(NC_):
                        last = nc.tensor.transpose(M[0:SEL, 0, c * TC:(c + 1) * TC], pick[s][:, c, :],
                                                   ident[0:TC, 0:TC])
                    last.then_inc(full["M"], 1)
                for s in range(SLOTS):
                    await_taken("M", "attn1", s, 3)
                    begin("M", "merge", s)
                    tokens(lambda i, c: pickT[s][:, c * TC:(c + 1) * TC], [ao[s][:, :]])
                    pe.wait_ge(row_ready, item[s])
                    begin("A", "merge", s)
                    tokens(lambda i, c: (xT[s][:, i, c * TC:(c + 1) * TC] if i < NK
                                         else mix_l[s][:, c * TC:(c + 1) * TC]),
                           [w_f[:, 0, W_M, :], w_f[:, 1, W_M, :], mix_r[s][:, :]], "A", A[0:TC, :, 0:D])
                for s in range(SLOTS):
                    turn_tokens("norm2", s, xn[s])
                for s in range(SLOTS):
                    await_taken("M", "norm2", s)
                    for x, at in (("A", 0), ("B", 3)):
                        begin(x, "ffn0", s)
                        channels(x, [area[x][:, j, 0:T] for j in range(3)],
                                 [lambda kc, j=j: w1[:, kc, (at + j) * 128:(at + j + 1) * 128] for j in range(3)], xT[s])
                for s in range(SLOTS):
                    await_taken("B", "ffn0", s)
                    begin("M", "ffn0", s)
                    tokens(lambda i, c: hid[s][:, i, c * TC:(c + 1) * TC], [w2[:, i, :] for i in range(F0 // 128)])
                for s in range(SLOTS):
                    turn_tokens("norm3", s, xn[s])
                for s in range(SLOTS):
                    await_taken("M", "norm3", s)
                    for j, x in enumerate("AB"):
                        begin(x, "qkv1", s)
                        channels(x, [area[x][:, g_, 0:T] for g_ in range(NG)],
                                 [lambda kc, g_=g_: w_qk1[:, kc, j, 4 * g_:4 * g_ + 4, :].rearrange("p h d -> p (h d)")
                                  for g_ in range(NG)], xT[s])
                    begin("M", "qkv1", s)
                    tokens(lambda i, c: xT[s][:, i, c * TC:(c + 1) * TC], [w_v1[:, i, :] for i in range(NK)])
                for s in range(SLOTS):
                    await_taken("A", "qkv1", s)
                    await_taken("B", "qkv1", s)
                    for hh in range(H):
                        scores("AB"[hh % 2], s, hh, "rowmax", q2, k2)
                    pe.wait_ge(mx_ready, item[s])
                    begin("M", "rowmax", s)
                    apart(pe)
                    for c in range(NC_):
                        last = nc.tensor.transpose(M[0:H, 0, c * TC:(c + 1) * TC], mx[s][:, c, :], ident[0:TC, 0:TC])
                    last.then_inc(full["M"], 1)
                for s in range(SLOTS):
                    await_taken("M", "rowmax", s)
                    for hh in range(H + 1):
                        if hh < H:
                            scores("AB"[hh % 2], s, hh, "attn2", k2, q2)
                        if hh:
                            p = hh - 1
                            if p == 0:
                                begin("M", "attn2", s)
                            await_taken("AB"[p % 2], "attn2", s, p // 2)
                            for qc in range(NC_):
                                for c in range(NC_):
                                    at = (qc % 2) * 256 + p * (HD + 1)
                                    last = mm(M[0:TC, qc // 2, at:at + HD + 1], pT[p % 2][:, c, qc * TC:(qc + 1) * TC],
                                              v1[s][:, c, p, :], start=(c == 0), stop=(c == NC_ - 1))
                            last.then_inc(pv2_used, 1)
                    mm(M[0:1, 1, 511:512], ones_b[0:1, :], ones_b[0:1, :], start=True, stop=True).then_inc(full["M"], 1)
                for s in range(SLOTS):
                    await_taken("M", "attn2", s)
                    begin("M", "proj1", s, 0)
                    for kc in range(NK):
                        for c in range(NC_):
                            last = nc.tensor.transpose(M[0:KC, kc, c * TC:(c + 1) * TC],
                                                       xn[s][:, c, kc * KC:(kc + 1) * KC], ident[0:TC, 0:TC])
                    last.then_inc(full["M"], 1)
                    await_taken("M", "proj1", s, 0)
                    begin("M", "proj1", s, 1)
                    tokens(lambda i, c: xT[s][:, i, c * TC:(c + 1) * TC], [w_p1[:, i, :] for i in range(NK)])
                for s in range(SLOTS):
                    turn_tokens("norm4", s, xn[s])
                for s in range(SLOTS):
                    await_taken("M", "norm4", s)
                    begin("M", "router", s)
                    for c in range(NC_):
                        for kc in range(NK):
                            last = mm(M[0:TC, 0, 3 * c:3 * c + 3], xT[s][:, kc, c * TC:(c + 1) * TC],
                                      w_router[:, kc, :], start=(kc == 0), stop=(kc == NK - 1))
                    last.then_inc(full["M"], 1)
                for s in range(SLOTS):
                    for e in range(NEXP + 1):
                        if e < NEXP:
                            for i, x in enumerate("AB"):
                                begin(x, "ffn1", s, e)
                                channels(x, [area[x][:, j, 0:T] for j in range(3)],
                                         [lambda kc, j=j: w_gu[:, kc, e, i, j * 128:(j + 1) * 128] for j in range(3)],
                                         xT[s])
                        if e:
                            await_taken("B", "ffn1", s, e - 1)
                            begin("M", "ffn1", s, e - 1)
                            tokens(lambda i, c: hid[s][:, 3 * ((e - 1) % 2) + i, c * TC:(c + 1) * TC],
                                   [w_dn[:, e - 1, i, :] for i in range(3)])


_TRANSPOSED = {"L0_attn_Wqkv": "L0_attn_WqkvT", "L0_attn_Wproj": "L0_attn_WprojT", "L1_attn_qkv_w": "L1_attn_qkv_wT",
               "L1_attn_proj_w": "L1_attn_proj_wT"}
_UNUSED = {"L1_attn_qkv_B", "L1_attn_proj_B"}


def kernel(**inputs):
    import numpy as np
    import concourse.bacc as bacc
    from concourse.bass_utils import run_bass_kernel_spmd

    nc = bacc.Bacc("TRN2", target_bir_lowering=False, num_devices=1)
    arrays, args = {}, {}
    for name, value in inputs.items():
        if name in _UNUSED:
            continue
        a = np.asarray(value)
        if name in _TRANSPOSED:
            name, a = _TRANSPOSED[name], a.T
        if a.ndim == 0:
            a = a.reshape(1)
        a = np.ascontiguousarray(a)
        arrays[f"in_{name}"] = a
        args[name] = nc.dram_tensor(f"in_{name}", a.shape, mybir.dt.from_np(a.dtype), kind="ExternalInput").ap()
    out = nc.dram_tensor("out_0", (BATCH, T, D), F32, kind="ExternalOutput").ap()
    early_fusion(nc, args, out)
    r = run_bass_kernel_spmd(nc, [arrays], core_ids=[0])
    return r.results[0]["out_0"]
```

```python
from contextlib import ExitStack

import numpy as np

import concourse.bass as bass
from concourse import mybir

F32 = mybir.dt.float32
BF16 = mybir.dt.bfloat16
ALU = mybir.AluOpType
ACT = mybir.ActivationFunctionType
AX = mybir.AxisListType

BATCH, CH, IMG, PATCH, D, TXT = 32, 12, 224, 16, 192, 77
GRID = IMG // PATCH
IMG_TOK = GRID * GRID
T = IMG_TOK + TXT
NC_ = 3
TC = T // NC_
KC = 96
NK = D // KC
H, HD = 12, 16
HK = KC // HD
HP = 32
NG = 3
CUT = 137
W2C = T + CUT
SEL = 41
F0, F1, NEXP = 768, 384, 4
EPS = 1e-5
MAGIC = 12582912.0
OFF = 128.0
HALF_ROWS = PATCH // 2
XP = 112
XG = CH * GRID * 2 // XP
TAIL = IMG_TOK - 2 * TC
Q_PARTS = (0, 0, 1, 0, 2, 1)
K_PARTS = (0, 1, 0, 2, 0, 1)
SROWS = HD * len(Q_PARTS)
STACK_DMAS = 16 * 2 * len(Q_PARTS)

FIRST = ("pool.0 pool.1 pool.2 tok n0s n0n qk0.0 qk0.1 v0 vs " + " ".join(f"a0.{k}" for k in range(H + 1))
         + " pr0 n1s n1n n2n gate k1 v1 rta rtb pk0 gt pk1 s1.0 s1.1 t1.0 t1.1 c1 ct wo mg n3s n3n").split()
LAST = ("f0.0 f0.1 f0.2 fd n4s n4n qk1.0 qk1.1 v2 " + " ".join(f"mx.{k}" for k in range(18)) + " mt "
        "a2.0 a2.1 a2.2 a2.3 a2.4 ob.0 a2.5 a2.6 a2.7 a2.8 ob.1 a2.9 a2.10 a2.11 a2.12 ob.2 pr1 n5s n5n rtr "
        "ex.0 ex.1 ex.2 ex.3 dn.0 ex.4 ex.5 ex.6 dn.1 ex.7 ex.8 ex.9 dn.2 ex.10 ex.11 dn.3").split()
TURN = ("f0.0 f0.1 pool.0 f0.2 pool.1 pool.2 fd n4s tok n4n n0s qk1.0 qk1.1 n0n v2 qk0.0 qk0.1 v0 vs "
        "a0.0 a0.1 a0.2 a0.3 "
        + " ".join(f"a0.{k} mx.{2 * k - 8} mx.{2 * k - 7}" for k in range(4, 12)) +
        " mx.16 a0.12 mx.17 mt pr0 a2.0 n1s a2.1 a2.2 a2.3 n1n a2.4 a2.5 n2n a2.6 ob.0 k1 v1 gate a2.7 rta a2.8 "
        "ob.1 rtb a2.9 pk0 gt a2.10 pk1 a2.11 s1.0 s1.1 a2.12 ob.2 t1.0 pr1 t1.1 n5s c1 n5n ct ex.0 wo rtr mg ex.1 n3s "
        "ex.2 ex.3 dn.0 n3n ex.4 ex.5 ex.6 dn.1 ex.7 ex.8 ex.9 dn.2 ex.10 ex.11 dn.3").split()
assert sorted(TURN) == sorted(FIRST + LAST)


def areas(stage):
    name, _, k = stage.partition(".")
    k = int(k or 0)
    pair = "AB"[k % 2]
    if name == "a0":
        return ([pair] if k < H else []) + (["M"] if k % 4 == 1 else [])
    if name == "a2":
        return ([pair] if k < H else []) + (["N"] if k and k % 4 == 0 else [])
    if name in ("qk0", "qk1", "s1", "f0", "ex", "t1"):
        return [pair]
    return {"tok": ["M"], "n0n": ["M"], "v0": ["M"], "vs": ["M"], "pr0": ["M"], "n2n": ["M"], "gate": ["M"],
            "k1": ["A"], "v1": ["M"], "rta": ["A", "M"], "rtb": ["M"], "pk0": ["M"], "gt": ["B"], "pk1": ["M"],
            "c1": ["M"], "ct": ["M"], "wo": ["M"], "mg": ["M", "A"], "n3n": ["M"], "fd": ["M"],
            "n4n": ["N"], "mx": ["N"], "v2": ["N"], "mt": ["N"], "ob": ["N"], "pr1": ["N"], "n5n": ["N"], "rtr": ["N"],
            "dn": ["N"]}.get(name, [])


def count(stages, area):
    return sum(areas(x).count(area) for x in stages)


VECTOR_STEPS, POOL_STEPS, CONSTS = 44, 7, 27


def early_fusion(nc, ins, out):
    pooled_dram = nc.dram_tensor("pooled_dram", (BATCH, CH, GRID, 2, GRID), F32).ap()
    ctx = ExitStack()
    with ctx:
        def sb(name, shape, dt=F32):
            return ctx.enter_context(nc.sbuf_tensor(name, shape, dt))

        def within(base, at, shape, dt=F32):
            size = int(np.prod(shape[1:])) * mybir.dt.size(dt) // 4
            assert int(np.prod(shape[1:])) * mybir.dt.size(dt) % 4 == 0 and at + size <= base.shape[1], shape
            view = base[0:shape[0], at:at + size].bitcast(dt)
            names = "abcd"[:len(shape) - 1]
            return view.rearrange(f"p ({' '.join(names)}) -> p {' '.join(names)}",
                                  **dict(zip(names[1:], shape[2:]))) if len(shape) > 2 else view

        def sem(name):
            return ctx.enter_context(nc.semaphore(name))

        area = {x: ctx.enter_context(nc.psum_tensor(f"area_{x.lower()}", [128, 2, 512], F32)) for x in "ABMN"}
        A, B, M, N = (area[x] for x in "ABMN")

        def by_token(x, width=D):
            return area[x][0:TC, :, :].rearrange("p b (h n) -> p (b h) n", h=2)[:, 0:NC_, 0:width]

        def by_channel(x, n=T):
            return area[x][0:KC, :, 0:n]

        ident = sb("ident", [128, 128])
        ones = sb("ones", [128, 128])
        ones_b = sb("ones_b", [128, 1], BF16)
        minus_half = sb("minus_half", [128, NC_])
        ranks = sb("ranks", [128, SEL])
        earlier = sb("earlier", [TC, NC_, T], BF16)
        sum_row = sb("sum_row", [128, 128])
        head_mask = sb("head_mask", [KC, HK])
        scal = sb("scal", [128, 16])
        cw = sb("cw", [CH, D])
        w_qk0 = sb("w_qk0", [KC, NK, 2 * D])
        w_v0 = sb("w_v0", [KC, NK, D])
        w_p0 = sb("w_p0", [128, 3, NG, D], BF16)
        rows = sb("rows", [TC, 10, D])
        bproj0, g1, b1, bv0, bo, g2, b2, bf2, bv1, bproj1 = [rows[:, i, :] for i in range(10)]
        w_r = sb("w_r", [KC, NK])
        w_f = sb("w_f", [KC, NK, 5, D])
        W_Q, W_K, W_V, W_O, W_M = range(5)
        b_qk = sb("b_qk", [KC, 2, NK])
        w1 = sb("w1", [KC, NK, F0])
        bf1 = sb("bf1", [128, F0 // 128])
        w2 = sb("w2", [128, F0 // 128, D])
        w_qk1 = sb("w_qk1", [KC, NK, 2 * D])
        b_qk1 = sb("b_qk1", [KC, 2, NK])
        w_v1 = sb("w_v1", [KC, NK, D])
        w_p1 = sb("w_p1", [128, NG, D])
        w_gu = sb("w_gu", [KC, NK, NEXP, 2, F1])
        w_dn = sb("w_dn", [128, NEXP, F1 // 128, D])
        w_router = sb("w_router", [KC, NK, 3])
        b_router = sb("b_router", [TC, 3])

        img = sb("img", [XP, XG, HALF_ROWS * IMG])
        part = sb("part", [XP, XG, GRID])
        scratch0 = sb("scratch0", [128, F0 // 128 * T])
        halves = sb("halves", [CH, GRID, 2, GRID])
        pooled = within(scratch0, 0, [CH, IMG_TOK])
        h0 = sb("h0", [TC, NC_, D])
        hb0 = sb("hb0", [TC, NC_, D])
        y = sb("y", [TC, NC_, D])
        xn0 = sb("xn0", [TC, NC_, D])
        xT0 = sb("xT0", [KC, NK, T])
        t32 = within(scratch0, 0, [KC, NK, T])
        r16 = within(scratch0, 2 * T, [KC, NK, T], BF16)
        qk0 = within(scratch0, 3 * T, [KC, 2, NK, T], BF16)
        q0s = sb("q0s", [KC, H, T], BF16)
        k0s = sb("k0s", [KC, H, T], BF16)
        v0 = sb("v0", [KC, NC_, H, HP], BF16)
        vsum = sb("vsum", [128, NG])
        pa = [sb(f"pa{i}", [KC, 2, W2C], BF16) for i in range(2)]
        pq = [sb(f"pq{i}", [KC, 2, W2C], BF16) for i in range(2)]
        o32 = within(scratch0, 5 * T, [128, T])
        o0 = sb("o0", [128, NG, T], BF16)
        e_s = sb("e_s", [TC, NC_])
        score = sb("score", [TC, NC_])
        score_b = within(scratch0, 0, [TC, NC_, TC])
        score_row = within(scratch0, T, [TC, T])
        ties = within(scratch0, 2 * T, [TC, T])
        rank = sb("rank", [TC, NC_])
        unpicked = sb("unpicked", [TC, NC_])
        pick = sb("pick", [TC, NC_, SEL])
        mean_s = sb("mean_s", [KC, 4])
        mix_l = sb("mix_l", [2, T])
        mix_r = sb("mix_r", [2, D])
        selT = sb("selT", [KC, NK, SEL])
        qsel = sb("qsel", [KC, NK, SEL])
        qblk = within(scratch0, 4 * T, [KC, NK, HK, SEL])
        k1 = sb("k1", [KC, NK, T])
        v1 = sb("v1", [KC, NC_, H, HD + 1])
        smx = sb("smx", [3 * SEL, 4])
        p1 = within(scratch0, 0, [3 * SEL, 4, T])
        rec = sb("rec", [SEL, H])
        ctx1 = sb("ctx1", [SEL, D])
        ctxT = sb("ctxT", [KC, NK, SEL])
        ao = sb("ao", [SEL, D])
        pickT = sb("pickT", [SEL, T])
        hs = y
        hid0 = within(scratch0, 0, [128, F0 // 128, T])
        w_p0f, w_p0r = hid0[:, 0:3, 0:D], hid0[:, 3:6, 0:D]
        p1T = sb("p1T", [KC, NC_, 4 * 3 * SEL])
        stats0 = sb("stats0", [TC, NC_, 6])
        mv0 = sb("mv0", [TC, NC_, 2])
        rstd0 = sb("rstd0", [TC, NC_])
        h1 = sb("h1", [TC, NC_, D])
        hb1 = sb("hb1", [TC, NC_, D])
        xn1 = sb("xn1", [TC, NC_, D])
        xT1 = sb("xT1", [KC, NK, T])
        stats1 = sb("stats1", [TC, NC_, 6])
        mv1 = sb("mv1", [TC, NC_, 2])
        rstd1 = sb("rstd1", [TC, NC_])
        scratch1 = sb("scratch1", [128, 6 * T])
        parts = within(scratch1, 0, [KC, 2, 3, NK, T], BF16)
        hid1 = within(scratch1, 0, [128, 6, T])
        q1s = sb("q1s", [SROWS + 2, H, T], BF16)
        k1s = sb("k1s", [SROWS + 2, H, T], BF16)
        v2 = sb("v2", [KC, NC_, H, HP])
        mx = sb("mx", [TC, H * NC_])
        mrow = sb("mrow", [H, 2, T], BF16)
        pT_both = sb("pT_both", [KC, 2 * 2 * W2C])
        pT = [within(pT_both, i * 2 * W2C, [KC, 2, W2C]) for i in range(2)]
        x32 = within(pT_both, 0, [KC, 2, NK, T])
        oS = sb("oS", [128, T])
        rec2 = sb("rec2", [128, T])
        oN_sg = sb("oN_sg", [128, NG * T])
        oN = within(oN_sg, 0, [128, NG, T])
        sg = within(oN_sg, 0, [128, 2, T])
        lg = sb("lg", [TC, NC_, 3])
        er = sb("er", [TC, NC_, 3])
        pr = sb("pr", [TC, NC_, 3])
        cmp_ = sb("cmp", [TC, NC_, 6])
        cwt = sb("cwt", [TC, NC_, 3])
        tot = sb("tot", [TC, NC_])
        outb = sb("outb", [TC, NC_, D])

        full = {a: sem(f"{a.lower()}_full") for a in area}
        taken = {a: sem(f"{a.lower()}_taken") for a in area}
        vector_step, pool_step, waits_apart = sem("vector_step"), sem("pool_step"), sem("waits_apart")
        weights_in, zeroed, consts_ready, weights_ready = (sem(x) for x in (
            "weights_in", "zeroed", "consts_ready", "weights_ready"))
        image_in = [sem(f"image_in{i}") for i in range(XG)]
        text_in, halves_out, halves_in, out_done = sem("text_in"), sem("halves_out"), sem("halves_in"), sem("out_done")
        q0_in, k0_in, stack_in, mrow_in = sem("q0_in"), sem("k0_in"), sem("stack_in"), sem("mrow_in")
        part_ready = sem("part_ready")
        stats_ready, rstd_ready, xn_ready = ([sem(f"{x}{l}") for l in range(2)]
                                             for x in ("stats_ready", "rstd_ready", "xn_ready"))
        clamped, pv0_used, pv2_used, o0_ready, oN_ready, silu_ready = (sem(x) for x in (
            "clamped", "pv0_used", "pv2_used", "o0_ready", "oN_ready", "silu_ready"))
        smx_ready = sem("smx_ready")
        x32_ready, parts_ready = sem("x32_ready"), sem("parts_ready")
        (pooled_ready, hb0_ready, q0_ready, k0_ready, v0_ready, vsum_ready, spread_ready, row_ready, mean_ready,
         pick_ready, qblk_ready, hs_ready, res0_ready, h_ready, hb1_ready, mrow_ready, lg_ready, er_ready,
         out_ready) = (sem(x) for x in (
             "pooled_ready hb0_ready q0_ready k0_ready v0_ready vsum_ready spread_ready row_ready mean_ready "
             "pick_ready qblk_ready hs_ready res0_ready h_ready hb1_ready mrow_ready lg_ready er_ready "
             "out_ready").split())

        S_Q, S_K, S_V, S_ATT, S_AFT, BR, R_Q, R_K, R_V, C_P, C_O, N_BR, TMP, NOTE = range(14)

        def col(c, n=128):
            return scal[0:n, c:c + 1]

        loads = []

        def load(dst, src):
            loads.append((dst, src))

        for c, name in ((S_Q, "s_q"), (S_K, "s_k"), (S_V, "s_v"), (S_ATT, "s_attn"), (S_AFT, "s_after")):
            load(col(c), ins[f"L0_attn_{name}"].partition_broadcast(128))
        load(col(BR), ins["L0_ffn_br"].partition_broadcast(128))
        load(cw[:, :], ins["L0_tok_channel_weights"])

        def chan(a):
            return a.rearrange("(k p) n -> p k n", p=KC)

        load(w_qk0[:, :, :], chan(ins["L0_attn_Wqkv"][:, 0:2 * D]))
        load(w_qk1[:, :, :], chan(ins["L1_attn_qkv_w"][:, 0:2 * D]))
        load(w_v0[:, :, :], chan(ins["L0_attn_Wqkv"][:, 2 * D:3 * D]))
        load(w_v1[:, :, :], chan(ins["L1_attn_qkv_w"][:, 2 * D:3 * D]))
        for dst, name in ((w_p0f, "L0_attn_Wproj"), (w_p1, "L1_attn_proj_w")):
            wp = ins[name].rearrange("(g j d) n -> j d g n", g=NG, d=HD)
            for j in range(4):
                load(dst[HP * j:HP * j + HD, :, :], wp[j])
        for i, name in enumerate(("L0_attn_bproj", "L0_ffn_g1", "L0_ffn_b1", "L0_ffn_bv", "L0_ffn_bo", "L0_ffn_g2",
                                  "L0_ffn_b2", "L0_ffn_bf2", None, "L1_attn_proj_b")):
            src = ins[name] if name else ins["L1_attn_qkv_b"][2 * D:3 * D]
            load(rows[:, i, :], src.partition_broadcast(TC))
        load(w_r[:, :], ins["L0_ffn_Wr"].rearrange("(k p) -> p k", p=KC))
        for i, name in enumerate(("Wq", "Wk", "Wv", "Wo", "Wm")):
            load(w_f[:, :, i, :], chan(ins[f"L0_ffn_{name}"]))
        for i, name in enumerate(("bq", "bk")):
            load(b_qk[:, i, :], ins[f"L0_ffn_{name}"].rearrange("(k p) -> p k", p=KC))
        load(w1[:, :, :], chan(ins["L0_ffn_W1"]))
        load(bf1[:, :], ins["L0_ffn_bf1"].rearrange("(c p) -> p c", p=128))
        load(w2[:, :, :], ins["L0_ffn_W2"].rearrange("(c p) n -> p c n", p=128))
        for i in range(2):
            load(b_qk1[:, i, :], ins["L1_attn_qkv_b"][i * D:(i + 1) * D].rearrange("(k p) -> p k", p=KC))
        for i, name in enumerate(("gate", "up")):
            load(w_gu[:, :, 0, i, :], chan(ins[f"L1_ffn_shared_{name}"]))
            for e in range(3):
                load(w_gu[:, :, e + 1, i, :], chan(ins[f"L1_ffn_routed_{name}"][e]))
        for e in range(NEXP):
            load(w_dn[:, e, :, :], (ins["L1_ffn_routed_down"][e - 1] if e else ins["L1_ffn_shared_down"]).rearrange(
                "(c p) n -> p c n", p=128))
        load(w_router[:, :, :], chan(ins["L1_ffn_router_w"]))
        load(b_router[:, :], ins["L1_ffn_routing_bias"].partition_broadcast(TC))
        load(mix_r[1:2, :], ins["L0_ffn_bm"].rearrange("(a n) -> a n", a=1))

        img_dram = ins["x"].rearrange("b c (i r) w -> b (c i r w)", r=PATCH).rearrange(
            "b (g p n) -> b p g n", g=XG, p=XP)
        half_dram = pooled_dram.rearrange("b c i a j -> b (c i a j)").rearrange(
            "b (g p n) -> b p g n", g=XG, p=XP)

        class Turn:

            def __init__(self, eng, stages, it=None):
                self.eng, self.stages = eng, stages
                fixed = stages is not TURN or isinstance(it, int)
                self.it = 0 if stages is FIRST else BATCH - 1 if stages is LAST else it

                def value(x):
                    return x if fixed else eng.snap(x)

                self.n1 = self.it
                self.n0 = 0 if stages is FIRST else self.it + 1
                self.done0, self.done1 = value(self.n0 + 1), value(self.n1 + 1)
                self.base = {x: 0 if stages is FIRST else value(self.it * count(TURN, x) + count(FIRST, x))
                             for x in area}

            def at(self, x, stage, k=0):
                i = self.stages.index(stage)
                return self.base[x] + (count(self.stages[:i], x) + k)

            def begin(self, x, stage, k=0, lag=0):
                self.eng.wait_ge(taken[x], self.at(x, stage, k) + (1 - lag))

            def await_full(self, x, stage, k=0):
                self.eng.wait_ge(full[x], self.at(x, stage, k) + 1)

            def await_taken(self, x, stage, k=0):
                self.eng.wait_ge(taken[x], self.at(x, stage, k) + 2)

        def apart(eng):
            eng.sem_inc(waits_apart, 1)

        def go(eng, programs):
            programs(Turn(eng, FIRST))
            with eng.Fori(0, BATCH - 1) as it:
                programs(Turn(eng, TURN, it))
            programs(Turn(eng, LAST))

        block = ctx.enter_context(nc.Block())

        @block.sync
        def _(sp):
            sp.wait_ge(zeroed, 3)
            with nc.allow_non_contiguous_dma(reason="vectors onto partitions, once"):
                for dst, src in loads:
                    sp.dma_start(dst, src).then_inc(weights_in, 16)
            for p_ in range(XG):
                sp.dma_start(img[:, p_, :], img_dram[0, :, p_, :]).then_inc(image_in[p_], 16)
            sp.dma_start(h0[TAIL:TC, 2, :], ins["txt"][0]).then_inc(text_in, 16)

            def program(t, more):
                n0, n1 = t.n0, t.n1
                for stage in t.stages:
                    name, _, k = stage.partition(".")
                    k = int(k or 0)
                    if name == "pool":
                        sp.wait_ge(part_ready, n0 * XG + (k + 1))
                        if more:
                            sp.dma_start(img[:, k, :], img_dram[n0 + 1, :, k, :]).then_inc(image_in[k], 16)
                        if k == XG - 1:
                            sp.dma_start(half_dram[n0], part[:, :, :]).then_inc(halves_out, 16)
                            sp.wait_ge(halves_out, n0 * 16 + 16)
                            sp.dma_start(halves[:, :, :, :], pooled_dram[n0]).then_inc(halves_in, 16)
                    elif name == "qk0":
                        sp.wait_ge((q0_ready, k0_ready)[k], t.done0)
                        sp.dma_start((q0s, k0s)[k][0:HD, :, :], qk0[:, k, :, :]).then_inc((q0_in, k0_in)[k], 16)
                    elif name == "qk1":
                        sp.wait_ge(parts_ready, n1 * 2 + (k + 1))
                        for r, p_ in enumerate((Q_PARTS, K_PARTS)[k]):
                            sp.dma_start((q1s, k1s)[k][HD * r:HD * r + HD, :, :],
                                         parts[:, k, p_, :, :]).then_inc(stack_in, 16)
                    elif name == "mt":
                        sp.wait_ge(mrow_ready, t.done1)
                        for i in range(2):
                            sp.dma_start(q1s[SROWS + i:SROWS + i + 1, :, :], mrow[:, i, :]).then_inc(mrow_in, 16)
                    elif name == "fd" and t.stages is TURN:
                        sp.wait_ge(res0_ready, t.done1)
                        sp.dma_start(h0[TAIL:TC, 2, :], ins["txt"][n0]).then_inc(text_in, 16)
                    elif stage == "dn.3":
                        sp.wait_ge(out_ready, t.done1)
                        sp.dma_start(out[n1].rearrange("(c p) d -> p c d", p=TC), outb[:, :, :]).then_inc(out_done, 16)

            program(Turn(sp, FIRST), True)
            with sp.Fori(0, BATCH - 2) as it:
                program(Turn(sp, TURN, it), True)
            program(Turn(sp, TURN, BATCH - 2), False)
            program(Turn(sp, LAST), False)
            sp.wait_ge(out_done, 16 * BATCH + 1)

        @block.gpsimd
        def _(pool):
            g = nc.gpsimd
            for t_ in (w_p1[:, :, :], w_p0f, scal[:, :]):
                g.memset(t_, 0.0).then_inc(zeroed, 1)
            n = 0

            def const(ins_):
                nonlocal n
                n += 1
                ins_.then_inc(consts_ready, 1)
                pool.wait_ge(consts_ready, n)

            const(g.memset(mix_l[:, :], 1.0))
            const(g.memset(ident[:, :], 0.0))
            const(g.affine_select(out=ident[:, :], in_=ident[:, :], compare_op=ALU.not_equal, fill=1.0, base=0,
                                  pattern=[[-1, 128]], channel_multiplier=1))
            const(g.memset(ones[:, :], 1.0))
            const(g.memset(ones_b[:, :], 1.0))
            const(g.memset(minus_half[:, :], -0.5))
            const(g.iota(ranks[:, :], pattern=[[1, SEL]], base=0, channel_multiplier=0,
                         allow_small_or_imprecise_dtypes=True))
            const(g.memset(earlier[:, :, :], 1.0))
            const(g.affine_select(out=earlier[:, :, :], in_=earlier[:, :, :], compare_op=ALU.is_gt, fill=0.0, base=0,
                                  pattern=[[TC, NC_], [-1, T]], channel_multiplier=1))
            const(g.memset(head_mask[:, :], 1.0))
            const(g.affine_select(out=head_mask[:, :], in_=head_mask[:, :], compare_op=ALU.is_ge, fill=0.0, base=0,
                                  pattern=[[-HD, HK]], channel_multiplier=1))
            const(g.affine_select(out=head_mask[:, :], in_=head_mask[:, :], compare_op=ALU.is_ge, fill=0.0,
                                  base=HD - 1, pattern=[[HD, HK]], channel_multiplier=-1))
            const(g.memset(sum_row[:, :], 0.0))
            view = sum_row[:, :].rearrange("p (j n) -> p j n", n=HP)
            const(g.affine_select(out=view, in_=view, compare_op=ALU.not_equal, fill=1.0, base=-HD,
                                  pattern=[[-HP, 4], [0, HP]], channel_multiplier=1))
            for t_ in (v0[:, :, :, :], v1[:, :, :, :], v2[:, :, :, :], p1T[:, :, :], pq[0][:, :, :], pq[1][:, :, :],
                       pT[0][:, :, :], pT[1][:, :, :]):
                const(g.memset(t_, 0.0))
            const(g.memset(v1[0:TC, :, :, HD:HD + 1], 1.0))
            const(g.memset(v2[0:TC, :, :, HD:HD + 1], 1.0))
            for t_ in (q0s, k0s):
                const(g.memset(t_[:, :, :], 0.0))
            const(g.memset(k1s[SROWS:SROWS + 2, :, :], 1.0))
            assert n == CONSTS, n
            pool.wait_ge(weights_in, 16 * len(loads))
            steps = [0]

            def program(t):
                base_step = 0 if t.stages is FIRST else pool.snap(t.it * POOL_STEPS + first_steps[0]) \
                    if t.stages is TURN else first_steps[0] + (BATCH - 1) * POOL_STEPS
                steps[0] = 0

                def link(ins_):
                    steps[0] += 1
                    ins_.then_inc(pool_step, 1)
                    pool.wait_ge(pool_step, base_step + steps[0])

                def inv_std(layer, k):
                    norms = (4, 2)[layer]
                    mv, rstd = ((mv0, rstd0), (mv1, rstd1))[layer]
                    pool.wait_ge(stats_ready[layer], (t.n0, t.n1)[layer] * norms + (k + 1))
                    apart(pool)
                    link(g.tensor_scalar(rstd[:, :], mv[:, :, 1], EPS, None, ALU.add))
                    g.tensor_tensor(rstd[:, :], rstd[:, :], minus_half[0:TC, :], ALU.pow).then_inc(rstd_ready[layer], 1)

                def add_row(dst, src, row):
                    return g.tensor_tensor(dst[:, :, :], src[:, :, :],
                                           row.unsqueeze(1).to_broadcast([TC, NC_, D]), ALU.add)

                for stage in t.stages:
                    if stage == "n0s":
                        inv_std(0, 0)
                        add_row(hb0, h0, bproj0).then_inc(hb0_ready, 1)
                    elif stage == "n1s":
                        inv_std(0, 1)
                    elif stage == "n1n":
                        inv_std(0, 2)
                    elif stage == "n3s":
                        inv_std(0, 3)
                        link(g.tensor_tensor(hb0[:, :, :], h0[:, :, :], hs[:, :, :], ALU.add))
                        add_row(hb0, hb0, bf2).then_inc(res0_ready, 1)
                    elif stage == "n4s":
                        inv_std(1, 0)
                        add_row(hb1, h1, bproj1).then_inc(hb1_ready, 1)
                    elif stage == "n5s":
                        inv_std(1, 1)

            first_steps = [0]
            program(Turn(pool, FIRST))
            first_steps[0] = steps[0]
            with pool.Fori(0, BATCH - 1) as it:
                program(Turn(pool, TURN, it))
                assert steps[0] == POOL_STEPS, steps
            program(Turn(pool, LAST))

        @block.scalar
        def _(act):
            a = nc.scalar
            act.wait_ge(consts_ready, CONSTS)
            act.wait_ge(weights_ready, 1)

            def program(t):
                for stage in t.stages:
                    name, _, k = stage.partition(".")
                    k = int(k or 0)
                    x = "AB"[k % 2]
                    if name == "tok":
                        t.await_full("M", stage)
                        a.copy(h0[:, 0:2, :], by_token("M")[:, 0:2, :])
                        a.copy(h0[0:TAIL, 2, :], by_token("M")[0:TAIL, 2, :]).then_inc(taken["M"], 1)
                    elif name in ("n0n", "n2n", "n3n"):
                        t.await_full("M", stage)
                        a.copy(xT0[:, :, :], by_channel("M")).then_inc(taken["M"], 1)
                    elif name in ("n4n", "n5n"):
                        t.await_full("N", stage)
                        a.copy(xT1[:, :, :], by_channel("N")).then_inc(taken["N"], 1)
                    elif name == "a0" and k < H:
                        t.await_full(x, stage)
                        if t.stages is not FIRST or k >= 2:
                            act.wait_ge(clamped, t.n0 * H + (k - 1))
                        a.activation(pa[k % 2][0:TC, :, :], area[x][0:TC, :, 0:W2C], ACT.Copy, bias=OFF,
                                     scale=col(C_P, TC)).then_inc(taken[x], 1)
                    elif name == "gate":
                        t.await_full("M", stage)
                        a.activation(e_s[:, :], M[0:TC, 0, 0:NC_], ACT.Exp, bias=col(N_BR, TC),
                                     scale=-1.0).then_inc(taken["M"], 1)
                    elif name == "k1":
                        t.await_full("A", stage)
                        for kc in range(NK):
                            last = a.activation(k1[:, kc, :], A[0:KC, kc, 0:T], ACT.Identity, bias=b_qk[:, 1, kc:kc + 1])
                        last.then_inc(taken["A"], 1)
                    elif name == "rtb":
                        t.await_taken("A", "rta")
                        a.copy(mix_l[0:1, :], score_row[0:1, :]).then_inc(row_ready, 1)
                        t.await_full("M", stage)
                        a.copy(mix_r[0:1, :], M[0:1, 0, 0:D]).then_inc(taken["M"], 1)
                    elif name == "pk0":
                        t.await_full("M", stage)
                        a.copy(selT[:, :, :], by_channel("M", SEL)).then_inc(taken["M"], 1)
                    elif name == "gt":
                        t.await_full("B", stage)
                        a.copy(pickT[:, :], B[0:SEL, 0, 0:T]).then_inc(taken["B"], 1)
                    elif name == "s1":
                        act.wait_ge(smx_ready, t.n0 * 2 + (k + 1))
                        for i in range(2):
                            last = a.activation(p1[:, 2 * k + i, :], area[x][0:3 * SEL, i, 0:T], ACT.Exp,
                                                bias=smx[:, 2 * k + i:2 * k + i + 1], scale=HD ** -0.5)
                        last.then_inc(taken[x], 1)
                    elif name == "t1":
                        t.await_full(x, stage)
                        n_ = 2 - k
                        a.copy(p1T[0:TC, 2 * k:2 * k + n_, :], area[x][0:TC, 0:n_, 0:4 * 3 * SEL]).then_inc(taken[x], 1)
                    elif name == "ct":
                        t.await_full("M", stage)
                        a.copy(ctxT[:, :, :], by_channel("M", SEL)).then_inc(taken["M"], 1)
                    elif name == "f0":
                        t.await_full(x, stage)
                        for i in range(2):
                            last = a.activation(hid0[:, 2 * k + i, :], area[x][:, i, 0:T], ACT.Gelu,
                                                bias=bf1[:, 2 * k + i:2 * k + i + 1])
                        last.then_inc(taken[x], 1)
                    elif name == "qk1":
                        t.await_full(x, stage)
                        for kc in range(NK):
                            last = a.activation(x32[:, k, kc, :], area[x][0:KC, kc, 0:T], ACT.Identity,
                                                bias=b_qk1[:, k, kc:kc + 1])
                        last.then_inc(x32_ready, 1)
                        for kc in range(NK):
                            last = a.activation(parts[:, k, 0, kc, :], area[x][0:KC, kc, 0:T], ACT.Identity,
                                                bias=b_qk1[:, k, kc:kc + 1])
                        last.then_inc(taken[x], 1)
                    elif name == "a2":
                        if k < H:
                            t.await_full(x, stage)
                            act.wait_ge(pv2_used, t.n1 * H + (k + 1))
                            a.activation(pT[k % 2][0:TC, :, :], area[x][0:TC, :, 0:W2C], ACT.Exp,
                                         scale=HD ** -0.5).then_inc(taken[x], 1)
                        if k and k % 4 == 0:
                            if k > 4:
                                act.wait_ge(oN_ready, t.n1 * NG + (k // 4 - 1))
                            t.await_full("N", stage)
                            a.copy(oS[:, :], N[:, 0, 0:T]).then_inc(taken["N"], 1)
                    elif name == "rtr":
                        act.wait_ge(lg_ready, t.done1)
                        a.activation(er[:, :, :], lg[:, :, :], ACT.Exp, scale=-1.0).then_inc(er_ready, 1)
                    elif name == "ex":
                        t.await_full(x, stage)
                        a.activation(sg[:, k % 2, :], area[x][:, 0, 0:T], ACT.Silu).then_inc(silu_ready, 1)

            go(act, program)

        @block.vector
        def _(dve):
            v = nc.vector
            dve.wait_ge(weights_in, 16 * len(loads))
            dve.wait_ge(consts_ready, CONSTS)
            for x in area:
                dve.sem_inc(taken[x], 1)
            dve.sem_inc(out_done, 1)
            dve.sem_inc(pv2_used, 2)
            setup = [0]

            def once(ins_):
                setup[0] += 1
                ins_.then_inc(vector_step, 1)
                dve.wait_ge(vector_step, setup[0])

            for dst, src in ((R_Q, S_Q), (R_K, S_K), (R_V, S_V)):
                once(v.reciprocal(col(dst), col(src)))
            once(v.tensor_scalar(col(TMP), col(S_ATT), float(T), None, ALU.mult))
            once(v.reciprocal(col(TMP), col(TMP)))
            once(v.tensor_tensor(col(C_P), col(S_Q), col(S_K), ALU.mult))
            once(v.tensor_scalar(col(C_P), col(C_P), col(TMP), HD ** -0.5, ALU.mult, ALU.mult))
            once(v.reciprocal(col(TMP), col(S_AFT)))
            once(v.tensor_tensor(col(C_O), col(S_ATT), col(S_V), ALU.mult))
            once(v.tensor_tensor(col(C_O), col(C_O), col(TMP), ALU.mult))
            once(v.tensor_scalar(col(N_BR), col(BR), -1.0, None, ALU.mult))
            once(v.tensor_copy(w_p0[:, 0, :, :], w_p0f))
            once(v.tensor_tensor(w_p0r, w_p0f, w_p0[:, 0, :, :], ALU.subtract))
            once(v.tensor_copy(w_p0[:, 1, :, :], w_p0r))
            once(v.tensor_tensor(w_p0r, w_p0r, w_p0[:, 1, :, :], ALU.subtract))
            once(v.tensor_copy(w_p0[:, 2, :, :], w_p0r))
            v.tensor_copy(col(NOTE), col(TMP)).then_inc(weights_ready, 1)
            steps = [0]
            base_of = [setup[0]]

            def program(t):
                n0, n1 = t.n0, t.n1
                if t.stages is FIRST:
                    base_step = setup[0]
                elif t.stages is TURN:
                    base_step = dve.snap(t.it * VECTOR_STEPS + base_of[0])
                else:
                    base_step = base_of[0] + (BATCH - 1) * VECTOR_STEPS
                steps[0] = 0

                def link(ins_):
                    steps[0] += 1
                    ins_.then_inc(vector_step, 1)
                    dve.wait_ge(vector_step, base_step + steps[0])

                def stats(layer, src):
                    st, mv = ((stats0, mv0), (stats1, mv1))[layer]
                    for c in range(NC_):
                        last = v.bn_stats(st[:, c, :], src[:, c, :])
                    link(last)
                    apart(dve)
                    for c in range(NC_):
                        last = v.bn_aggr(mv[:, c, :], st[:, c, :])
                    last.then_inc(stats_ready[layer], 1)

                def normal(layer, k, src, dst, gain=None, shift=None):
                    mv, rstd = ((mv0, rstd0), (mv1, rstd1))[layer]
                    dve.wait_ge(rstd_ready[layer], (n0, n1)[layer] * (4, 2)[layer] + (k + 1))
                    for c in range(NC_):
                        last = v.tensor_scalar(dst[:, c, :], src[:, c, :], mv[:, c, 0:1], rstd[:, c:c + 1],
                                               ALU.subtract, ALU.mult)
                    if gain is not None:
                        link(last)
                        link(v.tensor_tensor(dst[:, :, :], dst[:, :, :], gain.unsqueeze(1).to_broadcast([TC, NC_, D]),
                                             ALU.mult))
                        last = v.tensor_tensor(dst[:, :, :], dst[:, :, :],
                                               shift.unsqueeze(1).to_broadcast([TC, NC_, D]), ALU.add)
                    return last

                for stage in t.stages:
                    name, _, k = stage.partition(".")
                    k = int(k or 0)
                    x = "AB"[k % 2]
                    if name == "pool":
                        dve.wait_ge(image_in[k], n0 * 16 + 16)
                        v.tensor_reduce(part[:, k, :], img[:, k, :].rearrange("p (r j w) -> p j r w", r=HALF_ROWS, j=GRID),
                                        AX.XY, ALU.add).then_inc(part_ready, 1)
                    elif name == "tok":
                        dve.wait_ge(halves_in, n0 * 16 + 16)
                        v.tensor_tensor(pooled[:, :].rearrange("p (i j) -> p i j", i=GRID), halves[:, :, 0, :],
                                        halves[:, :, 1, :], ALU.add).then_inc(pooled_ready, 1)
                    elif name == "n0s":
                        dve.wait_ge(text_in, n0 * 16 + 16)
                        t.await_taken("M", "tok")
                        stats(0, h0)
                    elif name == "n0n":
                        normal(0, 0, h0, xn0).then_inc(xn_ready[0], 1)
                    elif name == "qk0":
                        t.await_full(x, stage)
                        v.tensor_scalar(t32[:, :, :], by_channel(x), col((R_Q, R_K)[k], KC), MAGIC, ALU.mult,
                                        ALU.add).then_inc(taken[x], 1)
                        t.await_taken(x, stage)
                        link(v.tensor_scalar(r16[:, :, :], t32[:, :, :], MAGIC, -4.0, ALU.subtract, ALU.max))
                        v.tensor_scalar(qk0[:, k, :, :], r16[:, :, :], 3.0, None, ALU.min)\
                            .then_inc((q0_ready, k0_ready)[k], 1)
                    elif name == "v0":
                        t.await_full("M", stage)
                        v.tensor_scalar(y[:, :, :], by_token("M"), col(R_V, TC), MAGIC, ALU.mult, ALU.add)\
                            .then_inc(taken["M"], 1)
                        t.await_taken("M", stage)
                        link(v.tensor_scalar(y[:, :, :], y[:, :, :], MAGIC, -4.0, ALU.subtract, ALU.max))
                        v.tensor_scalar(v0[0:TC, :, :, 0:HD].rearrange("p c h d -> p (c h) d"),
                                        y[:, :, :].rearrange("p c (h d) -> p (c h) d", d=HD), 3.0, None,
                                        ALU.min).then_inc(v0_ready, 1)
                    elif name == "vs":
                        t.await_full("M", stage)
                        v.tensor_scalar(vsum[:, :], M[:, 0, 0:NG], OFF, None, ALU.mult).then_inc(taken["M"], 1)
                    elif name == "a0":
                        if k < H:
                            t.await_taken(x, stage)
                            if t.stages is not FIRST or k >= 2:
                                dve.wait_ge(pv0_used, n0 * H + (k - 1))
                            v.tensor_scalar(pq[k % 2][0:TC, :, :], pa[k % 2][0:TC, :, :], OFF, OFF + 7.0, ALU.max,
                                            ALU.min).then_inc(clamped, 1)
                        if k and k % 4 == 0:
                            gr = k // 4 - 1
                            use_ = f"a0.{k - 3}"
                            t.await_full("M", use_)
                            v.tensor_scalar(o32[:, :], M[:, gr % 2, 0:T], vsum[:, gr:gr + 1], col(C_O), ALU.subtract,
                                            ALU.mult).then_inc(taken["M"], 1)
                            t.await_taken("M", use_)
                            link(v.tensor_scalar(o32[:, :], o32[:, :], MAGIC, MAGIC, ALU.add, ALU.subtract))
                            v.tensor_scalar(o0[:, gr, :], o32[:, :], -4.0, 3.0, ALU.max, ALU.min).then_inc(o0_ready, 1)
                    elif name == "pr0":
                        t.await_full("M", stage)
                        dve.wait_ge(hb0_ready, t.done0)
                        v.scalar_tensor_tensor(h0[:, :, :], by_token("M"), col(S_AFT, TC), hb0[:, :, :], ALU.mult,
                                               ALU.add).then_inc(taken["M"], 1)
                    elif name == "n1s":
                        t.await_taken("M", "pr0")
                        stats(0, h0)
                    elif name == "n1n":
                        link(normal(0, 1, h0, y))
                        stats(0, y)
                    elif name == "n2n":
                        normal(0, 2, y, xn0, g1, b1).then_inc(xn_ready[0], 1)
                    elif name == "v1":
                        t.await_full("M", stage)
                        for c in range(NC_):
                            last = v.tensor_tensor(v1[0:TC, c, :, 0:HD],
                                                   by_token("M")[:, c, :].rearrange("p (h d) -> p h d", d=HD),
                                                   bv0.rearrange("p (h d) -> p h d", d=HD), ALU.add)
                        last.then_inc(taken["M"], 1)
                    elif name == "gate":
                        t.await_taken("M", stage)
                        link(v.tensor_scalar(score[:, :], e_s[:, :], 1.0, None, ALU.add))
                        link(v.reciprocal(score[:, :], score[:, :]))
                        v.tensor_copy(score_b[:, :, :], score[:, :].unsqueeze(2).to_broadcast([TC, NC_, TC]))\
                            .then_inc(spread_ready, 1)
                    elif name == "rta":
                        t.await_full("A", stage)
                        v.tensor_copy(score_row[:, :], A[0:TC, 0, 0:T]).then_inc(taken["A"], 1)
                        t.await_taken("A", stage)
                        t.await_full("M", stage)
                        v.tensor_copy(mean_s[:, 0:3], M[0:KC, 0, 0:3]).then_inc(taken["M"], 1)
                        t.await_taken("M", stage)
                        link(v.tensor_scalar(mean_s[:, 2:3], mean_s[:, 2:3], 1e-6, None, ALU.add))
                        link(v.reciprocal(mean_s[:, 3:4], mean_s[:, 2:3]))
                        v.tensor_scalar(mean_s[:, 0:2], mean_s[:, 0:2], mean_s[:, 3:4], None, ALU.mult)\
                            .then_inc(mean_ready, 1)
                        for c in range(NC_):
                            link(v.scalar_tensor_tensor(ties[:, :], score_row[:, :], score[:, c:c + 1],
                                                        earlier[:, c, :], ALU.is_equal, ALU.mult))
                            link(v.scalar_tensor_tensor(ties[:, :], score_row[:, :], score[:, c:c + 1], ties[:, :],
                                                        ALU.is_lt, ALU.add, accum_out=rank[:, c:c + 1]))
                        for c in range(NC_):
                            v.tensor_scalar(pick[:, c, :], ranks[0:TC, :], rank[:, c:c + 1], None, ALU.is_equal)
                        v.tensor_scalar(unpicked[:, :], rank[:, :], float(SEL), None, ALU.is_ge).then_inc(pick_ready, 1)
                    elif name == "pk1":
                        t.await_full("M", stage)
                        v.tensor_tensor(qsel[:, :, :], by_channel("M", SEL),
                                        b_qk[:, 0, :].unsqueeze(2).to_broadcast([KC, NK, SEL]), ALU.add)\
                            .then_inc(taken["M"], 1)
                        t.await_taken("M", stage)
                        for kc in range(NK):
                            last = v.tensor_tensor(qblk[:, kc, :, :],
                                                   qsel[:, kc, :].unsqueeze(1).to_broadcast([KC, HK, SEL]),
                                                   head_mask[:, :].unsqueeze(2).to_broadcast([KC, HK, SEL]), ALU.mult)
                        last.then_inc(qblk_ready, 1)
                    elif name == "s1":
                        t.await_full(x, stage)
                        at = slice(2 * k, 2 * k + 2)
                        link(v.tensor_reduce(smx[:, at], area[x][0:3 * SEL, :, 0:T], AX.X, ALU.max))
                        v.tensor_scalar(smx[:, at], smx[:, at], -HD ** -0.5, None, ALU.mult).then_inc(smx_ready, 1)
                    elif name == "c1":
                        t.await_full("M", stage)
                        heads_out = M[0:SEL, 0, 0:H * (HD + 1)].rearrange("p (h d) -> p h d", d=HD + 1)
                        link(v.reciprocal(rec[:, :], heads_out[:, :, HD]))
                        v.tensor_tensor(ctx1[:, :].rearrange("p (h d) -> p h d", d=HD), heads_out[:, :, 0:HD],
                                        rec[:, :].unsqueeze(2).to_broadcast([SEL, H, HD]), ALU.mult)\
                            .then_inc(taken["M"], 1)
                    elif name == "wo":
                        t.await_full("M", stage)
                        v.tensor_tensor(ao[:, :], M[0:SEL, 0, 0:D], bo[0:SEL, :], ALU.add).then_inc(taken["M"], 1)
                    elif name == "mg":
                        t.await_full("M", stage)
                        v.tensor_tensor(hs[:, :, :], by_token("M"), y[:, :, :], ALU.add).then_inc(taken["M"], 1)
                        t.await_taken("M", stage)
                        t.await_full("A", stage)
                        for c in range(NC_):
                            last = v.scalar_tensor_tensor(hs[:, c, :], by_token("A")[:, c, :], unpicked[:, c:c + 1],
                                                          hs[:, c, :], ALU.mult, ALU.add)
                        last.then_inc(taken["A"], 1)
                    elif name == "n3s":
                        t.await_taken("A", "mg")
                        stats(0, hs)
                    elif name == "n3n":
                        normal(0, 3, hs, xn0, g2, b2).then_inc(xn_ready[0], 1)
                    elif name == "fd":
                        t.await_full("M", stage)
                        dve.wait_ge(res0_ready, t.done1)
                        v.tensor_tensor(h1[:, :, :], by_token("M"), hb0[:, :, :], ALU.add).then_inc(taken["M"], 1)
                        t.await_taken("M", stage)
                    elif name == "n4s":
                        stats(1, h1)
                    elif name == "n4n":
                        normal(1, 0, h1, xn1).then_inc(xn_ready[1], 1)
                    elif name == "qk1":
                        dve.wait_ge(x32_ready, n1 * 2 + (k + 1))
                        t.await_taken(x, stage)
                        link(v.tensor_tensor(x32[:, k, :, :], x32[:, k, :, :], parts[:, k, 0, :, :], ALU.subtract))
                        link(v.tensor_copy(parts[:, k, 1, :, :], x32[:, k, :, :]))
                        v.tensor_tensor(parts[:, k, 2, :, :], x32[:, k, :, :], parts[:, k, 1, :, :], ALU.subtract)\
                            .then_inc(parts_ready, 1)
                    elif name == "v2":
                        t.await_full("N", stage)
                        for c in range(NC_):
                            last = v.tensor_tensor(v2[0:TC, c, :, 0:HD],
                                                   by_token("N")[:, c, :].rearrange("p (h d) -> p h d", d=HD),
                                                   bv1.rearrange("p (h d) -> p h d", d=HD), ALU.add)
                        last.then_inc(taken["N"], 1)
                    elif name == "mx":
                        t.await_full("N", stage)
                        v.tensor_reduce(mx[:, 2 * k:2 * k + 2], N[0:TC, :, 0:T], AX.X, ALU.max)\
                            .then_inc(taken["N"], 1)
                    elif name == "mt":
                        t.await_full("N", stage)
                        link(v.tensor_scalar(mrow[:, 0, :], N[0:H, 0, 0:T], -1.0, None, ALU.mult))
                        v.scalar_tensor_tensor(mrow[:, 1, :], N[0:H, 0, 0:T], -1.0, mrow[:, 0, :], ALU.mult,
                                               ALU.subtract).then_inc(taken["N"], 1)
                        t.await_taken("N", stage)
                        v.tensor_copy(col(NOTE), col(TMP)).then_inc(mrow_ready, 1)
                    elif name == "ob":
                        t.await_full("N", stage)
                        v.reciprocal(rec2[:, :], N[:, 1, 0:T]).then_inc(taken["N"], 1)
                        t.await_taken("N", stage)
                        v.tensor_tensor(oN[:, k, :], oS[:, :], rec2[:, :], ALU.mult).then_inc(oN_ready, 1)
                    elif name == "pr1":
                        t.await_full("N", stage)
                        dve.wait_ge(hb1_ready, t.done1)
                        v.tensor_tensor(h1[:, :, :], by_token("N"), hb1[:, :, :], ALU.add).then_inc(taken["N"], 1)
                    elif name == "n5s":
                        t.await_taken("N", "pr1")
                        stats(1, h1)
                    elif name == "n5n":
                        normal(1, 1, h1, xn1).then_inc(xn_ready[1], 1)
                    elif name == "rtr":
                        t.await_full("N", stage)
                        v.tensor_tensor(lg[:, :, :], N[0:TC, 0, 0:9].rearrange("p (c e) -> p c e", e=3),
                                        b_router[:, :].unsqueeze(1).to_broadcast([TC, NC_, 3]), ALU.add)\
                            .then_inc(taken["N"], 1)
                        t.await_taken("N", stage)
                        v.tensor_copy(col(NOTE), col(TMP)).then_inc(lg_ready, 1)
                    elif name == "ex":
                        if k == 1:
                            dve.wait_ge(er_ready, t.done1)
                            link(v.tensor_scalar(pr[:, :, :], er[:, :, :], 1.0, None, ALU.add))
                            link(v.reciprocal(pr[:, :, :], pr[:, :, :]))
                            pairs = ((0, 1, ALU.is_lt), (0, 2, ALU.is_lt), (1, 0, ALU.is_le), (1, 2, ALU.is_lt),
                                     (2, 0, ALU.is_le), (2, 1, ALU.is_le))
                            for i, (e, o, op) in enumerate(pairs):
                                last = v.tensor_tensor(cmp_[:, :, i], pr[:, :, e], pr[:, :, o], op)
                            link(last)
                            for e in range(3):
                                last = v.tensor_tensor(cwt[:, :, e], cmp_[:, :, 2 * e], cmp_[:, :, 2 * e + 1], ALU.mult)
                            link(last)
                            link(v.tensor_scalar(cwt[:, :, :], cwt[:, :, :], -1.0, 1.0, ALU.mult, ALU.add))
                            link(v.tensor_tensor(cwt[:, :, :], cwt[:, :, :], pr[:, :, :], ALU.mult))
                            link(v.tensor_reduce(tot[:, :], cwt[:, :, :], AX.X, ALU.add))
                            link(v.reciprocal(tot[:, :], tot[:, :]))
                            link(v.tensor_tensor(cwt[:, :, :], cwt[:, :, :],
                                                 tot[:, :].unsqueeze(2).to_broadcast([TC, NC_, 3]), ALU.mult))
                        if k >= 6 and k % 3 == 0:
                            t.await_full("N", f"dn.{k // 3 - 2}")
                        dve.wait_ge(silu_ready, n1 * (3 * NEXP) + (k + 1))
                        v.tensor_tensor(hid1[:, k % 6, :], sg[:, k % 2, :], area[x][:, 1, 0:T], ALU.mult)\
                            .then_inc(taken[x], 1)
                    elif name == "dn":
                        t.await_full("N", stage)
                        if k == 0:
                            dve.wait_ge(out_done, n1 * 16 + 1)
                            v.tensor_tensor(outb[:, :, :], by_token("N"), h1[:, :, :], ALU.add).then_inc(taken["N"], 1)
                        else:
                            for c in range(NC_):
                                last = v.scalar_tensor_tensor(outb[:, c, :], by_token("N")[:, c, :],
                                                              cwt[:, c, k - 1:k], outb[:, c, :], ALU.mult, ALU.add)
                            last.then_inc(taken["N"], 1)
                        t.await_taken("N", stage)
                        if k == NEXP - 1:
                            v.tensor_copy(col(NOTE), col(TMP)).then_inc(out_ready, 1)

            program(Turn(dve, FIRST))
            base_of[0] = setup[0] + steps[0]
            with dve.Fori(0, BATCH - 1) as it:
                program(Turn(dve, TURN, it))
                assert steps[0] == VECTOR_STEPS, steps
            program(Turn(dve, LAST))

        @block.tensor
        def _(pe):
            mm, turn_ = nc.tensor.matmul, nc.tensor.transpose
            pe.wait_ge(consts_ready, CONSTS)
            pe.wait_ge(weights_in, 16 * len(loads))
            pe.wait_ge(weights_ready, 1)

            def program(t):
                n0, n1 = t.n0, t.n1

                def flip(x, src, n=TC, chunks=NC_):
                    apart(pe)
                    for kc in range(NK):
                        for c in range(chunks):
                            last = turn_(area[x][0:KC, kc, c * n:(c + 1) * n],
                                         src[:, c, kc * KC:(kc + 1) * KC] if chunks > 1
                                         else src[:, kc * KC:(kc + 1) * KC], ident[0:n, 0:n])
                    last.then_inc(full[x], 1)

                def channels(x, w, rhs, n=T, rows_=KC):
                    for j in range(2):
                        for kc in range(NK):
                            last = mm(area[x][0:rows_, j, 0:n], w(j, kc), rhs[:, kc, 0:n], start=(kc == 0),
                                      stop=(kc == NK - 1))
                    last.then_inc(full[x], 1)

                def tokens(x, lhs, w):
                    for c in range(NC_):
                        for i, w_ in enumerate(w):
                            last = mm(by_token(x)[:, c, :], lhs(i, c), w_, start=(i == 0), stop=(i == len(w) - 1))
                    last.then_inc(full[x], 1)

                def chunk(xT):
                    return lambda i, c: xT[:, i, c * TC:(c + 1) * TC]

                def scores(x, lhs, rhs, hh):
                    for c, bank, at, q in ((0, 0, 0, slice(0, T)), (1, 1, 0, slice(0, T)), (2, 0, T, slice(0, CUT)),
                                           (2, 1, T, slice(T - CUT, T))):
                        last = mm(area[x][0:TC, bank, at:at + q.stop - q.start], lhs[:, hh, c * TC:(c + 1) * TC],
                                  rhs[:, hh, q], start=True, stop=True)
                    last.then_inc(full[x], 1)

                def weigh(x, bank, j, v_, p_):
                    o_ = area[x][HP * j:HP * j + HP, bank, :]
                    mm(o_[:, 0:T], v_[:, 0, :], p_[:, 0, 0:T], start=True, stop=False)
                    mm(o_[:, 0:T], v_[:, 1, :], p_[:, 1, 0:T], start=False, stop=False)
                    mm(o_[:, 0:CUT], v_[:, 2, :], p_[:, 0, T:W2C], start=False, stop=False)
                    return mm(o_[:, CUT:T], v_[:, 2, :], p_[:, 1, 2 * CUT:W2C], start=False, stop=True)

                for stage in t.stages:
                    name, _, k = stage.partition(".")
                    k = int(k or 0)
                    x = "AB"[k % 2]
                    if name == "tok":
                        pe.wait_ge(pooled_ready, t.done0)
                        t.begin("M", stage)
                        for c in range(NC_):
                            n_ = TC if c < 2 else TAIL
                            last = mm(by_token("M")[0:n_, c, :], pooled[:, c * TC:c * TC + n_], cw[:, :], start=True,
                                      stop=True)
                        last.then_inc(full["M"], 1)
                    elif name in ("n0n", "n2n", "n3n"):
                        pe.wait_ge(xn_ready[0], n0 * 3 + ("n0n", "n2n", "n3n").index(name) + 1)
                        t.begin("M", stage)
                        flip("M", xn0)
                    elif name == "qk0":
                        t.await_taken("M", "n0n")
                        t.begin(x, stage)
                        channels(x, lambda j, kc: w_qk0[:, kc, k * D + j * KC:k * D + (j + 1) * KC], xT0)
                    elif name == "v0":
                        t.begin("M", stage)
                        tokens("M", chunk(xT0), [w_v0[:, i, :] for i in range(NK)])
                    elif name == "vs":
                        pe.wait_ge(v0_ready, t.done0)
                        t.begin("M", stage)
                        for g_ in range(NG):
                            for c in range(NC_):
                                last = mm(M[:, 0, g_:g_ + 1],
                                          v0[:, c, 4 * g_:4 * g_ + 4, :].rearrange("p h d -> p (h d)"),
                                          ones_b[0:KC, :], start=(c == 0), stop=(c == NC_ - 1))
                        last.then_inc(full["M"], 1)
                    elif name == "a0":
                        if k == 0:
                            pe.wait_ge(q0_in, n0 * 16 + 16)
                            pe.wait_ge(k0_in, n0 * 16 + 16)
                        if k < H:
                            t.begin(x, stage)
                            scores(x, k0s, q0s, k)
                        if k:
                            p = k - 1
                            if p % 4 == 0:
                                t.begin("M", stage, lag=(1 if p else 0))
                            pe.wait_ge(clamped, n0 * H + (p + 1))
                            weigh("M", p // 4 % 2, p % 4, v0[:, :, p, :], pq[p % 2]).then_inc(pv0_used, 1)
                            if p % 4 == 3:
                                mm(M[0:1, p // 4 % 2, T:T + 1], ones_b[:, :], ones_b[:, :], start=True,
                                   stop=True).then_inc(full["M"], 1)
                    elif name == "pr0":
                        pe.wait_ge(o0_ready, n0 * NG + NG)
                        t.begin("M", stage)
                        tokens("M", lambda i, c: o0[:, i % NG, c * TC:(c + 1) * TC],
                               [w_p0[:, i // NG, i % NG, :] for i in range(3 * NG)])
                    elif name == "gate":
                        t.await_taken("M", "n2n")
                        t.begin("M", stage)
                        for c in range(NC_):
                            for kc in range(NK):
                                last = mm(M[0:TC, 0, c:c + 1], xT0[:, kc, c * TC:(c + 1) * TC], w_r[:, kc:kc + 1],
                                          start=(kc == 0), stop=(kc == NK - 1))
                        last.then_inc(full["M"], 1)
                    elif name == "k1":
                        t.await_taken("M", "n2n")
                        t.begin("A", stage)
                        channels("A", lambda j, kc: w_f[:, kc, W_K, j * KC:(j + 1) * KC], xT0)
                    elif name == "v1":
                        t.begin("M", stage)
                        tokens("M", chunk(xT0), [w_f[:, i, W_V, :] for i in range(NK)])
                    elif name == "rta":
                        pe.wait_ge(spread_ready, t.done0)
                        t.begin("A", stage)
                        apart(pe)
                        for c in range(NC_):
                            last = turn_(A[0:TC, 0, c * TC:(c + 1) * TC], score_b[:, c, :], ident[0:TC, 0:TC])
                        last.then_inc(full["A"], 1)
                        t.begin("M", stage)
                        for j in range(NK + 1):
                            for c in range(NC_):
                                lhs = xn0[:, c, j * KC:(j + 1) * KC] if j < NK else ones[0:TC, 0:KC]
                                last = mm(M[0:KC, 0, j:j + 1], lhs, score[:, c:c + 1], start=(c == 0),
                                          stop=(c == NC_ - 1))
                        last.then_inc(full["M"], 1)
                    elif name == "rtb":
                        pe.wait_ge(mean_ready, t.done0)
                        t.begin("M", stage)
                        for kc in range(NK):
                            last = mm(M[0:1, 0, 0:D], mean_s[:, kc:kc + 1], w_f[:, kc, W_M, :], start=(kc == 0),
                                      stop=(kc == NK - 1))
                        last.then_inc(full["M"], 1)
                    elif name == "pk0":
                        pe.wait_ge(pick_ready, t.done0)
                        t.begin("M", stage)
                        for kc in range(NK):
                            for c in range(NC_):
                                last = mm(M[0:KC, kc, 0:SEL], xn0[:, c, kc * KC:(kc + 1) * KC], pick[:, c, :],
                                          start=(c == 0), stop=(c == NC_ - 1))
                        last.then_inc(full["M"], 1)
                    elif name == "gt":
                        t.begin("B", stage)
                        apart(pe)
                        for c in range(NC_):
                            last = turn_(B[0:SEL, 0, c * TC:(c + 1) * TC], pick[:, c, :], ident[0:TC, 0:TC])
                        last.then_inc(full["B"], 1)
                    elif name == "pk1":
                        t.await_taken("M", "pk0")
                        t.begin("M", stage)
                        channels("M", lambda j, kc: w_f[:, kc, W_Q, j * KC:(j + 1) * KC], selT, SEL)
                    elif name == "s1":
                        pe.wait_ge(qblk_ready, t.done0)
                        t.begin(x, stage)
                        for i in range(2):
                            last = mm(area[x][0:3 * SEL, i, 0:T], qblk[:, k, 3 * i:3 * i + 3, :].rearrange("p h q -> p (h q)"),
                                      k1[:, k, :], start=True, stop=True)
                        last.then_inc(full[x], 1)
                    elif name == "t1":
                        t.await_taken("A", "s1.0")
                        t.await_taken("B", "s1.1")
                        t.begin(x, stage)
                        apart(pe)
                        for i in range(2 - k):
                            for g_ in range(4):
                                c = 2 * k + i
                                last = turn_(area[x][0:TC, i, g_ * 3 * SEL:(g_ + 1) * 3 * SEL],
                                             p1[:, g_, c * TC:(c + 1) * TC], ident[0:3 * SEL, 0:3 * SEL])
                        last.then_inc(full[x], 1)
                    elif name == "c1":
                        t.await_taken("A", "t1.0")
                        t.await_taken("B", "t1.1")
                        t.begin("M", stage)
                        for hh in range(H):
                            for c in range(NC_):
                                last = mm(M[0:SEL, 0, hh * (HD + 1):(hh + 1) * (HD + 1)],
                                          p1T[:, c, hh * SEL:(hh + 1) * SEL], v1[:, c, hh, :], start=(c == 0),
                                          stop=(c == NC_ - 1))
                        last.then_inc(full["M"], 1)
                    elif name == "ct":
                        t.begin("M", stage)
                        flip("M", ctx1, SEL, 1)
                    elif name == "wo":
                        t.await_taken("M", "ct")
                        t.begin("M", stage)
                        for kc in range(NK):
                            last = mm(M[0:SEL, 0, 0:D], ctxT[:, kc, :], w_f[:, kc, W_O, :], start=(kc == 0),
                                      stop=(kc == NK - 1))
                        last.then_inc(full["M"], 1)
                    elif name == "mg":
                        t.await_taken("B", "gt")
                        t.begin("M", stage)
                        tokens("M", lambda i, c: pickT[:, c * TC:(c + 1) * TC], [ao[:, :]])
                        pe.wait_ge(row_ready, t.done0)
                        t.begin("A", stage)
                        tokens("A", lambda i, c: (xT0[:, i, c * TC:(c + 1) * TC] if i < NK
                                                  else mix_l[:, c * TC:(c + 1) * TC]),
                               [w_f[:, 0, W_M, :], w_f[:, 1, W_M, :], mix_r[:, :]])
                    elif name == "f0":
                        if k == 0:
                            t.begin("M", stage)
                        t.begin(x, stage)
                        channels(x, lambda j, kc: w1[:, kc, (2 * k + j) * 128:(2 * k + j + 1) * 128], xT0, rows_=128)
                    elif name == "fd":
                        t.await_taken("B", "f0.1")
                        t.await_taken("A", "f0.2")
                        t.begin("M", stage)
                        tokens("M", chunk(hid0), [w2[:, i, :] for i in range(F0 // 128)])
                    elif name in ("n4n", "n5n"):
                        pe.wait_ge(xn_ready[1], n1 * 2 + ("n4n", "n5n").index(name) + 1)
                        t.begin("N", stage)
                        flip("N", xn1)
                    elif name == "qk1":
                        t.await_taken("N", "n4n")
                        t.begin(x, stage)
                        channels(x, lambda j, kc: w_qk1[:, kc, k * D + j * KC:k * D + (j + 1) * KC], xT1)
                    elif name == "v2":
                        t.begin("N", stage)
                        tokens("N", chunk(xT1), [w_v1[:, i, :] for i in range(NK)])
                    elif name == "mx":
                        if k == 0:
                            pe.wait_ge(stack_in, n1 * STACK_DMAS + STACK_DMAS)
                        t.begin("N", stage)
                        for i in range(2):
                            hh, c = divmod(2 * k + i, NC_)
                            last = mm(N[0:TC, i, 0:T], q1s[0:SROWS, hh, c * TC:(c + 1) * TC],
                                      k1s[0:SROWS, hh, :], start=True, stop=True)
                        last.then_inc(full["N"], 1)
                    elif name == "mt":
                        t.begin("N", stage)
                        apart(pe)
                        for c in range(NC_):
                            last = turn_(N[0:H, 0, c * TC:(c + 1) * TC], mx[:, c:H * NC_:NC_], ident[0:TC, 0:TC])
                        last.then_inc(full["N"], 1)
                    elif name == "a2":
                        if k == 0:
                            pe.wait_ge(mrow_in, n1 * 32 + 32)
                        if k < H:
                            t.begin(x, stage)
                            scores(x, k1s, q1s, k)
                        if k:
                            p = k - 1
                            if p == 0:
                                t.begin("N", stage)
                            elif p % 4 == 0:
                                t.await_taken("N", f"a2.{p}")
                            t.await_taken("AB"[p % 2], f"a2.{p}")
                            weigh("N", 0, p % 4, v2[:, :, p, :], pT[p % 2]).then_inc(pv2_used, 1)
                            if p % 4 == 3:
                                mm(N[0:1, 0, T:T + 1], ones_b[:, :], ones_b[:, :], start=True,
                                   stop=True).then_inc(full["N"], 1)
                    elif name == "ob":
                        t.await_taken("N", f"a2.{4 * k + 4}")
                        if k:
                            t.await_taken("N", f"ob.{k - 1}")
                        mm(N[:, 1, 0:T], sum_row[:, :], oS[:, :], start=True, stop=True).then_inc(full["N"], 1)
                    elif name == "pr1":
                        pe.wait_ge(oN_ready, n1 * NG + NG)
                        t.begin("N", stage)
                        tokens("N", chunk(oN), [w_p1[:, i, :] for i in range(NG)])
                    elif name == "rtr":
                        t.await_taken("N", "n5n")
                        t.begin("N", stage)
                        for c in range(NC_):
                            for kc in range(NK):
                                last = mm(N[0:TC, 0, 3 * c:3 * c + 3], xT1[:, kc, c * TC:(c + 1) * TC],
                                          w_router[:, kc, :], start=(kc == 0), stop=(kc == NK - 1))
                        last.then_inc(full["N"], 1)
                    elif name == "ex":
                        e, j_ = divmod(k, 3)
                        if k == 0:
                            t.await_taken("N", "n5n")
                        t.begin(x, stage)
                        channels(x, lambda i, kc: w_gu[:, kc, e, i, j_ * 128:(j_ + 1) * 128], xT1, rows_=128)
                    elif name == "dn":
                        last_ = f"ex.{3 * k + 2}"
                        t.await_taken("AB"[(3 * k + 2) % 2], last_)
                        t.await_taken("AB"[(3 * k + 1) % 2], f"ex.{3 * k + 1}")
                        t.begin("N", stage)
                        tokens("N", lambda i, c: hid1[:, 3 * (k % 2) + i, c * TC:(c + 1) * TC],
                               [w_dn[:, k, i, :] for i in range(3)])

            go(pe, program)


_TRANSPOSED = ("L0_attn_Wqkv", "L0_attn_Wproj", "L1_attn_qkv_w", "L1_attn_proj_w")
_BY_CHANNEL = ("L0_attn_Wqkv", "L1_attn_qkv_w", "L1_attn_qkv_b")
_UNREAD = ("L1_attn_qkv_B", "L1_attn_proj_B")


def kernel(**inputs):
    import concourse.bacc as bacc
    from concourse.bass_utils import run_bass_kernel_spmd

    nc = bacc.Bacc("TRN2", target_bir_lowering=False, num_devices=1)
    arrays, args = {}, {}
    for name, value in inputs.items():
        if name in _UNREAD:
            continue
        a = np.asarray(value)
        if name in _TRANSPOSED:
            a = a.T
        if name in _BY_CHANNEL:
            qk = a[..., :2 * D].reshape(a.shape[:-1] + (2, HK, NK, HD))
            qk = np.moveaxis(qk, -3, -1)
            a = np.concatenate([qk.reshape(a.shape[:-1] + (2 * D,)), a[..., 2 * D:]], axis=-1)
        a = np.ascontiguousarray(a.reshape(a.shape or (1,)))
        arrays[f"in_{name}"] = a
        args[name] = nc.dram_tensor(f"in_{name}", a.shape, mybir.dt.from_np(a.dtype), kind="ExternalInput").ap()
    out = nc.dram_tensor("out_0", (BATCH, T, D), F32, kind="ExternalOutput").ap()
    early_fusion(nc, args, out)
    r = run_bass_kernel_spmd(nc, [arrays], core_ids=[0])
    return r.results[0]["out_0"]
```

```python
from contextlib import ExitStack

import numpy as np

import concourse.bass as bass
from concourse import mybir

F32 = mybir.dt.float32
BF16 = mybir.dt.bfloat16
ALU = mybir.AluOpType
ACT = mybir.ActivationFunctionType
AX = mybir.AxisListType

BATCH, CH, IMG, PATCH, D, TXT = 32, 12, 224, 16, 192, 77
GRID = IMG // PATCH
IMG_TOK = GRID * GRID
T = IMG_TOK + TXT
NC_ = 3
TC = T // NC_
KC = 96
NK = D // KC
H, HD = 12, 16
HK = KC // HD
HP = 32
NG = 3
CUT = 137
W2C = T + CUT
MIX = 64
SEL = 41
F0, F1, NEXP = 768, 384, 4
EPS = 1e-5
MAGIC = 12582912.0
OFF = 128.0
HALF_ROWS = PATCH // 2
XP = 112
XG = CH * GRID * 2 // XP
TAIL = IMG_TOK - 2 * TC
Q_PARTS = (0, 0, 1, 0, 2, 1)
K_PARTS = (0, 1, 0, 2, 0, 1)
SROWS = HD * len(Q_PARTS)
STACK_DMAS = 16 * 2 * len(Q_PARTS)

def attend(k):
    m = 4 * (k - 1)
    return (f"a0.{k} " + (f"pv.{k - 2} " if k > 1 else "") + f"mx.{m} mx.{m + 1} cl.{k - 1} mx.{m + 2} mx.{m + 3} "
            + (f"og.{(k - 5) // 4} " if k in (5, 9) else ""))


TURN = (f"""
dy.0 cw pd fd tok ey.3 n4s ez.3 ey.4 n4n n4f n0s ez.4 n0n ey.5 ez.5 qk1.0 n0f qk1.1 qk0.0 qk0.1 v0 v2 ey.6 vs ez.6
dy.1 a0.0 {"".join(attend(k) for k in range(1, 10))} a0.10 pv.8 cl.9 mt a0.11 pv.9 ey.7 cl.10 pv.10 cl.11 pv.11 ez.7
ey.8 og.2 ez.8 pr0 n1s dy.2 n1n a2.0 a2.1 n2n pw.0 a2.2 pw.1 a2.3 pw.2 a2.4 pw.3 os.0 pool.0 n2f gate rta k1 a2.5 pw.4
a2.6 pk0 gt pk1 rtb s1.0 s1.1 v1 pw.5 ob.0 t1.0 t1.1 pool.1 a2.7 pw.6 c1 a2.8 ct pw.7 os.1 wo pool.2 a2.9 mg n3s pw.8
a2.10 a2.11 pw.9 pw.10 n3n ob.1 pw.11 n3f os.2 ey.9 ey.10 ez.9 ob.2 ey.11 ez.10 f0.0 ez.11 f0.1 pr1 f0.2 n5s n5n dy.3
n5f rtr ex.0 ex.1 em.0 ex.2 em.1 em.2
""").split()
LAYER0 = set("pool tok n0s n0n n0f qk0 v0 vs a0 cl pv og pr0 n1s n1n n2n n2f gate k1 v1 rta rtb pk0 gt pk1 s1 t1 c1 ct "
             "wo mg n3s n3n n3f pd f0".split())
OTHERS = {"ey", "ez", "dy", "cw"}


def part_of(wanted):
    return [x for x in TURN if wanted(x.split(".")[0])]


FIRST = ["first.0", "first.1", "first.2"] + part_of(lambda x: x in LAYER0)
SECOND = part_of(lambda x: x not in OTHERS)
LAST = part_of(lambda x: x not in LAYER0)
REST = part_of(lambda x: x in OTHERS)


def pair_of(name, k):
    return "AB"[(k + (name in ("a0", "cl"))) % 2]


def areas(stage):
    name, _, k = stage.partition(".")
    if name in ("a0", "a2", "qk0", "qk1", "s1", "f0", "ex", "ey", "t1"):
        return [pair_of(name, int(k))]
    if name in ("pv", "pw"):
        return [] if int(k) % 4 != 3 else ["M" if name == "pv" else "N"]
    return {"tok": ["M"], "n0f": ["M"], "v0": ["M"], "vs": ["M"], "pr0": ["M"], "n2f": ["M"], "gate": ["M"],
            "k1": ["A"], "v1": ["M"], "rta": ["A", "M"], "rtb": ["M"], "pk0": ["M"], "gt": ["B"], "pk1": ["M"],
            "c1": ["M"], "ct": ["M"], "wo": ["M"], "mg": ["M", "A"], "n3f": ["M"], "fd": ["M"],
            "n4f": ["N"], "mx": ["N"], "v2": ["N"], "mt": ["N"], "ob": ["N"], "pr1": ["N"], "n5f": ["N"], "rtr": ["N"],
            "dy": ["N"]}.get(name, [])


def count(stages, area):
    return sum(areas(x).count(area) for x in stages)


VECTOR_STEPS, POOL_STEPS, CONSTS = 45, 7, 27


def early_fusion(nc, ins, out):
    pooled_dram = nc.dram_tensor("pooled_dram", (BATCH, CH, GRID, 2, GRID), F32).ap()
    ctx = ExitStack()
    with ctx:
        def sb(name, shape, dt=F32):
            return ctx.enter_context(nc.sbuf_tensor(name, shape, dt))

        def within(base, at, shape, dt=F32):
            size = int(np.prod(shape[1:])) * mybir.dt.size(dt) // 4
            assert int(np.prod(shape[1:])) * mybir.dt.size(dt) % 4 == 0 and at + size <= base.shape[1], shape
            view = base[0:shape[0], at:at + size].bitcast(dt)
            names = "abcd"[:len(shape) - 1]
            return view.rearrange(f"p ({' '.join(names)}) -> p {' '.join(names)}",
                                  **dict(zip(names[1:], shape[2:]))) if len(shape) > 2 else view

        def sem(name):
            return ctx.enter_context(nc.semaphore(name))

        area = {x: ctx.enter_context(nc.psum_tensor(f"area_{x.lower()}", [128, 2, 512], F32)) for x in "ABMN"}
        A, B, M, N = (area[x] for x in "ABMN")

        def by_token(x, width=D):
            return area[x][0:TC, :, :].rearrange("p b (h n) -> p (b h) n", h=2)[:, 0:NC_, 0:width]

        def by_channel(x, n=T):
            return area[x][0:KC, :, 0:n]

        ident = sb("ident", [128, 128])
        ones = sb("ones", [128, 128])
        ones_b = sb("ones_b", [128, 1], BF16)
        minus_half = sb("minus_half", [128, NC_])
        ranks = sb("ranks", [128, SEL])
        earlier = sb("earlier", [TC, NC_, T], BF16)
        sum_row = sb("sum_row", [128, 128])
        head_mask = sb("head_mask", [KC, HK])
        scal = sb("scal", [128, 16])
        cw = sb("cw", [CH, D])
        w_qk0 = sb("w_qk0", [KC, NK, 2 * D])
        w_v0 = sb("w_v0", [KC, NK, D])
        w_p0 = sb("w_p0", [128, 3, NG, D], BF16)
        rows = sb("rows", [TC, 10, D])
        bproj0, g1, b1, bv0, bo, g2, b2, bf2, bv1, bproj1 = [rows[:, i, :] for i in range(10)]
        w_r = sb("w_r", [KC, NK])
        w_f = sb("w_f", [KC, NK, 5, D])
        W_Q, W_K, W_V, W_O, W_M = range(5)
        b_qk = sb("b_qk", [KC, 2, NK])
        w1 = sb("w1", [KC, NK, F0])
        bf1 = sb("bf1", [128, F0 // 128])
        w2 = sb("w2", [128, F0 // 128, D])
        w_qk1 = sb("w_qk1", [KC, NK, 2 * D])
        b_qk1 = sb("b_qk1", [KC, 2, NK])
        w_v1 = sb("w_v1", [KC, NK, D])
        w_p1 = sb("w_p1", [128, NG, D])
        w_gu = sb("w_gu", [KC, NK, NEXP, 2, F1])
        w_dn = sb("w_dn", [128, NEXP, F1 // 128, D])
        w_router = sb("w_router", [KC, NK, 3])
        b_router = sb("b_router", [TC, 3])

        img = sb("img", [XP, XG, HALF_ROWS * IMG])
        part = sb("part", [XP, XG, GRID])
        scratch0 = sb("scratch0", [128, F0 // 128 * T])
        halves = sb("halves", [CH, GRID, 2, GRID])
        pooled = sb("pooled", [CH, IMG_TOK])
        h0 = sb("h0", [TC, NC_, D])
        hb0 = sb("hb0", [TC, NC_, D])
        y = sb("y", [TC, NC_, D])
        xn0 = sb("xn0", [TC, NC_, D])
        xT0 = sb("xT0", [KC, NK, T])
        t32 = within(scratch0, 0, [KC, NK, T])
        r16 = within(scratch0, 2 * T, [KC, NK, T], BF16)
        qk0 = within(scratch0, 3 * T, [KC, 2, NK, T], BF16)
        q0s = sb("q0s", [KC, H, T], BF16)
        k0s = sb("k0s", [KC, H, T], BF16)
        v0 = sb("v0", [KC, NC_, H, HP], BF16)
        vsum = sb("vsum", [128, NG])
        pa = [sb(f"pa{i}", [KC, 2, W2C], BF16) for i in range(2)]
        pq = [sb(f"pq{i}", [KC, 2, W2C], BF16) for i in range(2)]
        o32 = within(scratch0, 5 * T, [128, T])
        o0_pick = sb("o0_pick", [128, NG * T // 2 + 1])
        o0 = o0_pick[:, :].bitcast(BF16)[:, 0:NG * T].rearrange("p (g n) -> p g n", g=NG)
        e_s = sb("e_s", [TC, NC_])
        score = sb("score", [TC, NC_])
        score_b = within(scratch0, 0, [TC, NC_, TC])
        score_row = within(scratch0, T, [TC, T])
        ties = within(scratch0, 2 * T, [TC, T])
        rank = sb("rank", [TC, NC_])
        unpicked = sb("unpicked", [TC, NC_])
        pick = sb("pick", [TC, NC_, KC])
        mean_s = sb("mean_s", [KC, 4])
        selT = sb("selT", [KC, NK, SEL])
        qsel = sb("qsel", [KC, NK, SEL])
        qblk = within(scratch0, 4 * T, [KC, NK, HK, SEL])
        k1 = sb("k1", [KC, NK, T])
        v1 = sb("v1", [KC, NC_, H, HD + 1])
        smx = sb("smx", [3 * SEL, 4])
        p1 = within(scratch0, 0, [3 * SEL, 4, T])
        rec = sb("rec", [SEL, H])
        ctx1 = within(scratch0, 4 * T, [SEL, D])
        ctxT = sb("ctxT", [KC, NK, SEL])
        ao = sb("ao", [KC, D])
        pickT = within(o0_pick, 0, [KC, T])
        hs = y
        hid0 = within(scratch0, 0, [128, F0 // 128, T])
        w_p0f, w_p0r = hid0[:, 0:3, 0:D], hid0[:, 3:6, 0:D]
        scratch1 = sb("scratch1", [128, 6 * T])
        parts = within(scratch1, 0, [KC, 2, 3, NK, T], BF16)
        p1T = within(scratch1, 0, [KC, NC_, 4 * 3 * SEL])
        stats0 = sb("stats0", [TC, NC_, 6])
        mv0 = sb("mv0", [TC, NC_, 2])
        rstd0 = sb("rstd0", [TC, NC_])
        h1 = sb("h1", [TC, NC_, D])
        hb1 = sb("hb1", [TC, NC_, D])
        scratch2 = sb("scratch2", [128, NC_ * D])
        xn1 = within(scratch2, 0, [TC, NC_, D])
        oS = within(scratch2, 0, [128, T])
        rec2 = within(scratch2, T, [128, T])
        xT1 = sb("xT1", [KC, NK, T])
        xT2 = sb("xT2", [KC, NK, T])
        stats1 = sb("stats1", [TC, NC_, 6])
        mv1 = sb("mv1", [TC, NC_, 2])
        rstd1 = sb("rstd1", [TC, NC_])
        hid1 = sb("hid1", [128, 6, T])
        q1s = sb("q1s", [SROWS + 2, H, T], BF16)
        k1s = sb("k1s", [SROWS + 2, H, T], BF16)
        v2 = sb("v2", [KC, NC_, H, HP])
        mx = sb("mx", [TC, H * NC_])
        mrow = sb("mrow", [H, 2, T], BF16)
        pT_both = sb("pT_both", [KC, 2 * 2 * W2C])
        pT = [within(pT_both, i * 2 * W2C, [KC, 2, W2C]) for i in range(2)]
        x32 = within(pT_both, 0, [KC, 2, NK, T])
        oN = sb("oN", [128, NG, T])
        sg = sb("sg", [128, 2, T])
        lg = sb("lg", [TC, NC_, 3])
        er = sb("er", [TC, NC_, 3])
        pr = sb("pr", [TC, NC_, 3])
        cmp_ = sb("cmp", [TC, NC_, 6])
        cwt = sb("cwt", [TC, NC_, 3])
        tot = sb("tot", [TC, NC_])
        outb = sb("outb", [TC, NC_, D])

        full = {a: sem(f"{a.lower()}_full") for a in area}
        taken = {a: sem(f"{a.lower()}_taken") for a in area}
        vector_step, pool_step, waits_apart = sem("vector_step"), sem("pool_step"), sem("waits_apart")
        weights_in, zeroed, consts_ready, weights_ready = (sem(x) for x in (
            "weights_in", "zeroed", "consts_ready", "weights_ready"))
        image_in = [sem(f"image_in{i}") for i in range(XG)]
        text_in, halves_out, halves_in, out_done = sem("text_in"), sem("halves_out"), sem("halves_in"), sem("out_done")
        q0_in, k0_in, stack_in, mrow_in = sem("q0_in"), sem("k0_in"), sem("stack_in"), sem("mrow_in")
        part_ready = sem("part_ready")
        stats_ready, rstd_ready, xn_ready = ([sem(f"{x}{l}") for l in range(2)]
                                             for x in ("stats_ready", "rstd_ready", "xn_ready"))
        clamped, pv0_used, pv2_used, o0_ready, oN_ready, silu_ready = (sem(x) for x in (
            "clamped", "pv0_used", "pv2_used", "o0_ready", "oN_ready", "silu_ready"))
        smx_ready = sem("smx_ready")
        x32_ready, parts_ready = sem("x32_ready"), sem("parts_ready")
        (pooled_ready, hb0_ready, q0_ready, k0_ready, v0_ready, vsum_ready, spread_ready, mean_ready,
         pick_ready, qblk_ready, res0_ready, hb1_ready, mrow_ready, lg_ready, er_ready,
         out_ready) = (sem(x) for x in (
             "pooled_ready hb0_ready q0_ready k0_ready v0_ready vsum_ready spread_ready mean_ready "
             "pick_ready qblk_ready res0_ready hb1_ready mrow_ready lg_ready er_ready "
             "out_ready").split())

        S_Q, S_K, S_V, S_ATT, S_AFT, BR, R_Q, R_K, R_V, C_P, C_O, N_BR, TMP, NOTE = range(14)

        def col(c, n=128):
            return scal[0:n, c:c + 1]

        loads = []

        def load(dst, src):
            loads.append((dst, src))

        for c, name in ((S_Q, "s_q"), (S_K, "s_k"), (S_V, "s_v"), (S_ATT, "s_attn"), (S_AFT, "s_after")):
            load(col(c), ins[f"L0_attn_{name}"].partition_broadcast(128))
        load(col(BR), ins["L0_ffn_br"].partition_broadcast(128))
        load(cw[:, :], ins["L0_tok_channel_weights"])

        def chan(a):
            return a.rearrange("(k p) n -> p k n", p=KC)

        load(w_qk0[:, :, :], chan(ins["L0_attn_Wqkv"][:, 0:2 * D]))
        load(w_qk1[:, :, :], chan(ins["L1_attn_qkv_w"][:, 0:2 * D]))
        load(w_v0[:, :, :], chan(ins["L0_attn_Wqkv"][:, 2 * D:3 * D]))
        load(w_v1[:, :, :], chan(ins["L1_attn_qkv_w"][:, 2 * D:3 * D]))
        for dst, name in ((w_p0f, "L0_attn_Wproj"), (w_p1, "L1_attn_proj_w")):
            wp = ins[name].rearrange("(g j d) n -> j d g n", g=NG, d=HD)
            for j in range(4):
                load(dst[HP * j:HP * j + HD, :, :], wp[j])
        for i, name in enumerate(("L0_attn_bproj", "L0_ffn_g1", "L0_ffn_b1", "L0_ffn_bv", "L0_ffn_bo", "L0_ffn_g2",
                                  "L0_ffn_b2", "L0_ffn_bf2", None, "L1_attn_proj_b")):
            src = ins[name] if name else ins["L1_attn_qkv_b"][2 * D:3 * D]
            load(rows[:, i, :], src.partition_broadcast(TC))
        load(w_r[:, :], ins["L0_ffn_Wr"].rearrange("(k p) -> p k", p=KC))
        for i, name in enumerate(("Wq", "Wk", "Wv", "Wo", "Wm")):
            load(w_f[:, :, i, :], chan(ins[f"L0_ffn_{name}"]))
        for i, name in enumerate(("bq", "bk")):
            load(b_qk[:, i, :], ins[f"L0_ffn_{name}"].rearrange("(k p) -> p k", p=KC))
        load(w1[:, :, :], chan(ins["L0_ffn_W1"]))
        load(bf1[:, :], ins["L0_ffn_bf1"].rearrange("(c p) -> p c", p=128))
        load(w2[:, :, :], ins["L0_ffn_W2"].rearrange("(c p) n -> p c n", p=128))
        for i in range(2):
            load(b_qk1[:, i, :], ins["L1_attn_qkv_b"][i * D:(i + 1) * D].rearrange("(k p) -> p k", p=KC))
        for i, name in enumerate(("gate", "up")):
            load(w_gu[:, :, 0, i, :], chan(ins[f"L1_ffn_shared_{name}"]))
            for e in range(3):
                load(w_gu[:, :, e + 1, i, :], chan(ins[f"L1_ffn_routed_{name}"][e]))
        for e in range(NEXP):
            load(w_dn[:, e, :, :], (ins["L1_ffn_routed_down"][e - 1] if e else ins["L1_ffn_shared_down"]).rearrange(
                "(c p) n -> p c n", p=128))
        load(w_router[:, :, :], chan(ins["L1_ffn_router_w"]))
        load(b_router[:, :], ins["L1_ffn_routing_bias"].partition_broadcast(TC))
        load(ao[MIX + 1:MIX + 2, :], ins["L0_ffn_bm"].rearrange("(a n) -> a n", a=1))

        img_dram = ins["x"].rearrange("b c (i r) w -> b (c i r w)", r=PATCH).rearrange(
            "b (g p n) -> b p g n", g=XG, p=XP)
        half_dram = pooled_dram.rearrange("b c i a j -> b (c i a j)").rearrange(
            "b (g p n) -> b p g n", g=XG, p=XP)

        class Turn:

            def __init__(self, eng, stages, it=None):
                self.eng, self.stages = eng, stages
                in_loop = self.in_loop = stages is TURN and not isinstance(it, int)
                it = {id(FIRST): -1, id(SECOND): 0, id(LAST): BATCH - 1, id(REST): BATCH}.get(id(stages), it)

                def value(x):
                    return eng.snap(x) if in_loop else x

                self.it = it
                self.n0, self.n1 = (0 if stages is FIRST else it + 1), it
                self.n2 = it - 1
                self.done0, self.done1, self.done2 = value(self.n0 + 1), value(it + 1), it
                self.base = {x: self.before(it, lambda part: count(part, x), value) for x in area}

            def before(self, it, amount, value=lambda x: x):
                if self.stages is FIRST:
                    return 0
                if self.stages is SECOND:
                    return amount(FIRST)
                if self.stages is REST:
                    return amount(FIRST) + amount(SECOND) + (BATCH - 2) * amount(TURN) + amount(LAST)
                return value(it * amount(TURN) + (amount(FIRST) + amount(SECOND) - amount(TURN)))

            def at(self, x, stage, k=0):
                i = self.stages.index(stage)
                return self.base[x] + (count(self.stages[:i], x) + k)

            def begin(self, x, stage, k=0, lag=0):
                self.eng.wait_ge(taken[x], self.at(x, stage, k) + (1 - lag))

            def begin_bank(self, x, stage):
                i = self.stages.index(stage)
                last = [s_ for s_ in self.stages[:i] if x in areas(s_)][-1]
                self.begin(x, stage, lag=int(last.split(".")[0] == stage.split(".")[0]))

            def await_full(self, x, stage, k=0):
                self.eng.wait_ge(full[x], self.at(x, stage, k) + 1)

            def await_taken(self, x, stage, k=0):
                self.eng.wait_ge(taken[x], self.at(x, stage, k) + 2)

        def apart(eng):
            eng.sem_inc(waits_apart, 1)

        def go(eng, programs):
            programs(Turn(eng, FIRST))
            programs(Turn(eng, SECOND))
            with eng.Fori(1, BATCH - 2) as it:
                programs(Turn(eng, TURN, it))
            programs(Turn(eng, TURN, BATCH - 2))
            programs(Turn(eng, LAST))
            programs(Turn(eng, REST))

        def steps_before(t, eng, steps_of):
            return t.before(t.it, lambda part: steps_of[id(part)],
                            eng.snap if t.in_loop else (lambda x: x))

        block = ctx.enter_context(nc.Block())

        @block.sync
        def _(sp):
            sp.wait_ge(zeroed, 4)
            with nc.allow_non_contiguous_dma(reason="vectors onto partitions, once"):
                for dst, src in loads:
                    sp.dma_start(dst, src).then_inc(weights_in, 16)
            for p_ in range(XG):
                sp.dma_start(img[:, p_, :], img_dram[0, :, p_, :]).then_inc(image_in[p_], 16)
            sp.dma_start(h0[TAIL:TC, 2, :], ins["txt"][0]).then_inc(text_in, 16)

            def program(t, more):
                n0, n1 = t.n0, t.n1
                for stage in t.stages:
                    name, _, k = stage.partition(".")
                    k = int(k or 0)
                    if name == "first" or name == "pool" and more:
                        m = 0 if name == "first" else n0 + 1
                        sp.wait_ge(part_ready, m * XG + (k + 1))
                        if more > 1:
                            sp.dma_start(img[:, k, :], img_dram[m + 1, :, k, :]).then_inc(image_in[k], 16)
                        if k == XG - 1:
                            sp.dma_start(half_dram[m], part[:, :, :]).then_inc(halves_out, 16)
                            sp.wait_ge(halves_out, m * 16 + 16)
                            sp.dma_start(halves[:, :, :, :], pooled_dram[m]).then_inc(halves_in, 16)
                    elif name == "qk0":
                        sp.wait_ge((q0_ready, k0_ready)[k], t.done0)
                        sp.dma_start((q0s, k0s)[k][0:HD, :, :], qk0[:, k, :, :]).then_inc((q0_in, k0_in)[k], 16)
                    elif name == "qk1":
                        sp.wait_ge(parts_ready, n1 * 2 + (k + 1))
                        for r, p_ in enumerate((Q_PARTS, K_PARTS)[k]):
                            sp.dma_start((q1s, k1s)[k][HD * r:HD * r + HD, :, :],
                                         parts[:, k, p_, :, :]).then_inc(stack_in, 16)
                    elif name == "mt":
                        sp.wait_ge(mrow_ready, t.done1)
                        for i in range(2):
                            sp.dma_start(q1s[SROWS + i:SROWS + i + 1, :, :], mrow[:, i, :]).then_inc(mrow_in, 16)
                    elif name == "fd" and t.stages is not LAST:
                        sp.wait_ge(res0_ready, t.done1)
                        sp.dma_start(h0[TAIL:TC, 2, :], ins["txt"][n0]).then_inc(text_in, 16)
                    elif stage == "dy.3":
                        sp.wait_ge(out_ready, t.done2)
                        sp.dma_start(out[t.n2].rearrange("(c p) d -> p c d", p=TC), outb[:, :, :]).then_inc(out_done, 16)

            program(Turn(sp, FIRST), 2)
            program(Turn(sp, SECOND), 2)
            with sp.Fori(1, BATCH - 3) as it:
                program(Turn(sp, TURN, it), 2)
            program(Turn(sp, TURN, BATCH - 3), 1)
            program(Turn(sp, TURN, BATCH - 2), 0)
            program(Turn(sp, LAST), 0)
            program(Turn(sp, REST), 0)
            sp.wait_ge(out_done, 16 * BATCH + 1)

        @block.gpsimd
        def _(pool):
            g = nc.gpsimd
            for t_ in (w_p1[:, :, :], w_p0f, scal[:, :], ao[:, :]):
                g.memset(t_, 0.0).then_inc(zeroed, 1)
            n = 0

            def const(ins_):
                nonlocal n
                n += 1
                ins_.then_inc(consts_ready, 1)
                pool.wait_ge(consts_ready, n)

            const(g.memset(pick[:, :, :], 0.0))
            const(g.memset(ident[:, :], 0.0))
            const(g.affine_select(out=ident[:, :], in_=ident[:, :], compare_op=ALU.not_equal, fill=1.0, base=0,
                                  pattern=[[-1, 128]], channel_multiplier=1))
            const(g.memset(ones[:, :], 1.0))
            const(g.memset(ones_b[:, :], 1.0))
            const(g.memset(minus_half[:, :], -0.5))
            const(g.iota(ranks[:, :], pattern=[[1, SEL]], base=0, channel_multiplier=0,
                         allow_small_or_imprecise_dtypes=True))
            const(g.memset(earlier[:, :, :], 1.0))
            const(g.affine_select(out=earlier[:, :, :], in_=earlier[:, :, :], compare_op=ALU.is_gt, fill=0.0, base=0,
                                  pattern=[[TC, NC_], [-1, T]], channel_multiplier=1))
            const(g.memset(head_mask[:, :], 1.0))
            const(g.affine_select(out=head_mask[:, :], in_=head_mask[:, :], compare_op=ALU.is_ge, fill=0.0, base=0,
                                  pattern=[[-HD, HK]], channel_multiplier=1))
            const(g.affine_select(out=head_mask[:, :], in_=head_mask[:, :], compare_op=ALU.is_ge, fill=0.0,
                                  base=HD - 1, pattern=[[HD, HK]], channel_multiplier=-1))
            const(g.memset(sum_row[:, :], 0.0))
            view = sum_row[:, :].rearrange("p (j n) -> p j n", n=HP)
            const(g.affine_select(out=view, in_=view, compare_op=ALU.not_equal, fill=1.0, base=-HD,
                                  pattern=[[-HP, 4], [0, HP]], channel_multiplier=1))
            for t_ in (v0[:, :, :, :], v1[:, :, :, :], v2[:, :, :, :], p1T[:, :, :], pq[0][:, :, :], pq[1][:, :, :],
                       pT[0][:, :, :], pT[1][:, :, :]):
                const(g.memset(t_, 0.0))
            const(g.memset(v1[0:TC, :, :, HD:HD + 1], 1.0))
            const(g.memset(v2[0:TC, :, :, HD:HD + 1], 1.0))
            for t_ in (q0s, k0s):
                const(g.memset(t_[:, :, :], 0.0))
            const(g.memset(k1s[SROWS:SROWS + 2, :, :], 1.0))
            assert n == CONSTS, n
            pool.wait_ge(weights_in, 16 * len(loads))
            steps = [0]
            steps_of = {id(TURN): POOL_STEPS}

            def program(t):
                base_step = steps_before(t, pool, steps_of)
                steps[0] = 0

                def link(ins_):
                    steps[0] += 1
                    ins_.then_inc(pool_step, 1)
                    pool.wait_ge(pool_step, base_step + steps[0])

                def inv_std(layer, k):
                    norms = (4, 2)[layer]
                    mv, rstd = ((mv0, rstd0), (mv1, rstd1))[layer]
                    pool.wait_ge(stats_ready[layer], (t.n0, t.n1)[layer] * norms + (k + 1))
                    apart(pool)
                    link(g.tensor_scalar(rstd[:, :], mv[:, :, 1], EPS, None, ALU.add))
                    g.tensor_tensor(rstd[:, :], rstd[:, :], minus_half[0:TC, :], ALU.pow).then_inc(rstd_ready[layer], 1)

                def add_row(dst, src, row):
                    return g.tensor_tensor(dst[:, :, :], src[:, :, :],
                                           row.unsqueeze(1).to_broadcast([TC, NC_, D]), ALU.add)

                for stage in t.stages:
                    if stage == "n0s":
                        inv_std(0, 0)
                        add_row(hb0, h0, bproj0).then_inc(hb0_ready, 1)
                    elif stage == "n1s":
                        inv_std(0, 1)
                    elif stage == "n1n":
                        inv_std(0, 2)
                    elif stage == "n3s":
                        inv_std(0, 3)
                        link(g.tensor_tensor(hb0[:, :, :], h0[:, :, :], hs[:, :, :], ALU.add))
                        add_row(hb0, hb0, bf2).then_inc(res0_ready, 1)
                    elif stage == "n4s":
                        inv_std(1, 0)
                        add_row(hb1, h1, bproj1).then_inc(hb1_ready, 1)
                    elif stage == "n5s":
                        inv_std(1, 1)
                assert t.stages is not TURN or steps[0] == POOL_STEPS, steps
                steps_of[id(t.stages)] = steps[0]

            go(pool, program)

        @block.scalar
        def _(act):
            a = nc.scalar
            act.wait_ge(consts_ready, CONSTS)
            act.wait_ge(weights_ready, 1)

            def program(t):
                for stage in t.stages:
                    name, _, k = stage.partition(".")
                    k = int(k or 0)
                    x = pair_of(name, k)
                    if name == "tok":
                        if t.stages is not FIRST:
                            act.wait_ge(res0_ready, t.done1)
                        t.await_full("M", stage)
                        a.copy(h0[:, 0:2, :], by_token("M")[:, 0:2, :])
                        a.copy(h0[0:TAIL, 2, :], by_token("M")[0:TAIL, 2, :]).then_inc(taken["M"], 1)
                    elif name in ("n0f", "n2f", "n3f"):
                        t.await_full("M", stage)
                        a.copy(xT0[:, :, :], by_channel("M")).then_inc(taken["M"], 1)
                    elif name in ("n4f", "n5f"):
                        t.await_full("N", stage)
                        a.copy((xT1 if name == "n4f" else xT2)[:, :, :], by_channel("N")).then_inc(taken["N"], 1)
                    elif name == "a0":
                        t.await_full(x, stage)
                        if t.stages is not FIRST or k >= 2:
                            act.wait_ge(clamped, t.n0 * H + (k - 1))
                        a.activation(pa[k % 2][0:TC, :, :], area[x][0:TC, :, 0:W2C], ACT.Copy, bias=OFF,
                                     scale=col(C_P, TC)).then_inc(taken[x], 1)
                    elif name == "gate":
                        t.await_full("M", stage)
                        a.activation(e_s[:, :], M[0:TC, 0, 0:NC_], ACT.Exp, bias=col(N_BR, TC),
                                     scale=-1.0).then_inc(taken["M"], 1)
                    elif name == "k1":
                        t.await_full("A", stage)
                        for kc in range(NK):
                            last = a.activation(k1[:, kc, :], A[0:KC, kc, 0:T], ACT.Identity, bias=b_qk[:, 1, kc:kc + 1])
                        last.then_inc(taken["A"], 1)
                    elif name == "rtb":
                        t.await_full("M", stage)
                        a.copy(ao[MIX:MIX + 1, :], M[0:1, 0, 0:D]).then_inc(taken["M"], 1)
                    elif name == "pk0":
                        t.await_full("M", stage)
                        a.copy(selT[:, :, :], by_channel("M", SEL)).then_inc(taken["M"], 1)
                    elif name == "gt":
                        t.await_full("B", stage)
                        a.copy(pickT[:, :], B[0:KC, 0, 0:T]).then_inc(taken["B"], 1)
                    elif name == "s1":
                        act.wait_ge(smx_ready, t.n0 * 2 + (k + 1))
                        for i in range(2):
                            last = a.activation(p1[:, 2 * k + i, :], area[x][0:3 * SEL, i, 0:T], ACT.Exp,
                                                bias=smx[:, 2 * k + i:2 * k + i + 1], scale=HD ** -0.5)
                        last.then_inc(taken[x], 1)
                    elif name == "t1":
                        t.await_full(x, stage)
                        n_ = 2 - k
                        a.copy(p1T[0:TC, 2 * k:2 * k + n_, :], area[x][0:TC, 0:n_, 0:4 * 3 * SEL]).then_inc(taken[x], 1)
                    elif name == "ct":
                        t.await_full("M", stage)
                        a.copy(ctxT[:, :, :], by_channel("M", SEL)).then_inc(taken["M"], 1)
                    elif name == "f0":
                        t.await_full(x, stage)
                        for i in range(2):
                            last = a.activation(hid0[:, 2 * k + i, :], area[x][:, i, 0:T], ACT.Gelu,
                                                bias=bf1[:, 2 * k + i:2 * k + i + 1])
                        last.then_inc(taken[x], 1)
                    elif name == "qk1":
                        t.await_full(x, stage)
                        for kc in range(NK):
                            last = a.activation(x32[:, k, kc, :], area[x][0:KC, kc, 0:T], ACT.Identity,
                                                bias=b_qk1[:, k, kc:kc + 1])
                        last.then_inc(x32_ready, 1)
                        for kc in range(NK):
                            last = a.activation(parts[:, k, 0, kc, :], area[x][0:KC, kc, 0:T], ACT.Identity,
                                                bias=b_qk1[:, k, kc:kc + 1])
                        last.then_inc(taken[x], 1)
                    elif name == "a2":
                        t.await_full(x, stage)
                        act.wait_ge(pv2_used, t.n1 * H + (k + 1))
                        a.activation(pT[k % 2][0:TC, :, :], area[x][0:TC, :, 0:W2C], ACT.Exp,
                                     scale=HD ** -0.5).then_inc(taken[x], 1)
                    elif name == "os":
                        if k:
                            act.wait_ge(oN_ready, t.n1 * NG + k)
                        t.await_full("N", f"pw.{4 * k + 3}")
                        a.copy(oS[:, :], N[:, 0, 0:T]).then_inc(taken["N"], 1)
                    elif name == "rtr":
                        act.wait_ge(lg_ready, t.done1)
                        a.activation(er[:, :, :], lg[:, :, :], ACT.Exp, scale=-1.0).then_inc(er_ready, 1)
                    elif name in ("ex", "ey"):
                        t.await_full(x, stage)
                        a.activation(sg[:, k % 2, :], area[x][:, 0, 0:T], ACT.Silu).then_inc(silu_ready, 1)

            go(act, program)

        @block.vector
        def _(dve):
            v = nc.vector
            dve.wait_ge(weights_in, 16 * len(loads))
            dve.wait_ge(consts_ready, CONSTS)
            for x in area:
                dve.sem_inc(taken[x], 1)
            dve.sem_inc(out_done, 1)
            dve.sem_inc(pv2_used, 2)
            setup = [0]

            def once(ins_):
                setup[0] += 1
                ins_.then_inc(vector_step, 1)
                dve.wait_ge(vector_step, setup[0])

            for dst, src in ((R_Q, S_Q), (R_K, S_K), (R_V, S_V)):
                once(v.reciprocal(col(dst), col(src)))
            once(v.tensor_scalar(col(TMP), col(S_ATT), float(T), None, ALU.mult))
            once(v.reciprocal(col(TMP), col(TMP)))
            once(v.tensor_tensor(col(C_P), col(S_Q), col(S_K), ALU.mult))
            once(v.tensor_scalar(col(C_P), col(C_P), col(TMP), HD ** -0.5, ALU.mult, ALU.mult))
            once(v.reciprocal(col(TMP), col(S_AFT)))
            once(v.tensor_tensor(col(C_O), col(S_ATT), col(S_V), ALU.mult))
            once(v.tensor_tensor(col(C_O), col(C_O), col(TMP), ALU.mult))
            once(v.tensor_scalar(col(N_BR), col(BR), -1.0, None, ALU.mult))
            once(v.tensor_copy(w_p0[:, 0, :, :], w_p0f))
            once(v.tensor_tensor(w_p0r, w_p0f, w_p0[:, 0, :, :], ALU.subtract))
            once(v.tensor_copy(w_p0[:, 1, :, :], w_p0r))
            once(v.tensor_tensor(w_p0r, w_p0r, w_p0[:, 1, :, :], ALU.subtract))
            once(v.tensor_copy(w_p0[:, 2, :, :], w_p0r))
            v.tensor_copy(col(NOTE), col(TMP)).then_inc(weights_ready, 1)
            steps = [0]
            steps_of = {id(TURN): VECTOR_STEPS}

            def program(t):
                n0, n1 = t.n0, t.n1
                base_step = steps_before(t, dve, steps_of)
                steps[0] = setup[0]

                def link(ins_):
                    steps[0] += 1
                    ins_.then_inc(vector_step, 1)
                    dve.wait_ge(vector_step, base_step + steps[0])

                def stats(layer, src):
                    st, mv = ((stats0, mv0), (stats1, mv1))[layer]
                    for c in range(NC_):
                        last = v.bn_stats(st[:, c, :], src[:, c, :])
                    link(last)
                    apart(dve)
                    for c in range(NC_):
                        last = v.bn_aggr(mv[:, c, :], st[:, c, :])
                    last.then_inc(stats_ready[layer], 1)

                def normal(layer, k, src, dst, gain=None, shift=None):
                    mv, rstd = ((mv0, rstd0), (mv1, rstd1))[layer]
                    dve.wait_ge(rstd_ready[layer], (n0, n1)[layer] * (4, 2)[layer] + (k + 1))
                    for c in range(NC_):
                        last = v.tensor_scalar(dst[:, c, :], src[:, c, :], mv[:, c, 0:1], rstd[:, c:c + 1],
                                               ALU.subtract, ALU.mult)
                    if gain is not None:
                        link(last)
                        link(v.tensor_tensor(dst[:, :, :], dst[:, :, :], gain.unsqueeze(1).to_broadcast([TC, NC_, D]),
                                             ALU.mult))
                        last = v.tensor_tensor(dst[:, :, :], dst[:, :, :],
                                               shift.unsqueeze(1).to_broadcast([TC, NC_, D]), ALU.add)
                    return last

                for stage in t.stages:
                    name, _, k = stage.partition(".")
                    k = int(k or 0)
                    x = pair_of(name, k)
                    if name == "first" or name == "pool" and (t.in_loop or t.stages is not TURN):
                        dve.wait_ge(image_in[k], 16 if name == "first" else n0 * 16 + 32)
                        v.tensor_reduce(part[:, k, :], img[:, k, :].rearrange("p (r j w) -> p j r w", r=HALF_ROWS, j=GRID),
                                        AX.XY, ALU.add).then_inc(part_ready, 1)
                    elif name == "pd":
                        dve.wait_ge(halves_in, n0 * 16 + 16)
                        v.tensor_tensor(pooled[:, :].rearrange("p (i j) -> p i j", i=GRID), halves[:, :, 0, :],
                                        halves[:, :, 1, :], ALU.add).then_inc(pooled_ready, 1)
                    elif name == "n0s":
                        dve.wait_ge(text_in, n0 * 16 + 16)
                        t.await_taken("M", "tok")
                        stats(0, h0)
                    elif name == "n0n":
                        normal(0, 0, h0, xn0).then_inc(xn_ready[0], 1)
                    elif name == "qk0":
                        t.await_full(x, stage)
                        v.tensor_scalar(t32[:, :, :], by_channel(x), col((R_Q, R_K)[k], KC), MAGIC, ALU.mult,
                                        ALU.add).then_inc(taken[x], 1)
                        t.await_taken(x, stage)
                        link(v.tensor_scalar(r16[:, :, :], t32[:, :, :], MAGIC, -4.0, ALU.subtract, ALU.max))
                        v.tensor_scalar(qk0[:, k, :, :], r16[:, :, :], 3.0, None, ALU.min)\
                            .then_inc((q0_ready, k0_ready)[k], 1)
                    elif name == "v0":
                        t.await_full("M", stage)
                        v.tensor_scalar(y[:, :, :], by_token("M"), col(R_V, TC), MAGIC, ALU.mult, ALU.add)\
                            .then_inc(taken["M"], 1)
                        t.await_taken("M", stage)
                        link(v.tensor_scalar(y[:, :, :], y[:, :, :], MAGIC, -4.0, ALU.subtract, ALU.max))
                        v.tensor_scalar(v0[0:TC, :, :, 0:HD].rearrange("p c h d -> p (c h) d"),
                                        y[:, :, :].rearrange("p c (h d) -> p (c h) d", d=HD), 3.0, None,
                                        ALU.min).then_inc(v0_ready, 1)
                    elif name == "vs":
                        t.await_full("M", stage)
                        v.tensor_scalar(vsum[:, :], M[:, 0, 0:NG], OFF, None, ALU.mult).then_inc(taken["M"], 1)
                    elif name == "cl":
                        t.await_taken(x, f"a0.{k}")
                        if t.stages is not FIRST or k >= 2:
                            dve.wait_ge(pv0_used, n0 * H + (k - 1))
                        v.tensor_scalar(pq[k % 2][0:TC, :, :], pa[k % 2][0:TC, :, :], OFF, OFF + 7.0, ALU.max,
                                        ALU.min).then_inc(clamped, 1)
                    elif name == "og":
                        t.await_full("M", f"pv.{4 * k + 3}")
                        v.tensor_scalar(o32[:, :], M[:, k % 2, 0:T], vsum[:, k:k + 1], col(C_O), ALU.subtract,
                                        ALU.mult).then_inc(taken["M"], 1)
                        t.await_taken("M", f"pv.{4 * k + 3}")
                        link(v.tensor_scalar(o32[:, :], o32[:, :], MAGIC, MAGIC, ALU.add, ALU.subtract))
                        v.tensor_scalar(o0[:, k, :], o32[:, :], -4.0, 3.0, ALU.max, ALU.min).then_inc(o0_ready, 1)
                    elif name == "pr0":
                        t.await_full("M", stage)
                        dve.wait_ge(hb0_ready, t.done0)
                        v.scalar_tensor_tensor(h0[:, :, :], by_token("M"), col(S_AFT, TC), hb0[:, :, :], ALU.mult,
                                               ALU.add).then_inc(taken["M"], 1)
                    elif name == "n1s":
                        t.await_taken("M", "pr0")
                        stats(0, h0)
                    elif name == "n1n":
                        link(normal(0, 1, h0, y))
                        stats(0, y)
                    elif name == "n2n":
                        normal(0, 2, y, xn0, g1, b1).then_inc(xn_ready[0], 1)
                    elif name == "v1":
                        t.await_full("M", stage)
                        for c in range(NC_):
                            last = v.tensor_tensor(v1[0:TC, c, :, 0:HD],
                                                   by_token("M")[:, c, :].rearrange("p (h d) -> p h d", d=HD),
                                                   bv0.rearrange("p (h d) -> p h d", d=HD), ALU.add)
                        last.then_inc(taken["M"], 1)
                    elif name == "gate":
                        t.await_taken("M", stage)
                        link(v.tensor_scalar(score[:, :], e_s[:, :], 1.0, None, ALU.add))
                        link(v.reciprocal(score[:, :], score[:, :]))
                        v.tensor_copy(score_b[:, :, :], score[:, :].unsqueeze(2).to_broadcast([TC, NC_, TC]))\
                            .then_inc(spread_ready, 1)
                    elif name == "rta":
                        t.await_full("A", stage)
                        v.tensor_copy(score_row[:, :], A[0:TC, 0, 0:T]).then_inc(taken["A"], 1)
                        t.await_taken("A", stage)
                        for c in range(NC_):
                            link(v.scalar_tensor_tensor(ties[:, :], score_row[:, :], score[:, c:c + 1],
                                                        earlier[:, c, :], ALU.is_equal, ALU.mult))
                            link(v.scalar_tensor_tensor(ties[:, :], score_row[:, :], score[:, c:c + 1], ties[:, :],
                                                        ALU.is_lt, ALU.add, accum_out=rank[:, c:c + 1]))
                        for c in range(NC_):
                            v.tensor_scalar(pick[:, c, 0:SEL], ranks[0:TC, :], rank[:, c:c + 1], None, ALU.is_equal)
                        link(v.tensor_scalar(unpicked[:, :], rank[:, :], float(SEL), None, ALU.is_ge))
                        v.tensor_copy(pick[:, :, MIX + 1], unpicked[:, :])
                        v.tensor_tensor(pick[:, :, MIX], score[:, :], unpicked[:, :], ALU.mult).then_inc(pick_ready, 1)
                        t.await_full("M", stage)
                        v.tensor_copy(mean_s[:, 0:3], M[0:KC, 0, 0:3]).then_inc(taken["M"], 1)
                        t.await_taken("M", stage)
                        link(v.tensor_scalar(mean_s[:, 2:3], mean_s[:, 2:3], 1e-6, None, ALU.add))
                        link(v.reciprocal(mean_s[:, 3:4], mean_s[:, 2:3]))
                        v.tensor_scalar(mean_s[:, 0:2], mean_s[:, 0:2], mean_s[:, 3:4], None, ALU.mult)\
                            .then_inc(mean_ready, 1)
                    elif name == "pk1":
                        t.await_full("M", stage)
                        v.tensor_tensor(qsel[:, :, :], by_channel("M", SEL),
                                        b_qk[:, 0, :].unsqueeze(2).to_broadcast([KC, NK, SEL]), ALU.add)\
                            .then_inc(taken["M"], 1)
                        t.await_taken("M", stage)
                        for kc in range(NK):
                            last = v.tensor_tensor(qblk[:, kc, :, :],
                                                   qsel[:, kc, :].unsqueeze(1).to_broadcast([KC, HK, SEL]),
                                                   head_mask[:, :].unsqueeze(2).to_broadcast([KC, HK, SEL]), ALU.mult)
                        last.then_inc(qblk_ready, 1)
                    elif name == "s1":
                        t.await_full(x, stage)
                        at = slice(2 * k, 2 * k + 2)
                        link(v.tensor_reduce(smx[:, at], area[x][0:3 * SEL, :, 0:T], AX.X, ALU.max))
                        v.tensor_scalar(smx[:, at], smx[:, at], -HD ** -0.5, None, ALU.mult).then_inc(smx_ready, 1)
                    elif name == "c1":
                        t.await_full("M", stage)
                        heads_out = M[0:SEL, 0, 0:H * (HD + 1)].rearrange("p (h d) -> p h d", d=HD + 1)
                        link(v.reciprocal(rec[:, :], heads_out[:, :, HD]))
                        v.tensor_tensor(ctx1[:, :].rearrange("p (h d) -> p h d", d=HD), heads_out[:, :, 0:HD],
                                        rec[:, :].unsqueeze(2).to_broadcast([SEL, H, HD]), ALU.mult)\
                            .then_inc(taken["M"], 1)
                    elif name == "wo":
                        t.await_full("M", stage)
                        v.tensor_tensor(ao[0:SEL, :], M[0:SEL, 0, 0:D], bo[0:SEL, :], ALU.add).then_inc(taken["M"], 1)
                    elif name == "mg":
                        t.await_full("M", stage)
                        v.tensor_tensor(hs[:, :, :], by_token("M"), y[:, :, :], ALU.add).then_inc(taken["M"], 1)
                        t.await_taken("M", stage)
                        t.await_full("A", stage)
                        for c in range(NC_):
                            last = v.scalar_tensor_tensor(hs[:, c, :], by_token("A")[:, c, :], unpicked[:, c:c + 1],
                                                          hs[:, c, :], ALU.mult, ALU.add)
                        last.then_inc(taken["A"], 1)
                    elif name == "n3s":
                        t.await_taken("A", "mg")
                        stats(0, hs)
                    elif name == "n3n":
                        normal(0, 3, hs, xn0, g2, b2).then_inc(xn_ready[0], 1)
                    elif name == "fd":
                        t.await_full("M", stage)
                        dve.wait_ge(res0_ready, t.done1)
                        v.tensor_tensor(h1[:, :, :], by_token("M"), hb0[:, :, :], ALU.add).then_inc(taken["M"], 1)
                        t.await_taken("M", stage)
                    elif name == "n4s":
                        stats(1, h1)
                    elif name == "n4n":
                        normal(1, 0, h1, xn1).then_inc(xn_ready[1], 1)
                    elif name == "qk1":
                        dve.wait_ge(x32_ready, n1 * 2 + (k + 1))
                        t.await_taken(x, stage)
                        link(v.tensor_tensor(x32[:, k, :, :], x32[:, k, :, :], parts[:, k, 0, :, :], ALU.subtract))
                        link(v.tensor_copy(parts[:, k, 1, :, :], x32[:, k, :, :]))
                        v.tensor_tensor(parts[:, k, 2, :, :], x32[:, k, :, :], parts[:, k, 1, :, :], ALU.subtract)\
                            .then_inc(parts_ready, 1)
                    elif name == "v2":
                        t.await_full("N", stage)
                        for c in range(NC_):
                            last = v.tensor_tensor(v2[0:TC, c, :, 0:HD],
                                                   by_token("N")[:, c, :].rearrange("p (h d) -> p h d", d=HD),
                                                   bv1.rearrange("p (h d) -> p h d", d=HD), ALU.add)
                        last.then_inc(taken["N"], 1)
                    elif name == "mx":
                        t.await_full("N", stage)
                        v.tensor_reduce(mx[:, k:k + 1], N[0:TC, k % 2, 0:T], AX.X, ALU.max)\
                            .then_inc(taken["N"], 1)
                    elif name == "mt":
                        t.await_full("N", stage)
                        link(v.tensor_scalar(mrow[:, 0, :], N[0:H, 0, 0:T], -1.0, None, ALU.mult))
                        v.scalar_tensor_tensor(mrow[:, 1, :], N[0:H, 0, 0:T], -1.0, mrow[:, 0, :], ALU.mult,
                                               ALU.subtract).then_inc(taken["N"], 1)
                        t.await_taken("N", stage)
                        v.tensor_copy(col(NOTE), col(TMP)).then_inc(mrow_ready, 1)
                    elif name == "ob":
                        t.await_full("N", stage)
                        v.reciprocal(rec2[:, :], N[:, 1, 0:T]).then_inc(taken["N"], 1)
                        t.await_taken("N", stage)
                        v.tensor_tensor(oN[:, k, :], oS[:, :], rec2[:, :], ALU.mult).then_inc(oN_ready, 1)
                    elif name == "pr1":
                        t.await_full("N", stage)
                        dve.wait_ge(hb1_ready, t.done1)
                        v.tensor_tensor(h1[:, :, :], by_token("N"), hb1[:, :, :], ALU.add).then_inc(taken["N"], 1)
                    elif name == "n5s":
                        t.await_taken("N", "pr1")
                        stats(1, h1)
                    elif name == "n5n":
                        normal(1, 1, h1, xn1).then_inc(xn_ready[1], 1)
                    elif name == "rtr":
                        t.await_full("N", stage)
                        v.tensor_tensor(lg[:, :, :], N[0:TC, 0, 0:9].rearrange("p (c e) -> p c e", e=3),
                                        b_router[:, :].unsqueeze(1).to_broadcast([TC, NC_, 3]), ALU.add)\
                            .then_inc(taken["N"], 1)
                        t.await_taken("N", stage)
                        v.tensor_copy(col(NOTE), col(TMP)).then_inc(lg_ready, 1)
                    elif name == "cw":
                        dve.wait_ge(er_ready, t.done2)
                        link(v.tensor_scalar(pr[:, :, :], er[:, :, :], 1.0, None, ALU.add))
                        link(v.reciprocal(pr[:, :, :], pr[:, :, :]))
                        pairs = ((0, 1, ALU.is_lt), (0, 2, ALU.is_lt), (1, 0, ALU.is_le), (1, 2, ALU.is_lt),
                                 (2, 0, ALU.is_le), (2, 1, ALU.is_le))
                        for i, (e, o, op) in enumerate(pairs):
                            last = v.tensor_tensor(cmp_[:, :, i], pr[:, :, e], pr[:, :, o], op)
                        link(last)
                        for e in range(3):
                            last = v.tensor_tensor(cwt[:, :, e], cmp_[:, :, 2 * e], cmp_[:, :, 2 * e + 1], ALU.mult)
                        link(last)
                        link(v.tensor_scalar(cwt[:, :, :], cwt[:, :, :], -1.0, 1.0, ALU.mult, ALU.add))
                        link(v.tensor_tensor(cwt[:, :, :], cwt[:, :, :], pr[:, :, :], ALU.mult))
                        link(v.tensor_reduce(tot[:, :], cwt[:, :, :], AX.X, ALU.add))
                        link(v.reciprocal(tot[:, :], tot[:, :]))
                        link(v.tensor_tensor(cwt[:, :, :], cwt[:, :, :],
                                             tot[:, :].unsqueeze(2).to_broadcast([TC, NC_, 3]), ALU.mult))
                    elif name in ("em", "ez"):
                        dve.wait_ge(silu_ready, (n1 if name == "em" else t.n2) * (3 * NEXP) + (k + 1))
                        v.tensor_tensor(hid1[:, k % 6, :], sg[:, k % 2, :], area[x][:, 1, 0:T], ALU.mult)\
                            .then_inc(taken[x], 1)
                    elif name == "dy":
                        t.await_full("N", stage)
                        if k == 0:
                            dve.wait_ge(out_done, t.n2 * 16 + 1)
                            v.tensor_tensor(outb[:, :, :], by_token("N"), h1[:, :, :], ALU.add).then_inc(taken["N"], 1)
                        else:
                            for c in range(NC_):
                                last = v.scalar_tensor_tensor(outb[:, c, :], by_token("N")[:, c, :],
                                                              cwt[:, c, k - 1:k], outb[:, c, :], ALU.mult, ALU.add)
                            last.then_inc(taken["N"], 1)
                        t.await_taken("N", stage)
                        if k == NEXP - 1:
                            v.tensor_copy(col(NOTE), col(TMP)).then_inc(out_ready, 1)

                assert t.stages is not TURN or steps[0] - setup[0] == VECTOR_STEPS, steps[0] - setup[0]
                steps_of[id(t.stages)] = steps[0] - setup[0]

            go(dve, program)

        @block.tensor
        def _(pe):
            mm, turn_ = nc.tensor.matmul, nc.tensor.transpose
            pe.wait_ge(consts_ready, CONSTS)
            pe.wait_ge(weights_in, 16 * len(loads))
            pe.wait_ge(weights_ready, 1)

            def program(t):
                n0, n1 = t.n0, t.n1

                def flip(x, src, n=TC, chunks=NC_):
                    apart(pe)
                    for kc in range(NK):
                        for c in range(chunks):
                            last = turn_(area[x][0:KC, kc, c * n:(c + 1) * n],
                                         src[:, c, kc * KC:(kc + 1) * KC] if chunks > 1
                                         else src[:, kc * KC:(kc + 1) * KC], ident[0:n, 0:n])
                    last.then_inc(full[x], 1)

                def channels(x, w, rhs, n=T, rows_=KC):
                    for j in range(2):
                        for kc in range(NK):
                            last = mm(area[x][0:rows_, j, 0:n], w(j, kc), rhs[:, kc, 0:n], start=(kc == 0),
                                      stop=(kc == NK - 1))
                    last.then_inc(full[x], 1)

                def tokens(x, lhs, w):
                    for c in range(NC_):
                        for i, w_ in enumerate(w):
                            last = mm(by_token(x)[:, c, :], lhs(i, c), w_, start=(i == 0), stop=(i == len(w) - 1))
                    last.then_inc(full[x], 1)

                def chunk(xT):
                    return lambda i, c: xT[:, i, c * TC:(c + 1) * TC]

                def scores(x, lhs, rhs, hh):
                    for c, bank, at, q in ((0, 0, 0, slice(0, T)), (1, 1, 0, slice(0, T)), (2, 0, T, slice(0, CUT)),
                                           (2, 1, T, slice(T - CUT, T))):
                        last = mm(area[x][0:TC, bank, at:at + q.stop - q.start], lhs[:, hh, c * TC:(c + 1) * TC],
                                  rhs[:, hh, q], start=True, stop=True)
                    last.then_inc(full[x], 1)

                def weigh(x, bank, j, v_, p_):
                    o_ = area[x][HP * j:HP * j + HP, bank, :]
                    mm(o_[:, 0:T], v_[:, 0, :], p_[:, 0, 0:T], start=True, stop=False)
                    mm(o_[:, 0:T], v_[:, 1, :], p_[:, 1, 0:T], start=False, stop=False)
                    mm(o_[:, 0:CUT], v_[:, 2, :], p_[:, 0, T:W2C], start=False, stop=False)
                    return mm(o_[:, CUT:T], v_[:, 2, :], p_[:, 1, 2 * CUT:W2C], start=False, stop=True)

                for stage in t.stages:
                    name, _, k = stage.partition(".")
                    k = int(k or 0)
                    x = pair_of(name, k)
                    if name == "tok":
                        pe.wait_ge(pooled_ready, t.done0)
                        t.begin("M", stage)
                        for c in range(NC_):
                            n_ = TC if c < 2 else TAIL
                            last = mm(by_token("M")[0:n_, c, :], pooled[:, c * TC:c * TC + n_], cw[:, :], start=True,
                                      stop=True)
                        last.then_inc(full["M"], 1)
                    elif name in ("n0f", "n2f", "n3f"):
                        pe.wait_ge(xn_ready[0], n0 * 3 + ("n0f", "n2f", "n3f").index(name) + 1)
                        t.begin("M", stage)
                        flip("M", xn0)
                    elif name == "qk0":
                        t.await_taken("M", "n0f")
                        t.begin(x, stage)
                        channels(x, lambda j, kc: w_qk0[:, kc, k * D + j * KC:k * D + (j + 1) * KC], xT0)
                    elif name == "v0":
                        t.begin("M", stage)
                        tokens("M", chunk(xT0), [w_v0[:, i, :] for i in range(NK)])
                    elif name == "vs":
                        pe.wait_ge(v0_ready, t.done0)
                        t.begin("M", stage)
                        for g_ in range(NG):
                            for c in range(NC_):
                                last = mm(M[:, 0, g_:g_ + 1],
                                          v0[:, c, 4 * g_:4 * g_ + 4, :].rearrange("p h d -> p (h d)"),
                                          ones_b[0:KC, :], start=(c == 0), stop=(c == NC_ - 1))
                        last.then_inc(full["M"], 1)
                    elif name == "a0":
                        if k == 0:
                            pe.wait_ge(q0_in, n0 * 16 + 16)
                            pe.wait_ge(k0_in, n0 * 16 + 16)
                        t.begin(x, stage)
                        scores(x, k0s, q0s, k)
                    elif name == "pv":
                        if k % 4 == 0:
                            t.begin("M", stage, lag=(1 if k else 0))
                        pe.wait_ge(clamped, n0 * H + (k + 1))
                        weigh("M", k // 4 % 2, k % 4, v0[:, :, k, :], pq[k % 2]).then_inc(pv0_used, 1)
                        if k % 4 == 3:
                            mm(M[0:1, k // 4 % 2, T:T + 1], ones_b[:, :], ones_b[:, :], start=True,
                               stop=True).then_inc(full["M"], 1)
                    elif name == "pr0":
                        pe.wait_ge(o0_ready, n0 * NG + NG)
                        t.begin("M", stage)
                        tokens("M", lambda i, c: o0[:, i % NG, c * TC:(c + 1) * TC],
                               [w_p0[:, i // NG, i % NG, :] for i in range(3 * NG)])
                    elif name == "gate":
                        t.await_taken("M", "n2f")
                        t.begin("M", stage)
                        for c in range(NC_):
                            for kc in range(NK):
                                last = mm(M[0:TC, 0, c:c + 1], xT0[:, kc, c * TC:(c + 1) * TC], w_r[:, kc:kc + 1],
                                          start=(kc == 0), stop=(kc == NK - 1))
                        last.then_inc(full["M"], 1)
                    elif name == "k1":
                        t.await_taken("M", "n2f")
                        t.begin("A", stage)
                        channels("A", lambda j, kc: w_f[:, kc, W_K, j * KC:(j + 1) * KC], xT0)
                    elif name == "v1":
                        t.begin("M", stage)
                        tokens("M", chunk(xT0), [w_f[:, i, W_V, :] for i in range(NK)])
                    elif name == "rta":
                        pe.wait_ge(spread_ready, t.done0)
                        t.begin("A", stage)
                        apart(pe)
                        for c in range(NC_):
                            last = turn_(A[0:TC, 0, c * TC:(c + 1) * TC], score_b[:, c, :], ident[0:TC, 0:TC])
                        last.then_inc(full["A"], 1)
                        t.begin("M", stage)
                        for j in range(NK + 1):
                            for c in range(NC_):
                                lhs = xn0[:, c, j * KC:(j + 1) * KC] if j < NK else ones[0:TC, 0:KC]
                                last = mm(M[0:KC, 0, j:j + 1], lhs, score[:, c:c + 1], start=(c == 0),
                                          stop=(c == NC_ - 1))
                        last.then_inc(full["M"], 1)
                    elif name == "rtb":
                        pe.wait_ge(mean_ready, t.done0)
                        t.begin("M", stage)
                        for kc in range(NK):
                            last = mm(M[0:1, 0, 0:D], mean_s[:, kc:kc + 1], w_f[:, kc, W_M, :], start=(kc == 0),
                                      stop=(kc == NK - 1))
                        last.then_inc(full["M"], 1)
                    elif name == "pk0":
                        pe.wait_ge(pick_ready, t.done0)
                        t.begin("M", stage)
                        for kc in range(NK):
                            for c in range(NC_):
                                last = mm(M[0:KC, kc, 0:SEL], xn0[:, c, kc * KC:(kc + 1) * KC], pick[:, c, 0:SEL],
                                          start=(c == 0), stop=(c == NC_ - 1))
                        last.then_inc(full["M"], 1)
                    elif name == "gt":
                        t.begin("B", stage)
                        apart(pe)
                        for c in range(NC_):
                            last = turn_(B[0:KC, 0, c * TC:(c + 1) * TC], pick[:, c, :], ident[0:TC, 0:TC])
                        last.then_inc(full["B"], 1)
                    elif name == "pk1":
                        t.await_taken("M", "pk0")
                        t.begin("M", stage)
                        channels("M", lambda j, kc: w_f[:, kc, W_Q, j * KC:(j + 1) * KC], selT, SEL)
                    elif name == "s1":
                        pe.wait_ge(qblk_ready, t.done0)
                        t.begin(x, stage)
                        for i in range(2):
                            last = mm(area[x][0:3 * SEL, i, 0:T], qblk[:, k, 3 * i:3 * i + 3, :].rearrange("p h q -> p (h q)"),
                                      k1[:, k, :], start=True, stop=True)
                        last.then_inc(full[x], 1)
                    elif name == "t1":
                        t.await_taken("A", "s1.0")
                        t.await_taken("B", "s1.1")
                        t.begin(x, stage)
                        apart(pe)
                        for i in range(2 - k):
                            for g_ in range(4):
                                c = 2 * k + i
                                last = turn_(area[x][0:TC, i, g_ * 3 * SEL:(g_ + 1) * 3 * SEL],
                                             p1[:, g_, c * TC:(c + 1) * TC], ident[0:3 * SEL, 0:3 * SEL])
                        last.then_inc(full[x], 1)
                    elif name == "c1":
                        t.await_taken("A", "t1.0")
                        t.await_taken("B", "t1.1")
                        t.begin("M", stage)
                        for hh in range(H):
                            for c in range(NC_):
                                last = mm(M[0:SEL, 0, hh * (HD + 1):(hh + 1) * (HD + 1)],
                                          p1T[:, c, hh * SEL:(hh + 1) * SEL], v1[:, c, hh, :], start=(c == 0),
                                          stop=(c == NC_ - 1))
                        last.then_inc(full["M"], 1)
                    elif name == "ct":
                        t.begin("M", stage)
                        flip("M", ctx1, SEL, 1)
                    elif name == "wo":
                        t.await_taken("M", "ct")
                        t.begin("M", stage)
                        for kc in range(NK):
                            last = mm(M[0:SEL, 0, 0:D], ctxT[:, kc, :], w_f[:, kc, W_O, :], start=(kc == 0),
                                      stop=(kc == NK - 1))
                        last.then_inc(full["M"], 1)
                    elif name == "mg":
                        t.await_taken("B", "gt")
                        t.begin("M", stage)
                        tokens("M", lambda i, c: pickT[:, c * TC:(c + 1) * TC], [ao[:, :]])
                        t.begin("A", stage)
                        tokens("A", chunk(xT0), [w_f[:, i, W_M, :] for i in range(NK)])
                    elif name == "f0":
                        t.await_taken("M", "n3f")
                        t.begin(x, stage)
                        channels(x, lambda j, kc: w1[:, kc, (2 * k + j) * 128:(2 * k + j + 1) * 128], xT0, rows_=128)
                    elif name == "fd":
                        for y_ in "AB":
                            pe.wait_ge(taken[y_], t.base[y_] + 1)
                        t.begin("M", stage)
                        tokens("M", chunk(hid0), [w2[:, i, :] for i in range(F0 // 128)])
                    elif name in ("n4f", "n5f"):
                        pe.wait_ge(xn_ready[1], n1 * 2 + ("n4f", "n5f").index(name) + 1)
                        t.begin("N", stage)
                        flip("N", xn1)
                    elif name == "qk1":
                        t.await_taken("N", "n4f")
                        t.begin(x, stage)
                        channels(x, lambda j, kc: w_qk1[:, kc, k * D + j * KC:k * D + (j + 1) * KC], xT1)
                    elif name == "v2":
                        t.begin("N", stage)
                        tokens("N", chunk(xT1), [w_v1[:, i, :] for i in range(NK)])
                    elif name == "mx":
                        if k == 0:
                            pe.wait_ge(stack_in, n1 * STACK_DMAS + STACK_DMAS)
                        t.begin_bank("N", stage)
                        hh, c = divmod(k, NC_)
                        mm(N[0:TC, k % 2, 0:T], q1s[0:SROWS, hh, c * TC:(c + 1) * TC], k1s[0:SROWS, hh, :],
                           start=True, stop=True).then_inc(full["N"], 1)
                    elif name == "mt":
                        t.begin("N", stage)
                        apart(pe)
                        for c in range(NC_):
                            last = turn_(N[0:H, 0, c * TC:(c + 1) * TC], mx[:, c:H * NC_:NC_], ident[0:TC, 0:TC])
                        last.then_inc(full["N"], 1)
                    elif name == "a2":
                        if k == 0:
                            pe.wait_ge(mrow_in, n1 * 32 + 32)
                        t.begin(x, stage)
                        scores(x, k1s, q1s, k)
                    elif name == "pw":
                        if k == 0:
                            t.begin("N", stage)
                        elif k % 4 == 0:
                            t.await_taken("N", f"pw.{k - 1}")
                        t.await_taken(x, f"a2.{k}")
                        weigh("N", 0, k % 4, v2[:, :, k, :], pT[k % 2]).then_inc(pv2_used, 1)
                        if k % 4 == 3:
                            mm(N[0:1, 0, T:T + 1], ones_b[:, :], ones_b[:, :], start=True,
                               stop=True).then_inc(full["N"], 1)
                    elif name == "ob":
                        t.await_taken("N", f"pw.{4 * k + 3}")
                        if k:
                            t.await_taken("N", f"ob.{k - 1}")
                        mm(N[:, 1, 0:T], sum_row[:, :], oS[:, :], start=True, stop=True).then_inc(full["N"], 1)
                    elif name == "pr1":
                        pe.wait_ge(oN_ready, n1 * NG + NG)
                        t.begin("N", stage)
                        tokens("N", chunk(oN), [w_p1[:, i, :] for i in range(NG)])
                    elif name == "rtr":
                        t.await_taken("N", "n5f")
                        t.begin("N", stage)
                        for c in range(NC_):
                            for kc in range(NK):
                                last = mm(N[0:TC, 0, 3 * c:3 * c + 3], xT2[:, kc, c * TC:(c + 1) * TC],
                                          w_router[:, kc, :], start=(kc == 0), stop=(kc == NK - 1))
                        last.then_inc(full["N"], 1)
                    elif name in ("ex", "ey"):
                        e, j_ = divmod(k, 3)
                        if k == 0:
                            assert t.stages.index("rtr") < t.stages.index(stage)
                        t.begin(x, stage)
                        channels(x, lambda i, kc: w_gu[:, kc, e, i, j_ * 128:(j_ + 1) * 128], xT2, rows_=128)
                    elif name == "dy":
                        for i in (1, 2):
                            j_, stage_ = 3 * k + i, f"ey.{3 * k + i}"
                            if stage_ in t.stages:
                                t.await_taken("AB"[j_ % 2], stage_)
                            else:
                                pe.wait_ge(taken["AB"[j_ % 2]], t.base["AB"[j_ % 2]] + 1)
                        t.begin("N", stage)
                        tokens("N", lambda i, c: hid1[:, 3 * (k % 2) + i, c * TC:(c + 1) * TC],
                               [w_dn[:, k, i, :] for i in range(3)])

            go(pe, program)


_TRANSPOSED = ("L0_attn_Wqkv", "L0_attn_Wproj", "L1_attn_qkv_w", "L1_attn_proj_w")
_BY_CHANNEL = ("L0_attn_Wqkv", "L1_attn_qkv_w", "L1_attn_qkv_b")
_UNREAD = ("L1_attn_qkv_B", "L1_attn_proj_B")


def kernel(**inputs):
    import concourse.bacc as bacc
    from concourse.bass_utils import run_bass_kernel_spmd

    nc = bacc.Bacc("TRN2", target_bir_lowering=False, num_devices=1)
    arrays, args = {}, {}
    for name, value in inputs.items():
        if name in _UNREAD:
            continue
        a = np.asarray(value)
        if name in _TRANSPOSED:
            a = a.T
        if name in _BY_CHANNEL:
            qk = a[..., :2 * D].reshape(a.shape[:-1] + (2, HK, NK, HD))
            qk = np.moveaxis(qk, -3, -1)
            a = np.concatenate([qk.reshape(a.shape[:-1] + (2 * D,)), a[..., 2 * D:]], axis=-1)
        a = np.ascontiguousarray(a.reshape(a.shape or (1,)))
        arrays[f"in_{name}"] = a
        args[name] = nc.dram_tensor(f"in_{name}", a.shape, mybir.dt.from_np(a.dtype), kind="ExternalInput").ap()
    out = nc.dram_tensor("out_0", (BATCH, T, D), F32, kind="ExternalOutput").ap()
    early_fusion(nc, args, out)
    r = run_bass_kernel_spmd(nc, [arrays], core_ids=[0])
    return r.results[0]["out_0"]
```
